# Optimizing a Trainium2 kernel written in Bass

```python
import numpy as np
import jax
import jax.numpy as jnp

def _softmax(x, axis=-1):
    return jax.nn.softmax(x, axis=axis)

def _gelu(x):
    return jax.nn.gelu(x, approximate=True)

def _silu(x):
    return jax.nn.silu(x)

def _sigmoid(x):
    return jax.nn.sigmoid(x)

def _layernorm(x, axis=-1, eps=1e-05):
    m = jnp.mean(x, axis=axis, keepdims=True)
    v = jnp.var(x, axis=axis, keepdims=True)
    return (x - m) / jnp.sqrt(v + eps)

def _scatter_add(tgt, idx, src, axis=0):
    return tgt.at[idx].add(src)

def _segment_sum(src, seg, n):
    return jax.ops.segment_sum(src, seg, n)
kernel_name = 'mk_early_fusion_d1_tok_img1024_r4_02ce2a'

def setup_inputs(seed: int=0):
    np.random.seed(seed)
    _w = jnp.asarray

    def _rec_inputs():
        import jax
        import jax.numpy as jnp
        _rk = jax.random.key(seed)
        x = 7.57192e-06 + 1.00007 * jax.random.normal(jax.random.fold_in(_rk, 1), (4, 3, 96, 96), jnp.float32)
        txt = 0.000741161 + 1.00074 * jax.random.normal(jax.random.fold_in(_rk, 2), (4, 512, 256), jnp.float32)
        return (x, txt)
    x, txt = _rec_inputs()

    def _L0_tok_setup():
        import jax, jax.numpy as jnp
        import numpy as np
        IMG = 224
        PATCH = 16
        C_IN = 3
        D = 256
        B = 64
        PATCH_DIM = C_IN * PATCH * PATCH
        key = jax.random.key(seed)
        k1, k2, k3 = jax.random.split(key, 3)
        x = jax.random.normal(k1, (B, C_IN, IMG, IMG), dtype=jnp.float32)
        W = jax.random.normal(k2, (D, PATCH_DIM), dtype=jnp.float32) * (1.0 / np.sqrt(PATCH_DIM))
        b = jax.random.normal(k3, (D,), dtype=jnp.float32) * 0.02
        return {'x': x, 'W': W, 'b': b}
    _L0_tok_all = _L0_tok_setup()
    _L0_tok_in = {k: v for k, v in _L0_tok_all.items() if k in ('W', 'b')}
    del _L0_tok_all

    def _L0_attn_setup():
        import jax, jax.numpy as jnp
        import numpy as np
        import math
        B, T, E = (1, 512, 256)
        H = 16
        D = E // H
        L = 64
        key = jax.random.key(seed)
        ks = jax.random.split(key, 7)
        s = lambda fan: 1.0 / math.sqrt(fan)
        return {'hidden_states': jax.random.normal(ks[0], (B, T, E), dtype=jnp.float32), 'Wq': jax.random.normal(ks[1], (E, E), dtype=jnp.float32) * s(E), 'Wk_down': jax.random.normal(ks[2], (L, E), dtype=jnp.float32) * s(E), 'Wv_down': jax.random.normal(ks[3], (L, E), dtype=jnp.float32) * s(E), 'q_to_latent': jax.random.normal(ks[4], (H, D, L), dtype=jnp.float32) * s(D), 'v_up': jax.random.normal(ks[5], (H, L, D), dtype=jnp.float32) * s(L), 'Wout': jax.random.normal(ks[6], (E, E), dtype=jnp.float32) * s(E)}
    _L0_attn_all = _L0_attn_setup()
    _L0_attn_in = {k: v for k, v in _L0_attn_all.items() if k in ('Wq', 'Wk_down', 'Wv_down', 'q_to_latent', 'v_up', 'Wout')}
    del _L0_attn_all

    def _L0_ffn_setup():
        import jax, jax.numpy as jnp
        import numpy as np
        import math
        EMBED_DIM = 256
        FFN_DIM = 1024
        N_EXPERTS = 8
        TOP_K = 2
        CAP_FACTOR = 1.25
        key = jax.random.key(seed)
        k0, k1, k2, k3 = jax.random.split(key, 4)
        B, S = (4, 512)
        x = jax.random.normal(k0, (B, S, EMBED_DIM), dtype=jnp.float32)
        Wr = jax.random.normal(k1, (EMBED_DIM, N_EXPERTS), dtype=jnp.float32) * 0.02
        W1 = jax.random.normal(k2, (N_EXPERTS, EMBED_DIM, FFN_DIM), dtype=jnp.float32) * 0.02
        W2 = jax.random.normal(k3, (N_EXPERTS, FFN_DIM, EMBED_DIM), dtype=jnp.float32) * 0.02
        return {'x': x, 'Wr': Wr, 'W1': W1, 'W2': W2}
    _L0_ffn_all = _L0_ffn_setup()
    _L0_ffn_in = {k: v for k, v in _L0_ffn_all.items() if k in ('Wr', 'W1', 'W2')}
    del _L0_ffn_all
    return {'x': x, 'txt': txt, 'L0_tok_W': _L0_tok_in['W'], 'L0_tok_b': _L0_tok_in['b'], 'L0_attn_Wq': _L0_attn_in['Wq'], 'L0_attn_Wk_down': _L0_attn_in['Wk_down'], 'L0_attn_Wv_down': _L0_attn_in['Wv_down'], 'L0_attn_q_to_latent': _L0_attn_in['q_to_latent'], 'L0_attn_v_up': _L0_attn_in['v_up'], 'L0_attn_Wout': _L0_attn_in['Wout'], 'L0_ffn_Wr': _L0_ffn_in['Wr'], 'L0_ffn_W1': _L0_ffn_in['W1'], 'L0_ffn_W2': _L0_ffn_in['W2']}

def reference(x, txt, L0_tok_W, L0_tok_b, L0_attn_Wq, L0_attn_Wk_down, L0_attn_Wv_down, L0_attn_q_to_latent, L0_attn_v_up, L0_attn_Wout, L0_ffn_Wr, L0_ffn_W1, L0_ffn_W2):
    import jax
    import jax.numpy as jnp

    def _L0_tok_ref(x, W, b):
        import jax, jax.numpy as jnp
        import numpy as np
        IMG = 224
        PATCH = 16
        C_IN = 3
        D = 256
        B = 64
        PATCH_DIM = C_IN * PATCH * PATCH
        Bx, C, H, Wd = x.shape
        p = PATCH
        Hp, Wp = (H // p, Wd // p)
        patches = x.reshape(Bx, C, Hp, p, Wp, p).transpose(0, 2, 3, 1, 4, 5)
        patches = patches.reshape(Bx, -1, PATCH_DIM)
        return jnp.einsum('bnp,dp->bnd', patches, W) + b

    def _L0_attn_ref(hidden_states, Wq, Wk_down, Wv_down, q_to_latent, v_up, Wout):
        import jax, jax.numpy as jnp
        import numpy as np
        import math
        B, T, E = (1, 512, 256)
        H = 16
        D = E // H
        L = 64
        'RA_MLA_Attention forward (default config: coupling_scale=0 so the RA\n            reciprocal-band branch is inactive; no cache, no RoPE, dropout=0).'
        b, t, e = hidden_states.shape
        h, d, l = q_to_latent.shape
        Q = (hidden_states @ Wq.T).reshape(b, t, h, d)
        latent_k = hidden_states @ Wk_down.T
        latent_v = hidden_states @ Wv_down.T
        q_lat = jnp.einsum('bthd,hdl->bthl', Q, q_to_latent)
        logits = jnp.einsum('bthl,bsl->bhts', q_lat, latent_k) / math.sqrt(l)
        causal = jnp.tril(jnp.ones((t, t), dtype=bool))
        logits = jnp.where(causal[None, None], logits, jnp.float32(-1e+30))
        attn = jax.nn.softmax(logits, axis=-1)
        ctx_lat = jnp.einsum('bhts,bsl->bhtl', attn, latent_v)
        heads = jnp.einsum('bhtl,hld->bthd', ctx_lat, v_up)
        out = heads.reshape(b, t, h * d) @ Wout.T
        return out

    def _L0_ffn_ref(x, Wr, W1, W2):
        import jax, jax.numpy as jnp
        import numpy as np
        import math
        EMBED_DIM = 256
        FFN_DIM = 1024
        N_EXPERTS = 8
        TOP_K = 2
        CAP_FACTOR = 1.25
        B, S, D = x.shape
        t = B * S
        xf = x.reshape(t, D)
        probs = jax.nn.softmax(xf.astype(jnp.float32) @ Wr, axis=-1)
        topk_probs, topk_experts = jax.lax.top_k(probs, TOP_K)
        cap = max(math.ceil(t * TOP_K * CAP_FACTOR / N_EXPERTS), 1)
        y = jnp.zeros_like(xf)
        for e in range(N_EXPERTS):
            mask = topk_experts == e
            gate = jnp.sum(jnp.where(mask, topk_probs, 0.0), axis=-1)
            has = jnp.any(mask, axis=-1)
            g_masked = jnp.where(has, gate, -jnp.inf)
            vals, idx = jax.lax.top_k(g_masked, cap)
            g = jnp.where(jnp.isfinite(vals), vals, 0.0)
            xe = xf[idx]
            h = jax.nn.relu(xe @ W1[e]) @ W2[e]
            y = y.at[idx].add(g[:, None] * h)
        return y.reshape(B, S, D)
    h = _L0_tok_ref(x, L0_tok_W, L0_tok_b)
    h = jnp.concatenate([h, txt], axis=1)
    h = h + _L0_attn_ref(_layernorm(h, axis=-1), L0_attn_Wq, L0_attn_Wk_down, L0_attn_Wv_down, L0_attn_q_to_latent, L0_attn_v_up, L0_attn_Wout)
    h = h + _L0_ffn_ref(_layernorm(h, axis=-1), L0_ffn_Wr, L0_ffn_W1, L0_ffn_W2)
    return h

_drawn_inputs = setup_inputs


def setup_inputs(seed=0):
    import zlib

    import numpy as np

    out = dict(_drawn_inputs(seed))
    spreads = {}
    factors = {'L0_tok_b': 6.291}
    for name, (base, spread) in spreads.items():
        noise = np.random.default_rng([zlib.crc32(name.encode()), seed]).standard_normal(out[name].shape)
        drawn = base * np.exp(spread * noise) if base else spread * noise
        out[name] = jnp.asarray(drawn.astype(out[name].dtype))
    for name, factor in factors.items():
        out[name] = (out[name] * factor).astype(out[name].dtype)
    return out
```

```python
import concourse.bass as bass
from concourse import mybir
from contextlib import ExitStack


def early_fusion_kernel(nc, patchesT, txt, tokWT, tokb, WqT, WkvT, q2lT, vup, WoT, Wr, W1, W2, out):
    f32, bf16, u32 = mybir.dt.float32, mybir.dt.bfloat16, mybir.dt.uint32
    ALU = mybir.AluOpType
    ACT = mybir.ActivationFunctionType
    AX = mybir.AxisListType.X

    P = 128
    B, NTXT, D = txt.shape
    NIMG = patchesT.shape[1] // B
    T = NIMG + NTXT
    PK = patchesT.shape[0] // P
    DK = D // P
    HEADS, HD = 16, 16
    LAT = q2lT.shape[0]
    UH = P // HD
    UNITS = B * HEADS // UH
    HT = T // 2
    SP_ = 640
    NE, _, FF = W1.shape
    FK = FF // P
    NTOK = B * T
    TOPK = 2
    CAP = -(-NTOK * TOPK * 5 // (4 * NE))
    SLOTS = NE * CAP
    SROWS = -(-(SLOTS + 1) // P) * P
    EPS = 1e-5
    SCALE = float(LAT) ** -0.5
    NEG = -1e30
    QT = [(0, NIMG)] + [(NIMG + P * i, P) for i in range(NTXT // P)]
    NQ = len(QT)
    KT = [(P * i, min(P, T - P * i)) for i in range(-(-T // P))]
    NT = B * NQ
    QROWS = [0, 0, 0, 1, 1, 2]
    KROWS = [0, 1, 2, 0, 1, 0]
    CON = HD * len(QROWS)
    CONM = CON + 3

    SPIECE = [[(0, 0, 36, 0), (1, 0, 164, 36), (2, 0, 292, 200)],
              [(3, 0, 420, 0), (4, 512, 36, 420)],
              [(4, 0, 512, 0)]]
    TPIECE = [[(0, 0, 512, 0)],
              [(0, 512, 36, 0), (1, 128, 420, 36)],
              [(2, 256, 292, 0), (3, 384, 164, 292), (4, 512, 36, 456)]]
    TOFF = [0, 512, 968]
    PW = 1460
    DIAG = [(0, P), (512 + 36, P), (968, P), (968 + 292, P), (968 + 456, T - 4 * P)]
    SEG = []
    for pc, off in zip(TPIECE, TOFF):
        for kt, q0, w, c in pc:
            for h0 in (0, HT):
                lo, hi = max(q0, h0), min(q0 + w, h0 + HT)
                if lo < hi:
                    SEG.append((h0 // HT, kt, off + c + lo - q0, lo, hi - lo))
    SEG.sort()
    NP = 6

    order = []

    def batch_front(b):
        return [("embed", b), ("ln1", b), ("hT", b), ("kv", b), ("V", b)]

    def batch_back(b):
        return [("W", b), ("ln2", b), ("R", b)]

    order += batch_front(0) + [("Q", 0), ("K", 0), ("Q", 1), ("K", 1)]
    order += [("S", 0, j) for j in range(UH)] + [("M", 0)]
    for u in range(UNITS):
        nxt = u + 1 < UNITS
        s_at = {0: [0, 1], 1: [2], 2: [3, 4], 3: [5], 4: [6, 7]}
        for j in range(UH):
            if nxt:
                order += [("S", u + 1, i) for i in s_at.get(j, [])]
                if j == 5:
                    order += [("M", u + 1)]
            order += [("T", u, j)]
            if j == 0 and u > 0:
                order += [("PV", u - 1, 1)]
                if u % 2 == 0:
                    order += [("N", u // 2 - 1)]
            if u % 2 == 0 and u > 0 and j == 4:
                order += [("W", u // 2 - 1)]
            if j == 5:
                order += [("PV", u, 0)]
            if u == 0 and j < B - 1:
                order += [("embed", j + 1)]
            if u + 2 < UNITS:
                if u % 2 == 0:
                    b = u // 2 + 1
                    order += {1: [("ln1", b)], 2: [("hT", b)], 3: [("kv", b), ("V", b)]}.get(j, [])
                order += {4: [("Q", u + 2)], 6: [("K", u + 2)]}.get(j, [])
            if u % 2 == 1 and u > 1:
                b = (u - 3) // 2
                order += {0: [("ln2", b)], 2: [("R", b)]}.get(j, [])
    order += [("PV", UNITS - 1, 1), ("N", B - 1)] + batch_back(B - 1)

    fills = {}

    def fill_keys(job):
        k, a = job[0], job[1]
        return {"embed": [0], "hT": range(4), "kv": range(2), "V": range(3), "Q": range(2), "K": range(2),
                "M": range(2), "W": range(NQ), "R": range(2 * NQ)}.get(k, [])

    for job in order:
        for i in fill_keys(job):
            fills[(job[0], job[1], i)] = len(fills)
    ROUNDS = 30
    for key in [("cnt", r) for r in range(ROUNDS)] + [("cgt", 0), ("ceq", 0), ("pos", 0)]:
        fills[key] = len(fills)

    ln_order = [job for job in order if job[0] in ("ln1", "ln2")]
    ln_count = {job: n + 1 for n, job in enumerate(ln_order)}

    def fR(i, part):
        if part == 0:
            return 0 if i == 0 else 2 * i - 1
        return 2 * i + 2 if i < NQ - 1 else 2 * NQ - 1

    ctx = ExitStack()
    with ctx:
        def sem(name):
            return ctx.enter_context(nc.semaphore(name))

        def sb(name, shape, dt, where=ctx):
            return where.enter_context(nc.sbuf_tensor(name, shape, dt))

        xs_d = nc.dram_tensor("split_scratch", [2, UNITS, 3, P, T], bf16).ap()
        dn_d = nc.dram_tensor("den_scratch", [B, HEADS, T], f32).ap()
        rc_d = nc.dram_tensor("rden_scratch", [B, HEADS, T], f32).ap()
        xe_d = nc.dram_tensor("expert_in", [SROWS, 2 * D], bf16).ap()
        y_d = nc.dram_tensor("expert_out", [SLOTS + 1, D], f32).ap()

        ident = sb("ident", [P, P], f32)
        identb = sb("identb", [P, P], bf16)
        H = sb("H", [P, B, NQ, D], f32)
        XHL = sb("XHL", [P, NT, 2 * D], bf16)
        LG = sb("LG", [P, NT, NE], f32)
        zero = sb("zero", [P, 2 * D], bf16)
        ones = sb("ones", [P, P], f32)
        onesb = sb("onesb", [P, P], bf16)
        trib = sb("trib", [P, P], bf16)
        valid = sb("valid", [P, NT, NE], f32)
        iota8 = sb("iota8", [P, NT, NE], f32)
        base8 = sb("base8", [P, NT, NE], f32)
        sidx = sb("sidx", [P, TOPK, NT], u32)
        gidx = sb("gidx", [P, TOPK, NT], u32)
        gate = sb("gate", [P, TOPK, NT], f32)

        att = ExitStack()
        tb = sb("tb", [1, D], f32, att)
        wq = sb("wq", [P, DK, D], f32, att)
        wkv = sb("wkv", [P, DK, 2 * LAT], f32, att)
        q2l = sb("q2l", [LAT, HEADS * HD], f32, att)
        vu = sb("vu", [P, HEADS * HD], f32, att)
        wo = sb("wo", [P, 4, D], f32, att)
        wr = sb("wr", [P, DK, NE], f32, att)
        nhalf = sb("nhalf", [P, NQ], f32, att)
        maskn = sb("maskn", [P, T], f32, att)
        st = sb("st", [P, NQ, 6], f32, att)
        mv = sb("mv", [P, NQ, 2], f32, att)
        rs = sb("rs", [P, NQ], f32, att)
        ve = sb("ve", [P, NQ], f32, att)
        xh = sb("xh", [P, NQ, D], f32, att)
        hnT = sb("hnT", [P, DK, T], f32, att)
        lat = sb("lat", [P, T], f32, att)
        V = sb("V", [P, 2, NQ, HEADS, 1 + HD], f32, att)
        XS = sb("XS", [P, 2, 3, T], bf16, att)
        XR = sb("XR", [P, 2, T], f32, att)
        Qs = [sb(f"Qs{i}", [P, UH, T], bf16, att) for i in range(3)]
        Ks = [sb(f"Ks{i}", [P, UH, SP_], bf16, att) for i in range(3)]
        mx = sb("mx", [P, 2, NQ + 1, UH], f32, att)
        NS = sb("NS", [UH, 3, T], bf16, att)
        NR = sb("NR", [UH, T], f32, att)
        Pr = sb("Pr", [P, NP, PW], f32, att)
        Of = sb("Of", [P, 4, T], f32, att)
        emb = ExitStack()
        PT = sb("PT", [P, PK, B * NIMG], f32, emb)
        TW = sb("TW", [P, PK, D], f32, emb)
        emb.close()
        Rb = sb("Rb", [P, 4, T], f32, att)
        DG = sb("DG", [64, HEADS * T // 64], f32, att)
        xnT = sb("xnT", [P, 2, DK * P], f32, att)

        bankS = [ctx.enter_context(nc.psum_tensor(f"bankS{i}", [P, 512], f32)) for i in range(2)]
        bankT = [ctx.enter_context(nc.psum_tensor(f"bankT{i}", [P, 512], f32)) for i in range(2)]
        bankO = ctx.enter_context(nc.psum_tensor("bankO", [P, 2, 512], f32))
        bankM = [ctx.enter_context(nc.psum_tensor(f"bankM{i}", [P, 512], f32)) for i in range(2)]

        ld_tok, ld_att = sem("ld_tok"), sem("ld_att")
        ld_txt = [sem(f"ld_txt{b}") for b in range(B)]
        zeroed = sem("zeroed")
        pool_const, dve_const = sem("pool_const"), sem("dve_const")
        m_full = [sem(f"m_full{i}") for i in range(2)]
        m_used = [sem(f"m_used{i}") for i in range(2)]
        mean_ready, rstd_ready, xhat_ready = sem("mean_ready"), sem("rstd_ready"), sem("xhat_ready")
        hi_ready, mid_ready, lo_ready = sem("hi_ready"), sem("mid_ready"), sem("lo_ready")
        split_stored = [sem(f"split_stored{i}") for i in range(2)]
        stack_ready = [sem(f"stack_ready{i}") for i in range(3)]
        s_full = [sem(f"s_full{i}") for i in range(2)]
        s_used = [sem(f"s_used{i}") for i in range(2)]
        t_full = [sem(f"t_full{i}") for i in range(2)]
        t_used = [sem(f"t_used{i}") for i in range(2)]
        max_ready, nmhi_ready, nm_ready = sem("max_ready"), sem("nmhi_ready"), sem("nm_ready")
        maxrow_ready = [sem(f"maxrow_ready{i}") for i in range(2)]
        prob_ready = sem("prob_ready")
        o_full, o_used = sem("o_full"), sem("o_used")
        den_stored = [sem(f"den_stored{i}") for i in range(2)]
        den_packed, rden_ready, rden_stored, rden_spread = (sem("den_packed"), sem("rden_ready"),
                                                            sem("rden_stored"), sem("rden_spread"))
        ctx_ready = sem("ctx_ready")
        xn_ready, xhl_ready = sem("xn_ready"), sem("xhl_ready")
        rexp_in, rexp = sem("rexp_in"), sem("rexp")
        cnt_in = sem("cnt_in")
        idx_ready = sem("idx_ready")
        scattered = sem("scattered")
        dve_chain, pool_chain = sem("dve_chain"), sem("pool_chain")
        w_loaded, xe_loaded = [sem("w_loaded0"), sem("w_loaded1")], [sem("xe_loaded0"), sem("xe_loaded1")]
        whi_ready, wlo_ready = sem("whi_ready"), sem("wlo_ready")
        tr_full = [sem(f"tr_full{i}") for i in range(2)]
        tr_used = [sem(f"tr_used{i}") for i in range(2)]
        h_full = [sem(f"h_full{i}") for i in range(4)]
        hhi_ready = sem("hhi_ready")
        h_used = [sem(f"h_used{i}") for i in range(4)]
        y_full = [sem(f"y_full{i}") for i in range(2)]
        y_used = [sem(f"y_used{i}") for i in range(2)]
        y_stored = [sem("y_stored0"), sem("y_stored1")]
        gathered = [sem(f"gathered{i}") for i in range(4)]
        combined = sem("combined")
        stored = sem("stored")

        def filled(eng, key):
            n = fills[key]
            eng.wait_ge(m_full[n % 2], n // 2 + 1)

        def used(eng, key):
            n = fills[key]
            eng.wait_ge(m_used[n % 2], n // 2 + 1)

        def open_fill(pe, key):
            n = fills[key]
            if n >= 2:
                pe.wait_ge(m_used[n % 2], n // 2)
            return bankM[n % 2]

        att.close()
        ffn = ExitStack()
        EP = sb("EP", [P, NT, NE], f32, ffn)
        E2 = sb("E2", [P, NT, NE], f32, ffn)
        E3 = sb("E3", [P, NT, NE], f32, ffn)
        OH = sb("OH", [P, TOPK, NT, NE], f32, ffn)
        G = sb("G", [P, NT, NE], f32, ffn)
        KEEP = sb("KEEP", [P, NT, NE], f32, ffn)
        POS = sb("POS", [P, NT, NE], f32, ffn)
        Xb = sb("Xb", [P, NT, NE], bf16, ffn)
        r20 = sb("r20", [P, 4, NT], f32, ffn)
        v8 = sb("v8", [P, NT, 8], f32, ffn)
        i8 = sb("i8", [P, NT, 8], u32, ffn)
        i8f = sb("i8f", [P, NT, 8], f32, ffn)
        thr = sb("thr", [P, NE], f32, ffn)
        cand = sb("cand", [P, NE], f32, ffn)
        c8 = sb("c8", [P, NE], f32, ffn)
        t8 = sb("t8", [P, NE], f32, ffn)
        room = sb("room", [P, NE], f32, ffn)
        route = ExitStack()
        W1f = sb("W1f", [P, DK, FF], f32, ffn)
        W2f = sb("W2f", [P, FK, D], f32, ffn)
        W1s = sb("W1s", [P, 2, 2, DK, FF], bf16, ffn)
        W2s = sb("W2s", [P, 2, 2, FK, D], bf16, ffn)
        NST = -(-CAP // P)
        XE = sb("XE", [P, 2, NST, 2 * D], bf16, ffn)
        XT = sb("XT", [P, 2, 2 * DK, CAP], bf16, ffn)
        HH = sb("HH", [P, 2, FK, CAP], bf16, ffn)
        HL = sb("HL", [P, 2, FK, CAP], bf16, ffn)
        Y = sb("Y", [P, 2, NST, D], f32, ffn)
        ffn.close()
        comb = ExitStack()
        GY = sb("GY", [P, 4, TOPK, D], f32, comb)
        comb.close()
        ST = [(P * i, min(P, CAP - P * i)) for i in range(NST)]
        CH = [(0, (CAP + 1) // 2), ((CAP + 1) // 2, CAP // 2)]

        block = ctx.enter_context(nc.Block())

        @block.sync
        def _(sp):
            sp.dma_start(PT[:, :, :], patchesT.rearrange("(k p) n -> p k n", p=P)).then_inc(ld_tok, 16)
            sp.dma_start(TW[:, :, :], tokWT.rearrange("(k p) n -> p k n", p=P)).then_inc(ld_tok, 16)
            sp.dma_start(tb[:, :], tokb.unsqueeze(0)).then_inc(ld_tok, 16)
            for b in range(B):
                sp.dma_start(H[:, b, 1:, :], txt[b].rearrange("(i p) d -> p i d", p=P)).then_inc(ld_txt[b], 16)
                if b == 0:
                    sp.dma_start(wkv[:, :, :], WkvT.rearrange("(k p) n -> p k n", p=P)).then_inc(ld_att, 16)
                    sp.dma_start(wq[:, :, :], WqT.rearrange("(k p) n -> p k n", p=P)).then_inc(ld_att, 16)
                    sp.dma_start(q2l[:, :], q2lT).then_inc(ld_att, 16)
                    sp.dma_start(vu[LAT:2 * LAT, :], vup).then_inc(ld_att, 16)
                    sp.dma_start(wr[:, :, :], Wr.rearrange("(k p) n -> p k n", p=P)).then_inc(ld_att, 16)
                    sp.wait_ge(dve_const, 1)
                    wv = WoT.rearrange("(g j d) n -> j d g n", j=4, d=HD)
                    for j in range(4):
                        sp.dma_start(wo[32 * j + 1:32 * j + 1 + HD, :, :], wv[j]).then_inc(ld_att, 16)
            sp.dma_start(xe_d.rearrange("(p r) c -> p r c", p=P),
                         zero[:, :].unsqueeze(1).to_broadcast([P, SROWS // P, 2 * D])).then_inc(zeroed, 16)
            sp.dma_start(y_d[SLOTS:SLOTS + 1, :], zero[0:1, :].bitcast(f32)).then_inc(zeroed, 16)

            def split_out(which, u):
                stacks, rows = (Qs, QROWS) if which == 0 else (Ks, KROWS)
                sp.wait_ge(lo_ready, 2 * u + which + 1)
                sp.dma_start(xs_d[which, u].rearrange("s p t -> p s t"),
                             XS[:, which, :, :]).then_inc(split_stored[which], 16)
                sp.wait_ge(split_stored[which], 16 * (u + 1))
                if u >= 3:
                    n = 3 * UH * (u - 2) - 1
                    sp.wait_ge(t_full[n % 2], n // 2 + 1)
                for g, part in enumerate(rows):
                    sp.dma_start(stacks[u % 3][HD * g:HD * (g + 1), :, 0:T],
                                 xs_d[which, u, part].rearrange("(j d) t -> d j t", d=HD)
                                 ).then_inc(stack_ready[u % 3], 16)

            def max_rows(u):
                sp.wait_ge(nm_ready, u + 1)
                for g in range(3):
                    sp.dma_start(Qs[u % 3][CON + g:CON + g + 1, :, :],
                                 NS[:, g, :]).then_inc(maxrow_ready[u % 2], 16)

            def den_out(u, g):
                sp.wait_ge(o_used, 2 * u + g + 1)
                gg = 2 * (u % 2) + g
                sp.dma_start(dn_d[u // 2, 4 * gg:4 * gg + 4, :],
                             Of[0:P:32, gg, :]).then_inc(den_stored[(u // 2) % 2], 16)

            def den_spread(b):
                sp.wait_ge(den_stored[b % 2], 64 * (b // 2 + 1))
                if b == 0:
                    used(sp, ("embed", B - 1, 0))
                n = HEADS * T // 64
                sp.dma_start(DG[:, :], dn_d[b].rearrange("h t -> (h t)").rearrange("(p n) -> p n", n=n)
                             ).then_inc(den_packed, 16)
                sp.wait_ge(rden_ready, b + 1)
                sp.dma_start(rc_d[b].rearrange("h t -> (h t)").rearrange("(p n) -> p n", n=n),
                             DG[:, :]).then_inc(rden_stored, 16)
                sp.wait_ge(rden_stored, 16 * (b + 1))
                rv = rc_d[b].rearrange("(g j) t -> j g t", j=4)
                for j in range(4):
                    sp.dma_start(Rb[32 * j:32 * (j + 1), :, :],
                                 rv[j].partition_broadcast(32)).then_inc(rden_spread, 16)

            for job in order:
                k, a = job[0], job[1]
                if k == "Q":
                    split_out(0, a)
                elif k == "K":
                    split_out(1, a)
                elif k == "M":
                    max_rows(a)
                elif k == "PV":
                    den_out(a, job[2])
                elif k == "N":
                    den_spread(a)

            sp.wait_ge(idx_ready, 1)
            sp.dma_start(W1f[:, :, :], W1[0].rearrange("(k p) f -> p k f", p=P)).then_inc(w_loaded[0], 16)
            sp.dma_start(W2f[:, :, :], W2[0].rearrange("(k p) d -> p k d", p=P)).then_inc(w_loaded[0], 16)
            sp.wait_ge(scattered, 16 * TOPK * NT)

            def load_slots(e):
                nfull = CAP // P
                if e >= 2:
                    n = NST * (e - 1) - 1
                    sp.wait_ge(tr_full[n % 2], n // 2 + 1)
                sp.dma_start(XE[:, e % 2, 0:nfull, :],
                             xe_d[e * CAP:e * CAP + nfull * P, :].rearrange("(i p) c -> p i c", p=P)
                             ).then_inc(xe_loaded[e % 2], 16)
                sp.dma_start(XE[0:CAP - nfull * P, e % 2, nfull, :],
                             xe_d[e * CAP + nfull * P:(e + 1) * CAP, :]).then_inc(xe_loaded[e % 2], 16)

            load_slots(0)
            for e in range(NE):
                if e + 1 < NE:
                    sp.wait_ge(whi_ready, e + 1)
                    sp.wait_ge(wlo_ready, e + 1)
                    sp.dma_start(W1f[:, :, :], W1[e + 1].rearrange("(k p) f -> p k f", p=P)
                                 ).then_inc(w_loaded[(e + 1) % 2], 16)
                    sp.dma_start(W2f[:, :, :], W2[e + 1].rearrange("(k p) d -> p k d", p=P)
                                 ).then_inc(w_loaded[(e + 1) % 2], 16)
                    load_slots(e + 1)
                for i, (r0, n) in enumerate(ST):
                    q = e * NST + i
                    sp.wait_ge(y_used[q % 2], q // 2 + 1)
                    sp.dma_start(y_d[e * CAP + r0:e * CAP + r0 + n, :],
                                 Y[0:n, e % 2, i, :]).then_inc(y_stored[e % 2], 16)
            for t in range(NT):
                b, i = t // NQ, t % NQ
                sp.wait_ge(combined, t + 1)
                q0, n = QT[i]
                sp.dma_start(out[b, q0:q0 + n, :], H[0:n, b, i, :]).then_inc(stored, 16)
            sp.wait_ge(stored, 16 * NT)

        @block.gpsimd
        def _(pool):
            chain = [0]

            def link(ins):
                chain[0] += 1
                ins.then_inc(pool_chain, 1)
                pool.wait_ge(pool_chain, chain[0])

            link(nc.gpsimd.memset(ident[:, :], 0.0))
            link(nc.gpsimd.affine_select(out=ident[:, :], in_=ident[:, :], compare_op=ALU.not_equal, fill=1.0,
                                         base=0, pattern=[[-1, P]], channel_multiplier=1))
            nc.gpsimd.tensor_copy(identb[:, :], ident[:, :])
            link(nc.gpsimd.memset(maskn[:, :], 0.0))
            tri = maskn[:, T - P:T]
            link(nc.gpsimd.affine_select(out=tri, in_=tri, compare_op=ALU.is_ge, fill=NEG,
                                         base=0, pattern=[[-1, P]], channel_multiplier=1))
            link(nc.gpsimd.memset(trib[:, :], 1.0))
            link(nc.gpsimd.affine_select(out=trib[:, :], in_=trib[:, :], compare_op=ALU.is_gt, fill=0.0,
                                         base=0, pattern=[[1, P]], channel_multiplier=-1))
            link(nc.gpsimd.memset(valid[:, :, :], 1.0))
            for b in range(B):
                v = valid[:, b * NQ, :]
                link(nc.gpsimd.affine_select(out=v, in_=v, compare_op=ALU.is_gt, fill=0.0,
                                             base=NIMG, pattern=[[0, NE]], channel_multiplier=-1))
            nc.gpsimd.iota(iota8[:, :, :], pattern=[[0, NT], [1, NE]], base=0, channel_multiplier=0,
                           allow_small_or_imprecise_dtypes=True)
            nc.gpsimd.iota(base8[:, :, :], pattern=[[0, NT], [CAP, NE]], base=0, channel_multiplier=0,
                           allow_small_or_imprecise_dtypes=True)
            nc.gpsimd.memset(nhalf[:, :], -0.5).then_inc(pool_const, 1)

            norms = [0]

            def rstd():
                norms[0] += 1
                pool.wait_ge(mean_ready, norms[0])
                link(nc.gpsimd.tensor_scalar(ve[:, :], mv[:, :, 1], EPS, None, ALU.add))
                nc.gpsimd.tensor_tensor(rs[:, :], ve[:, :], nhalf[:, :], ALU.pow).then_inc(rstd_ready, 1)

            def low(which, u):
                pool.wait_ge(mid_ready, 2 * u + which + 1)
                nc.gpsimd.tensor_tensor(XS[:, which, 2, :], XR[:, which, :], XS[:, which, 1, :],
                                        ALU.subtract).then_inc(lo_ready, 1)

            def causal(u, j):
                hh = UH * u + j
                for i, (c, w) in enumerate(DIAG):
                    p = 0 if i == 0 else (1 if i == 1 else 2)
                    n = 3 * hh + p
                    pool.wait_ge(t_used[n % 2], n // 2 + 1)
                    v = Pr[:, hh % NP, c:c + w]
                    last = nc.gpsimd.affine_select(out=v, in_=v, compare_op=ALU.is_ge, fill=0.0,
                                                   base=0, pattern=[[1, w]], channel_multiplier=-1)
                last.then_inc(prob_ready, 1)

            for job in order:
                k, a = job[0], job[1]
                if k in ("ln1", "ln2"):
                    rstd()
                elif k == "Q":
                    low(0, a)
                elif k == "K":
                    low(1, a)
                elif k == "T":
                    causal(a, job[2])

            pool.wait_ge(idx_ready, 1)
            pool.wait_ge(zeroed, 32)
            for t in range(NT):
                n = QT[t % NQ][1]
                for c in range(TOPK):
                    nc.gpsimd.indirect_dma_start(
                        out=xe_d[:, :], out_offset=bass.IndirectOffsetOnAxis(ap=sidx[0:n, c, t:t + 1], axis=0),
                        in_=XHL[0:n, t, :], in_offset=None, bounds_check=SLOTS - 1, oob_is_err=False,
                    ).then_inc(scattered, 16)

            for e in range(NE):
                pool.wait_ge(w_loaded[e % 2], 32 * (e // 2 + 1))
                pool.wait_ge(whi_ready, e + 1)
                if e >= 2:
                    q = (e - 1) * NST - 1
                    pool.wait_ge(y_full[q % 2], q // 2 + 1)
                nc.gpsimd.tensor_tensor(W1s[:, e % 2, 1, :, :], W1f[:, :, :], W1s[:, e % 2, 0, :, :], ALU.subtract)
                nc.gpsimd.tensor_tensor(W2s[:, e % 2, 1, :, :], W2f[:, :, :], W2s[:, e % 2, 0, :, :],
                                        ALU.subtract).then_inc(wlo_ready, 1)

            for p in range(2):
                n = sum(1 for e in range(NE) if e % 2 == p)
                pool.wait_ge(y_stored[p], 16 * NST * n)
            for t in range(NT):
                n = QT[t % NQ][1]
                if t >= 4:
                    pool.wait_ge(combined, t - 3)
                for c in range(TOPK):
                    nc.gpsimd.indirect_dma_start(
                        out=GY[0:n, t % 4, c, :], out_offset=None, in_=y_d[:, :],
                        in_offset=bass.IndirectOffsetOnAxis(ap=gidx[0:n, c, t:t + 1], axis=0),
                    ).then_inc(gathered[t % 4], 16)

        @block.tensor
        def _(pe):
            pe.wait_ge(pool_const, 1)
            pe.wait_ge(dve_const, 2)

            def project(key, lhsT_of, rhs_of, nk, n=HT):
                bank = open_fill(pe, key)
                for k in range(nk):
                    last = nc.tensor.matmul(bank[:, 0:n], lhsT_of(k), rhs_of(k), start=(k == 0), stop=(k == nk - 1))
                last.then_inc(m_full[fills[key] % 2], 1)

            def embed(b):
                if b == 0:
                    pe.wait_ge(ld_tok, 48)
                bank = open_fill(pe, ("embed", b, 0))
                o = bank[0:NIMG, 0:D]
                for k in range(PK):
                    nc.tensor.matmul(o, PT[:, k, NIMG * b:NIMG * (b + 1)], TW[:, k, :], start=(k == 0), stop=False)
                nc.tensor.matmul(o, ones[0:1, 0:NIMG], tb[0:1, :], start=False, stop=True
                                 ).then_inc(m_full[fills[("embed", b, 0)] % 2], 1)

            def transpose_h(b):
                pe.wait_ge(xhat_ready, ln_count[("ln1", b)])
                for f in range(4):
                    k, tiles = f // 2, (QT[0:3] if f % 2 == 0 else QT[3:5])
                    bank = open_fill(pe, ("hT", b, f))
                    for q0, n in tiles:
                        i = QT.index((q0, n))
                        c = q0 - tiles[0][0]
                        last = nc.tensor.transpose(bank[:, c:c + n], xh[0:n, i, P * k:P * (k + 1)], ident[0:n, 0:n])
                    last.then_inc(m_full[fills[("hT", b, f)] % 2], 1)

            def kv(b):
                if b == 0:
                    pe.wait_ge(ld_att, 16 * 9)
                for f in range(4):
                    used(pe, ("hT", b, f))
                for hf in range(2):
                    project(("kv", b, hf), lambda k: wkv[:, k, :], lambda k: hnT[:, k, HT * hf:HT * (hf + 1)], DK)

            def values(b):
                for hf in range(2):
                    used(pe, ("kv", b, hf))
                for f in range(3):
                    bank = open_fill(pe, ("V", b, f))
                    for i in range(2 * f, min(2 * f + 2, len(KT))):
                        s0, n = KT[i]
                        last = nc.tensor.matmul(bank[0:n, D * (i % 2):D * (i % 2 + 1)], lat[LAT:2 * LAT, s0:s0 + n],
                                                vu[LAT:2 * LAT, :], start=True, stop=True)
                    last.then_inc(m_full[fills[("V", b, f)] % 2], 1)

            def queries(u):
                for f in range(4):
                    used(pe, ("hT", u // 2, f))
                m = P * (u % 2)
                for hf in range(2):
                    project(("Q", u, hf), lambda k: wq[:, k, m:m + P], lambda k: hnT[:, k, HT * hf:HT * (hf + 1)], DK)

            def keys(u):
                for hf in range(2):
                    used(pe, ("kv", u // 2, hf))
                m = P * (u % 2)
                for hf in range(2):
                    project(("K", u, hf), lambda k: q2l[:, m:m + P], lambda k: lat[0:LAT, HT * hf:HT * (hf + 1)], 1)

            def scores(u, j):
                if j == 0:
                    pe.wait_ge(stack_ready[u % 3], 16 * 12 * (u // 3 + 1))
                for p, piece in enumerate(SPIECE):
                    n = 3 * (UH * u + j) + p
                    if n >= 2:
                        pe.wait_ge(s_used[n % 2], n // 2)
                    for i, s0, w, c in piece:
                        q0, nq = QT[i]
                        last = nc.tensor.matmul(bankS[n % 2][0:nq, c:c + w], Qs[u % 3][0:CON, j, q0:q0 + nq],
                                                Ks[u % 3][0:CON, j, s0:s0 + w], start=True, stop=True)
                    last.then_inc(s_full[n % 2], 1)

            def transpose_max(u):
                pe.wait_ge(max_ready, u + 1)
                for f in range(2):
                    tiles = QT[0:3] if f == 0 else QT[3:5]
                    bank = open_fill(pe, ("M", u, f))
                    for q0, n in tiles:
                        i = QT.index((q0, n))
                        c = q0 - tiles[0][0]
                        last = nc.tensor.transpose(bank[0:UH, c:c + n], mx[0:n, u % 2, i, :], ident[0:n, 0:n])
                    last.then_inc(m_full[fills[("M", u, f)] % 2], 1)

            def scores_t(u, j):
                if j == 0:
                    pe.wait_ge(maxrow_ready[u % 2], 48 * (u // 2 + 1))
                for p, piece in enumerate(TPIECE):
                    n = 3 * (UH * u + j) + p
                    if n >= 2:
                        pe.wait_ge(t_used[n % 2], n // 2)
                    for i, q0, w, c in piece:
                        last = nc.tensor.matmul(bankT[n % 2][:, c:c + w], Ks[u % 3][0:CONM, j, P * i:P * (i + 1)],
                                                Qs[u % 3][0:CONM, j, q0:q0 + w], start=True, stop=True)
                    last.then_inc(t_full[n % 2], 1)

            def context(u, g):
                b, gi = u // 2, 2 * u + g
                pe.wait_ge(prob_ready, 4 * (gi + 1))
                used(pe, ("V", b, 2))
                used(pe, ("V", b, 1))
                if gi >= 1:
                    pe.wait_ge(o_used, gi)
                firsts = [SEG[0], next(s for s in SEG if s[0] == 1)]
                lasts = [[s for s in SEG if s[0] == h][-1] for h in range(2)]
                for s in SEG:
                    half, kt, c, q0, w = s
                    n = KT[kt][1]
                    for j in range(4):
                        hh = UH * u + 4 * g + j
                        last = nc.tensor.matmul(
                            bankO[32 * j:32 * j + 1 + HD, half, q0 - HT * half:q0 - HT * half + w],
                            V[0:n, b % 2, kt, (UH * (u % 2) + 4 * g + j), :],
                            Pr[0:n, hh % NP, c:c + w], start=(s in firsts), stop=(s in lasts),
                            tile_position=(0, 32 * j))
                last.then_inc(o_full, 1)

            def attend_out(b):
                pe.wait_ge(ctx_ready, b + 1)
                for i, (q0, n) in enumerate(QT):
                    bank = open_fill(pe, ("W", b, i))
                    for g in range(4):
                        last = nc.tensor.matmul(bank[0:n, 0:D], Of[:, g, q0:q0 + n], wo[:, g, :],
                                                start=(g == 0), stop=(g == 3))
                    last.then_inc(m_full[fills[("W", b, i)] % 2], 1)

            def router(b):
                pe.wait_ge(xhat_ready, ln_count[("ln2", b)])
                for i in range(NQ + 1):
                    if i < NQ:
                        n = QT[i][1]
                        bank = open_fill(pe, ("R", b, fR(i, 0)))
                        for k in range(DK):
                            last = nc.tensor.transpose(bank[:, k * n:(k + 1) * n], xh[0:n, i, P * k:P * (k + 1)],
                                                       ident[0:n, 0:n])
                        last.then_inc(m_full[fills[("R", b, fR(i, 0))] % 2], 1)
                    if i >= 1:
                        n = QT[i - 1][1]
                        used(pe, ("R", b, fR(i - 1, 0)))
                        bank = open_fill(pe, ("R", b, fR(i - 1, 1)))
                        for k in range(DK):
                            last = nc.tensor.matmul(bank[0:n, 0:NE], xnT[:, (i - 1) % 2, k * n:(k + 1) * n],
                                                    wr[:, k, :], start=(k == 0), stop=(k == DK - 1))
                        last.then_inc(m_full[fills[("R", b, fR(i - 1, 1))] % 2], 1)

            for job in order:
                k, a = job[0], job[1]
                if k == "embed":
                    embed(a)
                elif k == "hT":
                    transpose_h(a)
                elif k == "kv":
                    kv(a)
                elif k == "V":
                    values(a)
                elif k == "Q":
                    queries(a)
                elif k == "K":
                    keys(a)
                elif k == "S":
                    scores(a, job[2])
                elif k == "M":
                    transpose_max(a)
                elif k == "T":
                    scores_t(a, job[2])
                elif k == "PV":
                    context(a, job[2])
                elif k == "W":
                    attend_out(a)
                elif k == "R":
                    router(a)

            n_in = 0
            for r in range(ROUNDS):
                n_in += 1
                pe.wait_ge(cnt_in, n_in)
                bank = open_fill(pe, ("cnt", r))
                nc.tensor.matmul(bank[:, 0:NE], ones[:, :], c8[:, :], start=True, stop=True
                                 ).then_inc(m_full[fills[("cnt", r)] % 2], 1)
            n_in += 1
            pe.wait_ge(cnt_in, n_in)
            bank = open_fill(pe, ("cgt", 0))
            nc.tensor.matmul(bank[:, 0:NE], ones[:, :], c8[:, :], start=True, stop=True
                             ).then_inc(m_full[fills[("cgt", 0)] % 2], 1)
            for key in (("ceq", 0), ("pos", 0)):
                n_in += 1
                pe.wait_ge(cnt_in, n_in)
                bank = open_fill(pe, key)
                o = bank[:, 0:NT * NE].rearrange("p (t e) -> p t e", e=NE)
                nc.tensor.matmul(o, trib[:, :], Xb[:, :, :], start=True, stop=False)
                for t in range(NT - 1):
                    last = nc.tensor.matmul(o[:, t + 1:, :], onesb[:, :],
                                            Xb[:, t:t + 1, :].to_broadcast([P, NT - 1 - t, NE]),
                                            start=False, stop=(t == NT - 2))
                last.then_inc(m_full[fills[key] % 2], 1)

            trb = [bankT[i][:, 0:256].bitcast(bf16).rearrange("p (c s) -> p c s", c=4) for i in range(2)]
            hb = [bankS[0], bankS[1], bankO[:, 0, :], bankO[:, 1, :]]

            def slots_t(e):
                pe.wait_ge(xe_loaded[e % 2], 32 * (e // 2 + 1))
                for i, (r0, n) in enumerate(ST):
                    q = e * NST + i
                    if q >= 2:
                        pe.wait_ge(tr_used[q % 2], q // 2)
                    for c in range(4):
                        last = nc.tensor.transpose(trb[q % 2][:, c, 0:n], XE[0:n, e % 2, i, P * c:P * (c + 1)],
                                                   identb[0:n, 0:n])
                    last.then_inc(tr_full[q % 2], 1)

            def up(e):
                pe.wait_ge(wlo_ready, e + 1)
                pe.wait_ge(whi_ready, e + 1)
                for i in (NST - 2, NST - 1):
                    q = e * NST + i
                    pe.wait_ge(tr_used[q % 2], q // 2 + 1)
                for ft in range(FK):
                    banks = []
                    for hf in range(2):
                        q = 2 * (e * FK + ft) + hf
                        if q >= 4:
                            pe.wait_ge(h_used[q % 4], q // 4)
                        banks.append(hb[q % 4])
                    terms = [(k, a, c) for k in range(DK) for a, c in ((0, 0), (0, 1), (1, 0))]
                    for ti, (k, a, c) in enumerate(terms):
                        for hf, (c0, w) in enumerate(CH):
                            last = nc.tensor.matmul(banks[hf][:, 0:w], W1s[:, e % 2, a, k, P * ft:P * (ft + 1)],
                                                    XT[:, e % 2, 2 * c + k, c0:c0 + w],
                                                    start=(ti == 0), stop=(ti == len(terms) - 1))
                            if ti == len(terms) - 1:
                                last.then_inc(h_full[(2 * (e * FK + ft) + hf) % 4], 1)

            def down(e):
                for q in range(2 * (e + 1) * FK - 4, 2 * (e + 1) * FK):
                    pe.wait_ge(h_used[q % 4], q // 4 + 1)
                for i, (r0, n) in enumerate(ST):
                    q = e * NST + i
                    if q >= 2:
                        pe.wait_ge(y_used[q % 2], q // 2)
                    for ft in range(FK):
                        for ti, (a, c) in enumerate(((0, 0), (0, 1), (1, 0))):
                            hid = (HH, HL)[a]
                            last = nc.tensor.matmul(bankM[q % 2][0:n, 0:D], hid[:, e % 2, ft, r0:r0 + n],
                                                    W2s[:, e % 2, c, ft, :], start=(ft == 0 and ti == 0),
                                                    stop=(ft == FK - 1 and ti == 2))
                    last.then_inc(y_full[q % 2], 1)

            slots_t(0)
            for e in range(NE):
                up(e)
                if e + 1 < NE:
                    slots_t(e + 1)
                down(e)

        @block.scalar
        def _(act):
            def drain(key, dst, src):
                filled(act, key)
                nc.scalar.activation(dst, src, ACT.Copy).then_inc(m_used[fills[key] % 2], 1)

            def high(name, which, u):
                if u >= 1:
                    act.wait_ge(split_stored[which], 16 * u)
                for hf in range(2):
                    key = (name, u, hf)
                    filled(act, key)
                    nc.scalar.activation(XS[:, which, 0, HT * hf:HT * (hf + 1)], bankM[fills[key] % 2][:, 0:HT],
                                         ACT.Copy).then_inc(hi_ready, 1)

            for job in order:
                k, a = job[0], job[1]
                if k == "hT":
                    for f in range(4):
                        c0, w = (0, QT[3][0]) if f % 2 == 0 else (QT[3][0], 2 * P)
                        key = ("hT", a, f)
                        drain(key, hnT[:, f // 2, c0:c0 + w], bankM[fills[key] % 2][:, 0:w])
                elif k == "kv":
                    for hf in range(2):
                        key = ("kv", a, hf)
                        drain(key, lat[:, HT * hf:HT * (hf + 1)], bankM[fills[key] % 2][:, 0:HT])
                elif k == "V":
                    if a == 0:
                        act.wait_ge(dve_const, 2)
                    for f in range(3):
                        key = ("V", a, f)
                        filled(act, key)
                        for i in range(2 * f, min(2 * f + 2, len(KT))):
                            n = KT[i][1]
                            src = bankM[fills[key] % 2][0:n, D * (i % 2):D * (i % 2 + 1)]
                            last = nc.scalar.activation(V[0:n, a % 2, i, :, 1:1 + HD],
                                                        src.rearrange("p (h d) -> p h d", d=HD), ACT.Copy)
                        last.then_inc(m_used[fills[key] % 2], 1)
                elif k == "Q":
                    high("Q", 0, a)
                elif k == "K":
                    high("K", 1, a)
                elif k == "M":
                    if a >= 1:
                        act.wait_ge(maxrow_ready[(a - 1) % 2], 48 * ((a - 1) // 2 + 1))
                    for f in range(2):
                        c0, w = (0, QT[3][0]) if f == 0 else (QT[3][0], 2 * P)
                        key = ("M", a, f)
                        filled(act, key)
                        nc.scalar.activation(NS[:, 0, c0:c0 + w], bankM[fills[key] % 2][0:UH, 0:w], ACT.Copy,
                                             scale=-1.0).then_inc(nmhi_ready, 1)
                elif k == "T":
                    hh = UH * a + job[2]
                    if hh >= NP:
                        act.wait_ge(o_full, (hh - NP) // 4 + 1)
                    for p, piece in enumerate(TPIECE):
                        n = 3 * hh + p
                        w = sum(x[2] for x in piece)
                        act.wait_ge(t_full[n % 2], n // 2 + 1)
                        nc.scalar.activation(Pr[:, hh % NP, TOFF[p]:TOFF[p] + w], bankT[n % 2][:, 0:w], ACT.Exp,
                                             scale=SCALE).then_inc(t_used[n % 2], 1)
                elif k == "PV":
                    gi = 2 * a + job[2]
                    gg = gi % 4
                    act.wait_ge(o_full, gi + 1)
                    if gi >= 4:
                        used(act, ("W", gi // 4 - 1, NQ - 1))
                        act.wait_ge(den_stored[(gi // 4 - 1) % 2], 64 * ((gi // 4 - 1) // 2 + 1))
                    nc.scalar.activation(Of[:, gg, :].rearrange("p (h t) -> p h t", h=2), bankO[:, :, 0:HT],
                                         ACT.Copy).then_inc(o_used, 1)
                elif k == "R":
                    for i in range(NQ):
                        n = QT[i][1]
                        if i >= 2:
                            filled(act, ("R", a, fR(i - 2, 1)))
                        key = ("R", a, fR(i, 0))
                        drain(key, xnT[:, i % 2, 0:DK * n], bankM[fills[key] % 2][:, 0:DK * n])
            act.wait_ge(rexp_in, 1)
            nc.scalar.activation(E2[:, :, :], EP[:, :, :], ACT.Exp).then_inc(rexp, 1)

            hb = [bankS[0], bankS[1], bankO[:, 0, :], bankO[:, 1, :]]
            for e in range(NE):
                for ft in range(FK):
                    for hf, (c0, w) in enumerate(CH):
                        q = 2 * (e * FK + ft) + hf
                        act.wait_ge(h_full[q % 4], q // 4 + 1)
                        nc.scalar.activation(HH[:, e % 2, ft, c0:c0 + w], hb[q % 4][:, 0:w],
                                             ACT.Relu).then_inc(hhi_ready, 1)
                for i, (r0, n) in enumerate(ST):
                    q = e * NST + i
                    act.wait_ge(y_full[q % 2], q // 2 + 1)
                    if e >= 2 and i == 0:
                        act.wait_ge(y_stored[e % 2], 16 * NST * (e // 2))
                    nc.scalar.activation(Y[0:n, e % 2, i, :], bankM[q % 2][0:n, 0:D],
                                         ACT.Copy).then_inc(y_used[q % 2], 1)

        @block.vector
        def _(dve):
            chain = [0]

            def link(ins):
                chain[0] += 1
                ins.then_inc(dve_chain, 1)
                dve.wait_ge(dve_chain, chain[0])

            nc.vector.memset(wo[:, :, :], 0.0)
            nc.vector.memset(zero[:, :], 0.0).then_inc(dve_const, 1)
            nc.vector.memset(ones[:, :], 1.0)
            nc.vector.memset(onesb[:, :], 1.0)
            for b in range(B):
                nc.vector.memset(H[:, b, 0, :], 0.0)
            nc.vector.memset(V[:, :, :, :, 0:1], 1.0)
            for i in range(3):
                nc.vector.memset(Ks[i][:, :, T:SP_], 0.0)
                nc.vector.memset(Ks[i][CON:P, :, 0:T], 1.0)
            nc.vector.memset(mx[:, :, :, :], 0.0)
            nc.vector.memset(bankO[:, :, :], 0.0)
            nc.vector.memset(LG[:, :, :], 0.0).then_inc(dve_const, 1)

            norms = [0]

            def normalise(b):
                for i in range(NQ):
                    last = nc.vector.bn_stats(st[:, i, :], H[:, b, i, :])
                link(last)
                if norms[0]:
                    pass
                for i in range(NQ):
                    last = nc.vector.bn_aggr(mv[:, i, :], st[:, i, :])
                last.then_inc(mean_ready, 1)
                norms[0] += 1
                dve.wait_ge(mean_ready, norms[0])
                dve.wait_ge(rstd_ready, norms[0])
                for i in range(NQ):
                    last = nc.vector.tensor_scalar(xh[:, i, :], H[:, b, i, :], mv[:, i, 0:1], rs[:, i:i + 1],
                                                   ALU.subtract, ALU.mult)
                last.then_inc(xhat_ready, 1)
                dve.wait_ge(xhat_ready, norms[0])

            def xh_free():
                prev = ln_order[norms[0] - 1]
                if prev[0] == "ln1":
                    filled(dve, ("hT", prev[1], 3))
                    filled(dve, ("hT", prev[1], 2))
                else:
                    filled(dve, ("R", prev[1], fR(NQ - 1, 0)))

            def middle(name, which, u):
                if u >= 1:
                    dve.wait_ge(lo_ready, 2 * (u - 1) + which + 1)
                for hf in range(2):
                    key = (name, u, hf)
                    filled(dve, key)
                    dve.wait_ge(hi_ready, 4 * u + 2 * which + hf + 1)
                    c = slice(HT * hf, HT * (hf + 1))
                    last = nc.vector.tensor_tensor(XR[:, which, c], bankM[fills[key] % 2][:, 0:HT],
                                                   XS[:, which, 0, c], ALU.subtract)
                    last.then_inc(m_used[fills[key] % 2], 1)
                for hf in range(2):
                    used(dve, (name, u, hf))
                if u >= 1:
                    dve.wait_ge(split_stored[which], 16 * u)
                nc.vector.tensor_copy(XS[:, which, 1, :], XR[:, which, :]).then_inc(mid_ready, 1)

            def maxima(u, j):
                for p, piece in enumerate(SPIECE):
                    n = 3 * (UH * u + j) + p
                    dve.wait_ge(s_full[n % 2], n // 2 + 1)
                    for i, s0, w, c in piece:
                        nq = QT[i][1]
                        m0 = T - P if i == 0 else (s0 if i == NQ - 1 else T - w)
                        slot = NQ if (i == NQ - 1 and s0 > 0) else i
                        last = nc.vector.tensor_tensor_reduce(
                            out=bankS[n % 2][0:nq, c:c + w], in0=bankS[n % 2][0:nq, c:c + w], in1=maskn[0:nq, m0:m0 + w],
                            scale=1.0, scalar=-3.0e38, op0=ALU.add, op1=ALU.max,
                            accum_out=mx[0:nq, u % 2, slot, j:j + 1])
                    last.then_inc(s_used[n % 2], 1)

            def negative_max(u):
                for p in range(3):
                    n = 3 * (UH * u + UH - 1) + p
                    dve.wait_ge(s_used[n % 2], n // 2 + 1)
                nc.vector.tensor_tensor(mx[:, u % 2, NQ - 1, :], mx[:, u % 2, NQ - 1, :], mx[:, u % 2, NQ, :],
                                        ALU.max).then_inc(max_ready, 1)
                if u >= 1:
                    dve.wait_ge(maxrow_ready[(u - 1) % 2], 48 * ((u - 1) // 2 + 1))
                for f in range(2):
                    c0, w = (0, QT[3][0]) if f == 0 else (QT[3][0], 2 * P)
                    key = ("M", u, f)
                    filled(dve, key)
                    dve.wait_ge(nmhi_ready, 2 * u + f + 1)
                    nc.vector.scalar_tensor_tensor(out=NR[:, c0:c0 + w], in0=bankM[fills[key] % 2][0:UH, 0:w],
                                                   scalar=-1.0, in1=NS[:, 0, c0:c0 + w], op0=ALU.mult,
                                                   op1=ALU.subtract).then_inc(m_used[fills[key] % 2], 1)
                for f in range(2):
                    used(dve, ("M", u, f))
                link(nc.vector.tensor_copy(NS[:, 1, :], NR[:, :]))
                nc.vector.tensor_tensor(NS[:, 2, :], NR[:, :], NS[:, 1, :], ALU.subtract).then_inc(nm_ready, 1)

            for job in order:
                k, a = job[0], job[1]
                if k == "embed":
                    key = ("embed", a, 0)
                    filled(dve, key)
                    if a == 0:
                        dve.wait_ge(dve_const, 2)
                    nc.vector.tensor_copy(H[0:NIMG, a, 0, :], bankM[fills[key] % 2][0:NIMG, 0:D]
                                          ).then_inc(m_used[fills[key] % 2], 1)
                elif k == "ln1":
                    dve.wait_ge(ld_txt[a], 16)
                    used(dve, ("embed", a, 0))
                    if norms[0]:
                        xh_free()
                    normalise(a)
                elif k == "Q":
                    middle("Q", 0, a)
                elif k == "K":
                    middle("K", 1, a)
                elif k == "S":
                    if a == 0 and job[2] == 0:
                        dve.wait_ge(pool_const, 1)
                    maxima(a, job[2])
                elif k == "M":
                    negative_max(a)
                elif k == "W":
                    dve.wait_ge(rden_spread, 64 * (a + 1))
                    dve.wait_ge(o_used, 4 * (a + 1))
                    dve.wait_ge(den_stored[a % 2], 64 * (a // 2 + 1))
                    nc.vector.tensor_tensor(Of[:, :, :], Of[:, :, :], Rb[:, :, :], ALU.mult).then_inc(ctx_ready, 1)
                    for i, (q0, n) in enumerate(QT):
                        key = ("W", a, i)
                        filled(dve, key)
                        nc.vector.tensor_tensor(H[0:n, a, i, :], bankM[fills[key] % 2][0:n, 0:D], H[0:n, a, i, :],
                                                ALU.add).then_inc(m_used[fills[key] % 2], 1)
                elif k == "N":
                    dve.wait_ge(den_packed, 16 * (a + 1))
                    nc.vector.reciprocal(DG[:, :], DG[:, :]).then_inc(rden_ready, 1)
                elif k == "ln2":
                    used(dve, ("W", a, NQ - 2))
                    used(dve, ("W", a, NQ - 1))
                    xh_free()
                    normalise(a)
                    ts = slice(a * NQ, (a + 1) * NQ)
                    link(nc.vector.tensor_copy(XHL[:, ts, 0:D], xh[:, :, :]))
                    link(nc.vector.tensor_tensor(XHL[:, ts, D:2 * D], xh[:, :, :], XHL[:, ts, 0:D], ALU.subtract))
                elif k == "R":
                    for i in range(NQ):
                        key = ("R", a, fR(i, 1))
                        n = QT[i][1]
                        filled(dve, key)
                        nc.vector.tensor_copy(LG[0:n, a * NQ + i, :], bankM[fills[key] % 2][0:n, 0:NE]
                                              ).then_inc(m_used[fills[key] % 2], 1)

            used(dve, ("R", B - 1, fR(NQ - 1, 1)))
            dve.wait_ge(pool_const, 1)
            bc = [P, NT, NE]

            def wide(x):
                return x.unsqueeze(2).to_broadcast(bc)

            def over_tiles(x):
                return x.unsqueeze(1).to_broadcast(bc)

            link(nc.vector.reduce_max(r20[:, 0, :], LG[:, :, :], AX))
            nc.vector.tensor_tensor(EP[:, :, :], LG[:, :, :], wide(r20[:, 0, :]), ALU.subtract).then_inc(rexp_in, 1)
            dve.wait_ge(rexp, 1)
            link(nc.vector.reduce_sum(r20[:, 1, :], E2[:, :, :], AX))
            link(nc.vector.reciprocal(r20[:, 2, :], r20[:, 1, :]))
            link(nc.vector.tensor_tensor(EP[:, :, :], E2[:, :, :], wide(r20[:, 2, :]), ALU.mult))
            for t in range(NT):
                last = nc.vector.max(v8[:, t, :], EP[:, t, :])
            link(last)
            for t in range(NT):
                last = nc.vector.max_index(i8[:, t, :], v8[:, t, :], EP[:, t, :])
            link(last)
            link(nc.vector.tensor_copy(i8f[:, :, :], i8[:, :, :]))
            for c in range(TOPK):
                link(nc.vector.tensor_tensor(E2[:, :, :], iota8[:, :, :], wide(i8f[:, :, c]), ALU.is_equal))
                link(nc.vector.tensor_tensor(OH[:, c, :, :], E2[:, :, :], valid[:, :, :], ALU.mult))
            link(nc.vector.tensor_tensor(E3[:, :, :], OH[:, 0, :, :], OH[:, 1, :, :], ALU.add))
            link(nc.vector.tensor_tensor(G[:, :, :], EP[:, :, :], E3[:, :, :], ALU.mult))
            link(nc.vector.tensor_scalar(E2[:, :, :], E3[:, :, :], 1.0, None, ALU.subtract))
            link(nc.vector.tensor_tensor(G[:, :, :], G[:, :, :], E2[:, :, :], ALU.add))

            n_in = 0
            link(nc.vector.memset(thr[:, :], 0.0))

            def count(src):
                nonlocal_n = src.rearrange("p t e -> p e t")
                nc.vector.reduce_sum(c8[:, :], nonlocal_n, AX).then_inc(cnt_in, 1)

            for r in range(ROUNDS):
                bit = 1 << (ROUNDS - 1 - r)
                link(nc.vector.tensor_scalar(cand[:, :].bitcast(u32), thr[:, :].bitcast(u32), bit, None,
                                             ALU.bitwise_or))
                link(nc.vector.tensor_tensor(E2[:, :, :], G[:, :, :], over_tiles(cand[:, :]), ALU.is_ge))
                count(E2[:, :, :])
                key = ("cnt", r)
                filled(dve, key)
                nc.vector.scalar_tensor_tensor(out=t8[:, :], in0=bankM[fills[key] % 2][:, 0:NE], scalar=float(CAP),
                                               in1=cand[:, :], op0=ALU.is_ge, op1=ALU.mult
                                               ).then_inc(m_used[fills[key] % 2], 1)
                used(dve, key)
                link(nc.vector.tensor_tensor(thr[:, :], thr[:, :], t8[:, :], ALU.max))
            link(nc.vector.tensor_tensor(KEEP[:, :, :], G[:, :, :], over_tiles(thr[:, :]), ALU.is_gt))
            count(KEEP[:, :, :])
            key = ("cgt", 0)
            filled(dve, key)
            nc.vector.tensor_scalar(room[:, :], bankM[fills[key] % 2][:, 0:NE], -1.0, float(CAP), ALU.mult, ALU.add
                                    ).then_inc(m_used[fills[key] % 2], 1)
            link(nc.vector.tensor_tensor(E2[:, :, :], G[:, :, :], over_tiles(thr[:, :]), ALU.is_equal))
            nc.vector.tensor_copy(Xb[:, :, :], E2[:, :, :]).then_inc(cnt_in, 1)
            key = ("ceq", 0)
            filled(dve, key)
            used(dve, ("cgt", 0))
            nc.vector.tensor_tensor(E3[:, :, :], bankM[fills[key] % 2][:, 0:NT * NE].rearrange("p (t e) -> p t e", e=NE),
                                    over_tiles(room[:, :]), ALU.is_lt).then_inc(m_used[fills[key] % 2], 1)
            used(dve, key)
            link(nc.vector.tensor_tensor(E3[:, :, :], E3[:, :, :], E2[:, :, :], ALU.mult))
            link(nc.vector.tensor_tensor(KEEP[:, :, :], KEEP[:, :, :], E3[:, :, :], ALU.add))
            nc.vector.tensor_copy(Xb[:, :, :], KEEP[:, :, :]).then_inc(cnt_in, 1)
            key = ("pos", 0)
            filled(dve, key)
            nc.vector.tensor_tensor(POS[:, :, :], bankM[fills[key] % 2][:, 0:NT * NE].rearrange("p (t e) -> p t e", e=NE),
                                    base8[:, :, :], ALU.add).then_inc(m_used[fills[key] % 2], 1)
            used(dve, key)
            for c in range(TOPK):
                link(nc.vector.tensor_tensor(E2[:, :, :], OH[:, c, :, :], KEEP[:, :, :], ALU.mult))
                link(nc.vector.reduce_sum(r20[:, 0, :], E2[:, :, :], AX))
                link(nc.vector.tensor_tensor(E3[:, :, :], E2[:, :, :], POS[:, :, :], ALU.mult))
                link(nc.vector.reduce_sum(r20[:, 1, :], E3[:, :, :], AX))
                link(nc.vector.tensor_tensor(gate[:, c, :], r20[:, 0, :], v8[:, :, c], ALU.mult))
                link(nc.vector.tensor_scalar(r20[:, 2, :], r20[:, 0, :], -65536.0, 65536.0, ALU.mult, ALU.add))
                link(nc.vector.tensor_tensor(r20[:, 3, :], r20[:, 2, :], r20[:, 1, :], ALU.add))
                link(nc.vector.tensor_copy(sidx[:, c, :], r20[:, 3, :]))
                last = nc.vector.tensor_scalar(gidx[:, c, :], r20[:, 3, :], float(SLOTS), None, ALU.min)
                if c < TOPK - 1:
                    link(last)
            last.then_inc(idx_ready, 1)

            trb = [bankT[i][:, 0:256].bitcast(bf16).rearrange("p (c s) -> p c s", c=4) for i in range(2)]
            hb = [bankS[0], bankS[1], bankO[:, 0, :], bankO[:, 1, :]]

            def weights_high(e):
                dve.wait_ge(w_loaded[e % 2], 32 * (e // 2 + 1))
                if e >= 2:
                    q = (e - 1) * NST - 1
                    dve.wait_ge(y_full[q % 2], q // 2 + 1)
                nc.vector.tensor_copy(W1s[:, e % 2, 0, :, :], W1f[:, :, :])
                nc.vector.tensor_copy(W2s[:, e % 2, 0, :, :], W2f[:, :, :]).then_inc(whi_ready, 1)

            def slots_in(e):
                if e >= 2:
                    q = 2 * (e - 1) * FK - 1
                    dve.wait_ge(h_full[q % 4], q // 4 + 1)
                for i, (r0, n) in enumerate(ST):
                    q = e * NST + i
                    dve.wait_ge(tr_full[q % 2], q // 2 + 1)
                    nc.vector.tensor_copy(XT[:, e % 2, :, r0:r0 + n], trb[q % 2][:, :, 0:n]).then_inc(tr_used[q % 2], 1)

            weights_high(0)
            slots_in(0)
            for e in range(NE):
                if e >= 2:
                    q = (e - 1) * NST - 1
                    dve.wait_ge(y_full[q % 2], q // 2 + 1)
                for ft in range(FK):
                    for hf, (c0, w) in enumerate(CH):
                        q = 2 * (e * FK + ft) + hf
                        dve.wait_ge(hhi_ready, q + 1)
                        nc.vector.scalar_tensor_tensor(out=HL[:, e % 2, ft, c0:c0 + w], in0=hb[q % 4][:, 0:w], scalar=0.0,
                                                       in1=HH[:, e % 2, ft, c0:c0 + w], op0=ALU.max,
                                                       op1=ALU.subtract).then_inc(h_used[q % 4], 1)
                    if ft == 1 and e + 1 < NE:
                        weights_high(e + 1)
                if e + 1 < NE:
                    slots_in(e + 1)

            for t in range(NT):
                b, i = t // NQ, t % NQ
                n = QT[i][1]
                dve.wait_ge(gathered[t % 4], 32 * (t // 4 + 1))
                link(nc.vector.scalar_tensor_tensor(out=H[0:n, b, i, :], in0=GY[0:n, t % 4, 0, :],
                                                    scalar=gate[0:n, 0, t:t + 1], in1=H[0:n, b, i, :],
                                                    op0=ALU.mult, op1=ALU.add))
                nc.vector.scalar_tensor_tensor(out=H[0:n, b, i, :], in0=GY[0:n, t % 4, 1, :],
                                               scalar=gate[0:n, 1, t:t + 1], in1=H[0:n, b, i, :],
                                               op0=ALU.mult, op1=ALU.add).then_inc(combined, 1)


def kernel(**inputs):
    import numpy as np
    import concourse.bacc as bacc
    from concourse import mybir as mb
    from concourse.bass_utils import run_bass_kernel_spmd as run

    def c(a):
        return np.ascontiguousarray(a)

    x = np.asarray(inputs["x"])
    nb, ch, hh, ww = x.shape
    p = 16
    pt = x.reshape(nb, ch, hh // p, p, ww // p, p).transpose(0, 2, 3, 1, 4, 5).reshape(-1, ch * p * p).T
    q2l = np.asarray(inputs["L0_attn_q_to_latent"])
    vu = np.asarray(inputs["L0_attn_v_up"])
    arrays = {
        "patchesT": c(pt), "txt": c(inputs["txt"]), "tokWT": c(np.asarray(inputs["L0_tok_W"]).T),
        "tokb": c(inputs["L0_tok_b"]), "WqT": c(np.asarray(inputs["L0_attn_Wq"]).T),
        "WkvT": c(np.concatenate([np.asarray(inputs["L0_attn_Wk_down"]), np.asarray(inputs["L0_attn_Wv_down"])], 0).T),
        "q2lT": c(q2l.transpose(2, 0, 1).reshape(q2l.shape[2], -1)),
        "vup": c(vu.transpose(1, 0, 2).reshape(vu.shape[1], -1)),
        "WoT": c(np.asarray(inputs["L0_attn_Wout"]).T), "Wr": c(inputs["L0_ffn_Wr"]),
        "W1": c(inputs["L0_ffn_W1"]), "W2": c(inputs["L0_ffn_W2"]),
    }
    nc = bacc.Bacc("TRN2", target_bir_lowering=False, num_devices=1)
    args = [nc.dram_tensor(k, a.shape, mb.dt.from_np(a.dtype), kind="ExternalInput").ap() for k, a in arrays.items()]
    nb, nt, d = arrays["txt"].shape
    t = nt + arrays["patchesT"].shape[1] // nb
    o = nc.dram_tensor("out", (nb, t, d), mb.dt.float32, kind="ExternalOutput").ap()
    early_fusion_kernel(nc, *args, o)
    r = run(nc, [arrays], core_ids=[0])
    return r.results[0]["out"]
```

```python
import concourse.bass as bass
from concourse import mybir
from contextlib import ExitStack


def early_fusion_kernel(nc, patchesT, txt, tokWT, tokb, WqT, WkvT, q2lT, vup, WoT, Wr, W1, W2, out):
    f32, bf16, u32 = mybir.dt.float32, mybir.dt.bfloat16, mybir.dt.uint32
    ALU = mybir.AluOpType
    ACT = mybir.ActivationFunctionType
    AX = mybir.AxisListType.X

    P = 128
    B, NTXT, D = txt.shape
    NIMG = patchesT.shape[1] // B
    T = NIMG + NTXT
    PK = patchesT.shape[0] // P
    DK = D // P
    HEADS, HD = 16, 16
    LAT = q2lT.shape[0]
    UH = P // HD
    UNITS = B * HEADS // UH
    HT = T // 2
    SP_ = 640
    NE, _, FF = W1.shape
    FK = FF // P
    NTOK = B * T
    TOPK = 2
    CAP = -(-NTOK * TOPK * 5 // (4 * NE))
    SLOTS = NE * CAP
    SROWS = -(-(SLOTS + 1) // P) * P
    EPS = 1e-5
    SCALE = float(LAT) ** -0.5
    NEG = -1e30
    QT = [(0, NIMG)] + [(NIMG + P * i, P) for i in range(NTXT // P)]
    NQ = len(QT)
    KT = [(P * i, min(P, T - P * i)) for i in range(-(-T // P))]
    NT = B * NQ
    QROWS = [0, 0, 0, 1, 1, 2]
    KROWS = [0, 1, 2, 0, 1, 0]
    CON = HD * len(QROWS)
    CONM = CON + 3

    SPIECE = [[(0, 0, 36, 0), (1, 0, 164, 36), (2, 0, 292, 200)],
              [(3, 0, 420, 0), (4, 512, 36, 420)],
              [(4, 0, 512, 0)]]
    TPIECE = [[(0, 0, 512, 0)],
              [(0, 512, 36, 0), (1, 128, 420, 36)],
              [(2, 256, 292, 0), (3, 384, 164, 292), (4, 512, 36, 456)]]
    TOFF = [0, 512, 968]
    PW = 1460
    DIAG = [(0, P), (512 + 36, P), (968, P), (968 + 292, P), (968 + 456, T - 4 * P)]
    SEG = []
    for pc, off in zip(TPIECE, TOFF):
        for kt, q0, w, c in pc:
            for h0 in (0, HT):
                lo, hi = max(q0, h0), min(q0 + w, h0 + HT)
                if lo < hi:
                    SEG.append((h0 // HT, kt, off + c + lo - q0, lo, hi - lo))
    SEG.sort()
    HTILE = [(i, min(P, HT - i)) for i in range(0, HT, P)]
    NP = 7


    def spread(*lists):
        at = [((i + 0.5) / len(x), n, job) for n, x in enumerate(lists) for i, job in enumerate(x)]
        return [job for _, _, job in sorted(at, key=lambda a: a[:2])]

    def halves(name, u):
        return [(name, u, 0), (name, u, 1)]

    def maxima_of(u, heads):
        return [("S", u, j, p) for j in heads for p in range(len(SPIECE))]

    def unit_stages(u, j):
        if u % 2 == 0:
            b, pb = u // 2 + 1, u // 2 - 1
            front = {0: [("hT", b, 0), ("hT", b, 1)], 1: [("hT", b, 2), ("hT", b, 3)],
                     2: halves("kv", b) + halves("Q", u + 2) + [("Qx", u + 2)],
                     3: halves("K", u + 2) + [("Kx", u + 2), ("Qy", u + 2)],
                     4: [("Ky", u + 2)], 5: [("V", b, 0)], 6: [("V", b, 1)], 7: [("V", b, 2)]}
            back = {6: [("W", pb, i) for i in range(2)], 7: [("W", pb, i) for i in range(2, 4)]}
        else:
            b, pb = (u + 1) // 2 + 1, (u - 3) // 2
            front = {}
            if u + 2 < UNITS:
                front = {2: halves("Q", u + 2) + [("Qx", u + 2)], 3: halves("K", u + 2) + [("Kx", u + 2), ("Qy", u + 2)],
                         4: [("Ky", u + 2)]}
            if b < B:
                front.update({6: [("ln1s", b), ("rs", b)], 7: [("ln1", b)]})
            back = {0: [("W", pb, 4), ("ln2s", pb), ("rs", pb)], 1: [("ln2", pb)],
                    2: [("hl", pb), ("RT", pb, 0)], 3: [("RT", pb, 1), ("RL", pb, 0)],
                    4: [("RT", pb, 2), ("RL", pb, 1)], 5: [("RT", pb, 3), ("RL", pb, 2)],
                    6: [("RT", pb, 4), ("RL", pb, 3)], 7: [("RL", pb, 4)]}
        out = []
        if pb >= 0:
            out += back.get(j, [])
        if b < B or u % 2 == 1:
            out += front.get(j, [])
        return out

    order = [("embed", 0), ("ln1s", 0), ("rs", 0), ("ln1", 0)] + [("hT", 0, f) for f in range(4)]
    order += halves("kv", 0) + halves("Q", 0) + [("Qx", 0)] + halves("K", 0) + [("Kx", 0), ("Qy", 0), ("Ky", 0)]
    order += halves("Q", 1) + [("Qx", 1)] + halves("K", 1) + [("Kx", 1)]
    order += [("V", 0, f) for f in range(3)] + [("embed", 1), ("Qy", 1), ("Ky", 1)]
    order += spread(maxima_of(0, range(UH)), [("ln1s", 1), ("rs", 1), ("embed", 2), ("ln1", 1), ("embed", 3)])
    order += [("mxc", 0), ("M", 0, 0), ("M", 0, 1), ("Mx", 0)]
    S_AT = {0: [0], 1: [1], 2: [2, 3], 3: [4, 5], 4: [6], 5: [7]}
    for u in range(UNITS):
        nxt = u + 1 < UNITS
        for j in range(UH):
            ctx_of = (u - 1, 1) if j < 4 else (u, 0)
            half = (len(SEG) + 1) // 2
            parts = {1: range(half), 2: range(half, len(SEG))}.get(j % 4, [])
            pv = [("PV", *ctx_of, i) for i in parts] if ctx_of[0] >= 0 else []
            if j == 6 and nxt:
                order += [("mxc", u + 1)]
            norm = []
            if j % 4 == 3 and ctx_of[0] >= 0:
                norm = [("N", ctx_of[0] // 2, 2 * (ctx_of[0] % 2) + ctx_of[1])]
            order += spread([("T", u, j, p) for p in range(len(TPIECE))],
                            maxima_of(u + 1, S_AT.get(j, [])) if nxt else [], pv, norm,
                            ([("M", u + 1, 0), ("M", u + 1, 1), ("Mx", u + 1)] if j == 6 and nxt else []) +
                            unit_stages(u, j))
            if j % 4 == 2 and ctx_of[0] >= 0:
                order += [("O", *ctx_of)]
            if j % 4 == 3 and ctx_of[0] >= 0:
                b, g = ctx_of[0] // 2, 2 * (ctx_of[0] % 2) + ctx_of[1]
                order += [("Nx", b, g, 0), ("Nx", b, g, 1)]
    b = B - 1
    order += [("PV", UNITS - 1, 1, i) for i in range(len(SEG))] + [("O", UNITS - 1, 1)]
    order += [("N", b, 3), ("Nx", b, 3, 0), ("Nx", b, 3, 1)] + [("W", b, i) for i in range(NQ)]
    order += [("ln2s", b), ("rs", b), ("ln2", b), ("hl", b), ("RT", b, 0)]
    for i in range(1, NQ):
        order += [("RT", b, i), ("RL", b, i - 1)]
    order += [("RL", b, NQ - 1)]

    fills = {}
    for job in order:
        if job[0] in ("embed", "hT", "kv", "V", "Q", "K", "M", "N", "Nx", "W", "RT", "RL"):
            fills[job] = len(fills)
    ROUNDS = 30
    for key in [("cnt", r) for r in range(ROUNDS)] + [("cgt", 0), ("ceq", 0), ("pos", 0)]:
        fills[key] = len(fills)

    lo_count = {(job[0][0], job[1]): n + 1 for n, job in enumerate(x for x in order if x[0] in ("Qx", "Kx"))}
    ln_order = [job for job in order if job[0] in ("ln1", "ln2")]
    ln_count = {job: n + 1 for n, job in enumerate(ln_order)}

    ctx = ExitStack()
    with ctx:
        def sem(name):
            return ctx.enter_context(nc.semaphore(name))

        def sb(name, shape, dt, where=ctx):
            return where.enter_context(nc.sbuf_tensor(name, shape, dt))

        xs_d = nc.dram_tensor("split_scratch", [2, UNITS, 3, P, T], bf16).ap()
        xe_d = nc.dram_tensor("expert_in", [SROWS, 2 * D], bf16).ap()
        xhl_d = nc.dram_tensor("xhl_scratch", [P, NT, 2 * D], bf16).ap()
        y_d = nc.dram_tensor("expert_out", [SLOTS + 1, D], f32).ap()

        ident = sb("ident", [P, P], f32)
        identb = sb("identb", [P, P], bf16)
        H = sb("H", [P, B, NQ, D], f32)
        LG = sb("LG", [P, NT, NE], f32)
        zero = sb("zero", [P, 2 * D], bf16)
        ones = sb("ones", [P, P], f32)
        onesb = sb("onesb", [P, P], bf16)
        trib = sb("trib", [P, P], bf16)
        valid = sb("valid", [P, NT, NE], f32)
        iota8 = sb("iota8", [P, NT, NE], f32)
        base8 = sb("base8", [P, NT, NE], f32)
        sidx = sb("sidx", [P, TOPK, NT], u32)
        gidx = sb("gidx", [P, TOPK, NT], u32)
        gate = sb("gate", [P, TOPK, NT], f32)

        att = ExitStack()
        wq = sb("wq", [P, DK, D], f32, att)
        wkv = sb("wkv", [P, DK, 2 * LAT], f32, att)
        q2l = sb("q2l", [LAT, HEADS * HD], f32, att)
        vu = sb("vu", [P, HEADS * HD], f32, att)
        wo = sb("wo", [P, 4, D], f32, att)
        wr = sb("wr", [P, DK, NE], f32, att)
        nhalf = sb("nhalf", [P, NQ], f32, att)
        maskn = sb("maskn", [P, T], f32, att)
        st = sb("st", [P, NQ, 6], f32, att)
        mv = sb("mv", [P, NQ, 2], f32, att)
        rs = sb("rs", [P, NQ], f32, att)
        ve = sb("ve", [P, NQ], f32, att)
        xh = sb("xh", [P, NQ, D], f32, att)
        hnT = sb("hnT", [P, DK, T], f32, att)
        lat = sb("lat", [P, T], f32, att)
        V = sb("V", [P, 2, NQ, HEADS, 1 + HD], f32, att)
        XS = sb("XS", [P, 2, 3, T], bf16, att)
        XR = sb("XR", [P, T], f32, att)
        Qs = [sb(f"Qs{i}", [P, UH, T], bf16, att) for i in range(3)]
        Ks = [sb(f"Ks{i}", [P, UH, SP_], bf16, att) for i in range(3)]
        mx = sb("mx", [P, 2, NQ + 1, UH], f32, att)
        NS = sb("NS", [UH, 3, T], bf16, att)
        NR = sb("NR", [UH, T], f32, att)
        Pr = sb("Pr", [P, NP, PW], f32, att)
        Of = sb("Of", [P, 2, 4, T], f32, att)
        RD = sb("RD", [P, 2, len(HTILE), 4], f32, att)
        first = sb("first", [P, 4], f32, att)
        emb = ExitStack()
        PT = sb("PT", [P, PK, B * NIMG], f32, emb)
        TW = sb("TW", [P, PK, D], f32, emb)
        tb = sb("tb", [1, D], f32, emb)
        emb.close()
        XHL = sb("XHL", [P, 2, NQ, 2 * D], bf16, att)
        xnT = sb("xnT", [P, 2, DK * P], f32, att)

        bankS = [ctx.enter_context(nc.psum_tensor(f"bankS{i}", [P, 512], f32)) for i in range(2)]
        bankT = [ctx.enter_context(nc.psum_tensor(f"bankT{i}", [P, 512], f32)) for i in range(2)]
        bankO = ctx.enter_context(nc.psum_tensor("bankO", [P, 2, 512], f32))
        bankM = [ctx.enter_context(nc.psum_tensor(f"bankM{i}", [P, 512], f32)) for i in range(2)]

        ld_tok, ld_att = sem("ld_tok"), sem("ld_att")
        ld_txt = [sem(f"ld_txt{b}") for b in range(B)]
        zeroed = sem("zeroed")
        pool_const, dve_const = sem("pool_const"), sem("dve_const")
        keys_const = sem("keys_const")
        m_full = [sem(f"m_full{i}") for i in range(2)]
        m_used = [sem(f"m_used{i}") for i in range(2)]
        mean_ready, rstd_ready, xhat_ready = sem("mean_ready"), sem("rstd_ready"), sem("xhat_ready")
        hi_ready, lo_ready = sem("hi_ready"), sem("lo_ready")
        split_stored = [sem(f"split_stored{i}") for i in range(2)]
        stack_ready = [sem(f"stack_ready{i}") for i in range(3)]
        s_full = [sem(f"s_full{i}") for i in range(2)]
        s_used = [sem(f"s_used{i}") for i in range(2)]
        t_full = [sem(f"t_full{i}") for i in range(2)]
        t_used = [sem(f"t_used{i}") for i in range(2)]
        max_ready, nmhi_ready, nm_ready = sem("max_ready"), sem("nmhi_ready"), sem("nm_ready")
        maxrow_ready = [sem(f"maxrow_ready{i}") for i in range(2)]
        prob_ready = sem("prob_ready")
        o_full, o_used = sem("o_full"), sem("o_used")
        xhi_ready, xhl_ready = sem("xhi_ready"), sem("xhl_ready")
        xhl_stored, xhl_loaded = sem("xhl_stored"), sem("xhl_loaded")
        rexp_in, rexp = sem("rexp_in"), sem("rexp")
        cnt_in = sem("cnt_in")
        idx_ready = sem("idx_ready")
        scattered = sem("scattered")
        dve_chain, pool_chain = sem("dve_chain"), sem("pool_chain")
        w_loaded, xe_loaded = [sem("w_loaded0"), sem("w_loaded1")], [sem("xe_loaded0"), sem("xe_loaded1")]
        whi_ready, wlo_ready = sem("whi_ready"), sem("wlo_ready")
        tr_full = [sem(f"tr_full{i}") for i in range(2)]
        tr_used = [sem(f"tr_used{i}") for i in range(2)]
        h_full = [sem(f"h_full{i}") for i in range(4)]
        hhi_ready = sem("hhi_ready")
        h_used = [sem(f"h_used{i}") for i in range(4)]
        y_full = [sem(f"y_full{i}") for i in range(2)]
        y_used = [sem(f"y_used{i}") for i in range(2)]
        y_stored = [sem("y_stored0"), sem("y_stored1")]
        gathered = [sem(f"gathered{i}") for i in range(4)]
        combined = sem("combined")
        stored = sem("stored")

        def filled(eng, key):
            n = fills[key]
            eng.wait_ge(m_full[n % 2], n // 2 + 1)

        def used(eng, key):
            n = fills[key]
            eng.wait_ge(m_used[n % 2], n // 2 + 1)

        def open_fill(pe, key):
            n = fills[key]
            if n >= 2:
                pe.wait_ge(m_used[n % 2], n // 2)
            return bankM[n % 2]

        att.close()
        ffn = ExitStack()
        EP = sb("EP", [P, NT, NE], f32, ffn)
        E2 = sb("E2", [P, NT, NE], f32, ffn)
        E3 = sb("E3", [P, NT, NE], f32, ffn)
        OH = sb("OH", [P, TOPK, NT, NE], f32, ffn)
        G = sb("G", [P, NT, NE], f32, ffn)
        KEEP = sb("KEEP", [P, NT, NE], f32, ffn)
        POS = sb("POS", [P, NT, NE], f32, ffn)
        Xb = sb("Xb", [P, NT, NE], bf16, ffn)
        r20 = sb("r20", [P, 4, NT], f32, ffn)
        v8 = sb("v8", [P, NT, 8], f32, ffn)
        i8 = sb("i8", [P, NT, 8], u32, ffn)
        i8f = sb("i8f", [P, NT, 8], f32, ffn)
        thr = sb("thr", [P, NE], f32, ffn)
        cand = sb("cand", [P, NE], f32, ffn)
        c8 = sb("c8", [P, NE], f32, ffn)
        t8 = sb("t8", [P, NE], f32, ffn)
        room = sb("room", [P, NE], f32, ffn)
        route = ExitStack()
        XA = sb("XA", [P, NT, 2 * D], bf16, ffn)
        W1f = sb("W1f", [P, DK, FF], f32, ffn)
        W2f = sb("W2f", [P, FK, D], f32, ffn)
        W1s = sb("W1s", [P, 2, 2, DK, FF], bf16, ffn)
        W2s = sb("W2s", [P, 2, 2, FK, D], bf16, ffn)
        NST = -(-CAP // P)
        XE = sb("XE", [P, 2, NST, 2 * D], bf16, ffn)
        XT = sb("XT", [P, 2, 2 * DK, CAP], bf16, ffn)
        HH = sb("HH", [P, 2, FK, CAP], bf16, ffn)
        HL = sb("HL", [P, 2, FK, CAP], bf16, ffn)
        Y = sb("Y", [P, 2, NST, D], f32, ffn)
        ffn.close()
        comb = ExitStack()
        GY = sb("GY", [P, 4, TOPK, D], f32, comb)
        comb.close()
        ST = [(P * i, min(P, CAP - P * i)) for i in range(NST)]
        CH = [(0, (CAP + 1) // 2), ((CAP + 1) // 2, CAP // 2)]

        block = ctx.enter_context(nc.Block())

        @block.sync
        def _(sp):
            sp.dma_start(PT[:, :, :], patchesT.rearrange("(k p) n -> p k n", p=P)).then_inc(ld_tok, 16)
            sp.dma_start(TW[:, :, :], tokWT.rearrange("(k p) n -> p k n", p=P)).then_inc(ld_tok, 16)
            sp.dma_start(tb[:, :], tokb.unsqueeze(0)).then_inc(ld_tok, 16)
            for b in range(B):
                sp.dma_start(H[:, b, 1:, :], txt[b].rearrange("(i p) d -> p i d", p=P)).then_inc(ld_txt[b], 16)
                if b == 0:
                    sp.dma_start(wkv[:, :, :], WkvT.rearrange("(k p) n -> p k n", p=P)).then_inc(ld_att, 16)
                    sp.dma_start(wq[:, :, :], WqT.rearrange("(k p) n -> p k n", p=P)).then_inc(ld_att, 16)
                    sp.dma_start(q2l[:, :], q2lT).then_inc(ld_att, 16)
                    sp.dma_start(vu[LAT:2 * LAT, :], vup).then_inc(ld_att, 16)
                    sp.dma_start(wr[:, :, :], Wr.rearrange("(k p) n -> p k n", p=P)).then_inc(ld_att, 16)
                    sp.wait_ge(dve_const, 1)
                    wv = WoT.rearrange("(g j d) n -> j d g n", j=4, d=HD)
                    for j in range(4):
                        sp.dma_start(wo[32 * j + 1:32 * j + 1 + HD, :, :], wv[j]).then_inc(ld_att, 16)
            sp.dma_start(xe_d.rearrange("(p r) c -> p r c", p=P),
                         zero[:, :].unsqueeze(1).to_broadcast([P, SROWS // P, 2 * D])).then_inc(zeroed, 16)
            sp.dma_start(y_d[SLOTS:SLOTS + 1, :], zero[0:1, :].bitcast(f32)).then_inc(zeroed, 16)

            def split_out(which, u):
                sp.wait_ge(lo_ready, 2 * u + which + 1)
                sp.dma_start(xs_d[which, u].rearrange("s p t -> p s t"),
                             XS[:, which, :, :]).then_inc(split_stored[which], 16)

            def stack_in(which, u):
                stacks, rows = (Qs, QROWS) if which == 0 else (Ks, KROWS)
                sp.wait_ge(split_stored[which], 16 * (u + 1))
                if u >= 3:
                    n = 3 * UH * (u - 2) - 1
                    sp.wait_ge(t_full[n % 2], n // 2 + 1)
                for g, part in enumerate(rows):
                    sp.dma_start(stacks[u % 3][HD * g:HD * (g + 1), :, 0:T],
                                 xs_d[which, u, part].rearrange("(j d) t -> d j t", d=HD)
                                 ).then_inc(stack_ready[u % 3], 16)

            def max_rows(u):
                sp.wait_ge(nm_ready, u + 1)
                for g in range(3):
                    sp.dma_start(Qs[u % 3][CON + g:CON + g + 1, :, :],
                                 NS[:, g, :]).then_inc(maxrow_ready[u % 2], 16)

            for job in order:
                k, a = job[0], job[1]
                if k == "Qx":
                    split_out(0, a)
                elif k == "Kx":
                    split_out(1, a)
                elif k == "Qy":
                    stack_in(0, a)
                elif k == "Ky":
                    stack_in(1, a)
                elif k == "Mx":
                    max_rows(a)
                elif k == "RL" and job[2] == 0:
                    sp.wait_ge(xhl_ready, a + 1)
                    sp.dma_start(xhl_d[:, NQ * a:NQ * (a + 1), :], XHL[:, a % 2, :, :]).then_inc(xhl_stored, 16)

            sp.wait_ge(xhl_stored, 16 * B)
            used(sp, ("RL", B - 1, NQ - 1))
            sp.dma_start(XA[:, :, :], xhl_d).then_inc(xhl_loaded, 16)

            def load_weights(e):
                if e >= 1:
                    sp.wait_ge(whi_ready, e)
                    sp.wait_ge(wlo_ready, e)
                sp.dma_start(W1f[:, :, :], W1[e].rearrange("(k p) f -> p k f", p=P)).then_inc(w_loaded[e % 2], 16)
                sp.dma_start(W2f[:, :, :], W2[e].rearrange("(k p) d -> p k d", p=P)).then_inc(w_loaded[e % 2], 16)

            load_weights(0)
            sp.wait_ge(scattered, 16 * TOPK * NT)

            def load_slots(e):
                nfull = CAP // P
                if e >= 2:
                    n = NST * (e - 1) - 1
                    sp.wait_ge(tr_full[n % 2], n // 2 + 1)
                sp.dma_start(XE[:, e % 2, 0:nfull, :],
                             xe_d[e * CAP:e * CAP + nfull * P, :].rearrange("(i p) c -> p i c", p=P)
                             ).then_inc(xe_loaded[e % 2], 16)
                sp.dma_start(XE[0:CAP - nfull * P, e % 2, nfull, :],
                             xe_d[e * CAP + nfull * P:(e + 1) * CAP, :]).then_inc(xe_loaded[e % 2], 16)

            load_slots(0)
            load_weights(1)
            for e in range(NE):
                if e + 1 < NE:
                    load_slots(e + 1)
                if e + 2 < NE:
                    load_weights(e + 2)
                for i, (r0, n) in enumerate(ST):
                    q = e * NST + i
                    sp.wait_ge(y_used[q % 2], q // 2 + 1)
                    sp.dma_start(y_d[e * CAP + r0:e * CAP + r0 + n, :],
                                 Y[0:n, e % 2, i, :]).then_inc(y_stored[e % 2], 16)
            for t in range(NT):
                b, i = t // NQ, t % NQ
                sp.wait_ge(combined, t + 1)
                q0, n = QT[i]
                sp.dma_start(out[b, q0:q0 + n, :], H[0:n, b, i, :]).then_inc(stored, 16)
            sp.wait_ge(stored, 16 * NT)

        @block.gpsimd
        def _(pool):
            chain = [0]

            def link(ins):
                chain[0] += 1
                ins.then_inc(pool_chain, 1)
                pool.wait_ge(pool_chain, chain[0])

            link(nc.gpsimd.memset(ident[:, :], 0.0))
            link(nc.gpsimd.affine_select(out=ident[:, :], in_=ident[:, :], compare_op=ALU.not_equal, fill=1.0,
                                         base=0, pattern=[[-1, P]], channel_multiplier=1))
            nc.gpsimd.tensor_copy(identb[:, :], ident[:, :])
            link(nc.gpsimd.memset(maskn[:, :], 0.0))
            tri = maskn[:, T - P:T]
            link(nc.gpsimd.affine_select(out=tri, in_=tri, compare_op=ALU.is_ge, fill=NEG,
                                         base=0, pattern=[[-1, P]], channel_multiplier=1))
            link(nc.gpsimd.memset(first[:, :], 0.0))
            link(nc.gpsimd.affine_select(out=first[:, :], in_=first[:, :], compare_op=ALU.not_equal, fill=1.0,
                                         base=0, pattern=[[-32, 4]], channel_multiplier=1))
            link(nc.gpsimd.memset(trib[:, :], 1.0))
            link(nc.gpsimd.affine_select(out=trib[:, :], in_=trib[:, :], compare_op=ALU.is_gt, fill=0.0,
                                         base=0, pattern=[[1, P]], channel_multiplier=-1))
            link(nc.gpsimd.memset(valid[:, :, :], 1.0))
            for b in range(B):
                v = valid[:, b * NQ, :]
                link(nc.gpsimd.affine_select(out=v, in_=v, compare_op=ALU.is_gt, fill=0.0,
                                             base=NIMG, pattern=[[0, NE]], channel_multiplier=-1))
            nc.gpsimd.iota(iota8[:, :, :], pattern=[[0, NT], [1, NE]], base=0, channel_multiplier=0,
                           allow_small_or_imprecise_dtypes=True)
            nc.gpsimd.iota(base8[:, :, :], pattern=[[0, NT], [CAP, NE]], base=0, channel_multiplier=0,
                           allow_small_or_imprecise_dtypes=True)
            nc.gpsimd.memset(nhalf[:, :], -0.5).then_inc(pool_const, 1)

            norms = [0]

            def rstd():
                norms[0] += 1
                pool.wait_ge(mean_ready, norms[0])
                link(nc.gpsimd.tensor_scalar(ve[:, :], mv[:, :, 1], EPS, None, ALU.add))
                nc.gpsimd.tensor_tensor(rs[:, :], ve[:, :], nhalf[:, :], ALU.pow).then_inc(rstd_ready, 1)

            def key_constants():
                for i in range(3):
                    link(nc.gpsimd.memset(Ks[i][:, :, T:SP_].bitcast(f32), 0.0))
                    nc.gpsimd.memset(Ks[i][CON:P, :, 0:T].bitcast(u32), 0x3F803F80).then_inc(keys_const, 1)
                    pool.wait_ge(keys_const, i + 1)

            def causal(u, j, p):
                hh = UH * u + j
                n = 3 * hh + p
                pool.wait_ge(t_used[n % 2], n // 2 + 1)
                for c, w in ([DIAG[0]], [DIAG[1]], DIAG[2:])[p]:
                    v = Pr[:, hh % NP, c:c + w]
                    last = nc.gpsimd.affine_select(out=v, in_=v, compare_op=ALU.is_ge, fill=0.0,
                                                   base=0, pattern=[[1, w]], channel_multiplier=-1)
                if p == 2:
                    last.then_inc(prob_ready, 1)

            for job in order:
                k, a = job[0], job[1]
                if k == "rs":
                    rstd()
                    if a == 0 and norms[0] == 1:
                        key_constants()
                elif k == "T":
                    causal(*job[1:])
                elif k == "hl":
                    pool.wait_ge(xhi_ready, a + 1)
                    nc.gpsimd.tensor_tensor(XHL[:, a % 2, :, D:2 * D], xh[:, :, :], XHL[:, a % 2, :, 0:D],
                                            ALU.subtract).then_inc(xhl_ready, 1)

            pool.wait_ge(idx_ready, 1)
            pool.wait_ge(zeroed, 32)
            pool.wait_ge(xhl_loaded, 16)
            for t in range(NT):
                n = QT[t % NQ][1]
                for c in range(TOPK):
                    nc.gpsimd.indirect_dma_start(
                        out=xe_d[:, :], out_offset=bass.IndirectOffsetOnAxis(ap=sidx[0:n, c, t:t + 1], axis=0),
                        in_=XA[0:n, t, :], in_offset=None, bounds_check=SLOTS - 1, oob_is_err=False,
                    ).then_inc(scattered, 16)

            for e in range(NE):
                pool.wait_ge(w_loaded[e % 2], 32 * (e // 2 + 1))
                pool.wait_ge(whi_ready, e + 1)
                if e >= 2:
                    q = (e - 1) * NST - 1
                    pool.wait_ge(y_full[q % 2], q // 2 + 1)
                nc.gpsimd.tensor_tensor(W1s[:, e % 2, 1, :, :], W1f[:, :, :], W1s[:, e % 2, 0, :, :], ALU.subtract)
                nc.gpsimd.tensor_tensor(W2s[:, e % 2, 1, :, :], W2f[:, :, :], W2s[:, e % 2, 0, :, :],
                                        ALU.subtract).then_inc(wlo_ready, 1)

            for p in range(2):
                n = sum(1 for e in range(NE) if e % 2 == p)
                pool.wait_ge(y_stored[p], 16 * NST * n)
            for t in range(NT):
                n = QT[t % NQ][1]
                if t >= 4:
                    pool.wait_ge(combined, t - 3)
                for c in range(TOPK):
                    nc.gpsimd.indirect_dma_start(
                        out=GY[0:n, t % 4, c, :], out_offset=None, in_=y_d[:, :],
                        in_offset=bass.IndirectOffsetOnAxis(ap=gidx[0:n, c, t:t + 1], axis=0),
                    ).then_inc(gathered[t % 4], 16)

        @block.tensor
        def _(pe):
            pe.wait_ge(dve_const, 1)

            def project(key, lhsT_of, rhs_of, nk, n=HT):
                bank = open_fill(pe, key)
                for k in range(nk):
                    last = nc.tensor.matmul(bank[:, 0:n], lhsT_of(k), rhs_of(k), start=(k == 0), stop=(k == nk - 1))
                last.then_inc(m_full[fills[key] % 2], 1)

            def embed(b):
                if b == 0:
                    pe.wait_ge(ld_tok, 48)
                bank = open_fill(pe, ("embed", b))
                o = bank[0:NIMG, 0:D]
                for k in range(PK):
                    nc.tensor.matmul(o, PT[:, k, NIMG * b:NIMG * (b + 1)], TW[:, k, :], start=(k == 0), stop=False)
                nc.tensor.matmul(o, ones[0:1, 0:NIMG], tb[0:1, :], start=False, stop=True
                                 ).then_inc(m_full[fills[("embed", b)] % 2], 1)

            def transpose_h(b, f):
                if b == 0 and f == 0:
                    pe.wait_ge(pool_const, 1)
                if f == 0:
                    pe.wait_ge(xhat_ready, ln_count[("ln1", b)])
                k, tiles = f // 2, (QT[0:3] if f % 2 == 0 else QT[3:5])
                bank = open_fill(pe, ("hT", b, f))
                for q0, n in tiles:
                    i = QT.index((q0, n))
                    c = q0 - tiles[0][0]
                    last = nc.tensor.transpose(bank[:, c:c + n], xh[0:n, i, P * k:P * (k + 1)], ident[0:n, 0:n])
                last.then_inc(m_full[fills[("hT", b, f)] % 2], 1)

            def kv(b, hf):
                if b == 0 and hf == 0:
                    pe.wait_ge(ld_att, 16 * 9)
                for f in range(4):
                    used(pe, ("hT", b, f))
                project(("kv", b, hf), lambda k: wkv[:, k, :], lambda k: hnT[:, k, HT * hf:HT * (hf + 1)], DK)

            def values(b, f):
                for hf in range(2):
                    used(pe, ("kv", b, hf))
                bank = open_fill(pe, ("V", b, f))
                for i in range(2 * f, min(2 * f + 2, len(KT))):
                    s0, n = KT[i]
                    last = nc.tensor.matmul(bank[0:n, D * (i % 2):D * (i % 2 + 1)], lat[LAT:2 * LAT, s0:s0 + n],
                                            vu[LAT:2 * LAT, :], start=True, stop=True)
                last.then_inc(m_full[fills[("V", b, f)] % 2], 1)

            def queries(u, hf):
                for f in range(4):
                    used(pe, ("hT", u // 2, f))
                m = P * (u % 2)
                project(("Q", u, hf), lambda k: wq[:, k, m:m + P], lambda k: hnT[:, k, HT * hf:HT * (hf + 1)], DK)

            def keys(u, hf):
                for h in range(2):
                    used(pe, ("kv", u // 2, h))
                m = P * (u % 2)
                project(("K", u, hf), lambda k: q2l[:, m:m + P], lambda k: lat[0:LAT, HT * hf:HT * (hf + 1)], 1)

            def scores(u, j, p):
                if j == 0 and p == 0:
                    pe.wait_ge(stack_ready[u % 3], 16 * 12 * (u // 3 + 1))
                    if u < 3:
                        pe.wait_ge(keys_const, u + 1)
                n = 3 * (UH * u + j) + p
                if n >= 2:
                    pe.wait_ge(s_used[n % 2], n // 2)
                for i, s0, w, c in SPIECE[p]:
                    q0, nq = QT[i]
                    last = nc.tensor.matmul(bankS[n % 2][0:nq, c:c + w], Qs[u % 3][0:CON, j, q0:q0 + nq],
                                            Ks[u % 3][0:CON, j, s0:s0 + w], start=True, stop=True)
                last.then_inc(s_full[n % 2], 1)

            def transpose_max(u, f):
                pe.wait_ge(max_ready, u + 1)
                tiles = QT[0:3] if f == 0 else QT[3:5]
                bank = open_fill(pe, ("M", u, f))
                for q0, n in tiles:
                    i = QT.index((q0, n))
                    c = q0 - tiles[0][0]
                    last = nc.tensor.transpose(bank[0:UH, c:c + n], mx[0:n, u % 2, i, :], ident[0:n, 0:n])
                last.then_inc(m_full[fills[("M", u, f)] % 2], 1)

            def scores_t(u, j, p):
                if j == 0 and p == 0:
                    pe.wait_ge(maxrow_ready[u % 2], 48 * (u // 2 + 1))
                n = 3 * (UH * u + j) + p
                if n >= 2:
                    pe.wait_ge(t_used[n % 2], n // 2)
                for i, q0, w, c in TPIECE[p]:
                    last = nc.tensor.matmul(bankT[n % 2][:, c:c + w], Ks[u % 3][0:CONM, j, P * i:P * (i + 1)],
                                            Qs[u % 3][0:CONM, j, q0:q0 + w], start=True, stop=True)
                last.then_inc(t_full[n % 2], 1)

            def context(u, g, si):
                b, gi = u // 2, 2 * u + g
                if u == 0 and g == 0 and si == 0:
                    pe.wait_ge(dve_const, 2)
                if si == 0:
                    pe.wait_ge(prob_ready, 4 * (gi + 1))
                    used(pe, ("V", b, 2))
                    used(pe, ("V", b, 1))
                    if gi >= 1:
                        pe.wait_ge(o_used, gi)
                firsts = [SEG[0], next(s for s in SEG if s[0] == 1)]
                lasts = [[s for s in SEG if s[0] == h][-1] for h in range(2)]
                s = SEG[si]
                half, kt, c, q0, w = s
                n = KT[kt][1]
                for j in range(4):
                    hh = UH * u + 4 * g + j
                    last = nc.tensor.matmul(
                        bankO[32 * j:32 * j + 1 + HD, half, q0 - HT * half:q0 - HT * half + w],
                        V[0:n, b % 2, kt, (UH * (u % 2) + 4 * g + j), :],
                        Pr[0:n, hh % NP, c:c + w], start=(s in firsts), stop=(s in lasts),
                        tile_position=(0, 32 * j))
                if si == len(SEG) - 1:
                    last.then_inc(o_full, 1)

            def denominators(b, g):
                pe.wait_ge(o_used, 4 * b + g + 1)
                bank = open_fill(pe, ("N", b, g))
                d = bank[:, 0:2 * len(HTILE) * 4].rearrange("p (h i j) -> p h i j", h=2, j=4)
                for hf in range(2):
                    for i, (c0, w) in enumerate(HTILE):
                        c = HT * hf + c0
                        last = nc.tensor.matmul(d[0:w, hf, i, :], Of[:, b % 2, g, c:c + w], first[:, :],
                                                start=True, stop=True)
                last.then_inc(m_full[fills[("N", b, g)] % 2], 1)

            def reciprocals(b, g, hf):
                used(pe, ("N", b, g))
                bank = open_fill(pe, ("Nx", b, g, hf))
                for i, (c0, w) in enumerate(HTILE):
                    for j in range(4):
                        last = nc.tensor.matmul(bank[32 * j:32 * (j + 1), c0:c0 + w],
                                                RD[0:w, hf, i, j:j + 1].to_broadcast([w, 32]),
                                                ident[0:w, 0:w], start=True, stop=True, tile_position=(0, 32 * j))
                last.then_inc(m_full[fills[("Nx", b, g, hf)] % 2], 1)

            def attend_out(b, i):
                for hf in range(2):
                    used(pe, ("Nx", b, 3, hf))
                q0, n = QT[i]
                bank = open_fill(pe, ("W", b, i))
                for g in range(4):
                    last = nc.tensor.matmul(bank[0:n, 0:D], Of[:, b % 2, g, q0:q0 + n], wo[:, g, :],
                                            start=(g == 0), stop=(g == 3))
                last.then_inc(m_full[fills[("W", b, i)] % 2], 1)

            def router_t(b, i):
                pe.wait_ge(xhat_ready, ln_count[("ln2", b)])
                n = QT[i][1]
                bank = open_fill(pe, ("RT", b, i))
                for k in range(DK):
                    last = nc.tensor.transpose(bank[:, k * n:(k + 1) * n], xh[0:n, i, P * k:P * (k + 1)],
                                               ident[0:n, 0:n])
                last.then_inc(m_full[fills[("RT", b, i)] % 2], 1)

            def router(b, i):
                n = QT[i][1]
                used(pe, ("RT", b, i))
                bank = open_fill(pe, ("RL", b, i))
                for k in range(DK):
                    last = nc.tensor.matmul(bank[0:n, 0:NE], xnT[:, i % 2, k * n:(k + 1) * n],
                                            wr[:, k, :], start=(k == 0), stop=(k == DK - 1))
                last.then_inc(m_full[fills[("RL", b, i)] % 2], 1)

            stages = {"embed": embed, "hT": transpose_h, "kv": kv, "V": values, "Q": queries, "K": keys, "S": scores,
                      "M": transpose_max, "T": scores_t, "PV": context, "N": denominators, "Nx": reciprocals, "W": attend_out, "RT": router_t, "RL": router}
            for job in order:
                if job[0] in stages:
                    stages[job[0]](*job[1:])

            n_in = 0
            for r in range(ROUNDS):
                n_in += 1
                pe.wait_ge(cnt_in, n_in)
                bank = open_fill(pe, ("cnt", r))
                nc.tensor.matmul(bank[:, 0:NE], ones[:, :], c8[:, :], start=True, stop=True
                                 ).then_inc(m_full[fills[("cnt", r)] % 2], 1)
            n_in += 1
            pe.wait_ge(cnt_in, n_in)
            bank = open_fill(pe, ("cgt", 0))
            nc.tensor.matmul(bank[:, 0:NE], ones[:, :], c8[:, :], start=True, stop=True
                             ).then_inc(m_full[fills[("cgt", 0)] % 2], 1)
            for key in (("ceq", 0), ("pos", 0)):
                n_in += 1
                pe.wait_ge(cnt_in, n_in)
                bank = open_fill(pe, key)
                o = bank[:, 0:NT * NE].rearrange("p (t e) -> p t e", e=NE)
                nc.tensor.matmul(o, trib[:, :], Xb[:, :, :], start=True, stop=False)
                for t in range(NT - 1):
                    last = nc.tensor.matmul(o[:, t + 1:, :], onesb[:, :],
                                            Xb[:, t:t + 1, :].to_broadcast([P, NT - 1 - t, NE]),
                                            start=False, stop=(t == NT - 2))
                last.then_inc(m_full[fills[key] % 2], 1)

            trb = [bankT[i][:, 0:256].bitcast(bf16).rearrange("p (c s) -> p c s", c=4) for i in range(2)]
            hb = [bankS[0], bankS[1], bankO[:, 0, :], bankO[:, 1, :]]

            def slots_t(e, tiles):
                for i in tiles:
                    if i == 0:
                        pe.wait_ge(xe_loaded[e % 2], 32 * (e // 2 + 1))
                    n = ST[i][1]
                    q = e * NST + i
                    if q >= 2:
                        pe.wait_ge(tr_used[q % 2], q // 2)
                    for c in range(4):
                        last = nc.tensor.transpose(trb[q % 2][:, c, 0:n], XE[0:n, e % 2, i, P * c:P * (c + 1)],
                                                   identb[0:n, 0:n])
                    last.then_inc(tr_full[q % 2], 1)

            def up(e):
                pe.wait_ge(wlo_ready, e + 1)
                pe.wait_ge(whi_ready, e + 1)
                for i in (NST - 2, NST - 1):
                    q = e * NST + i
                    pe.wait_ge(tr_used[q % 2], q // 2 + 1)
                for ft in range(FK):
                    banks = []
                    for hf in range(2):
                        q = 2 * (e * FK + ft) + hf
                        if q >= 4:
                            pe.wait_ge(h_used[q % 4], q // 4)
                        banks.append(hb[q % 4])
                    terms = [(k, a, c) for k in range(DK) for a, c in ((0, 0), (0, 1), (1, 0))]
                    for ti, (k, a, c) in enumerate(terms):
                        for hf, (c0, w) in enumerate(CH):
                            last = nc.tensor.matmul(banks[hf][:, 0:w], W1s[:, e % 2, a, k, P * ft:P * (ft + 1)],
                                                    XT[:, e % 2, 2 * c + k, c0:c0 + w],
                                                    start=(ti == 0), stop=(ti == len(terms) - 1))
                            if ti == len(terms) - 1:
                                last.then_inc(h_full[(2 * (e * FK + ft) + hf) % 4], 1)

            def down(e):
                if e + 1 < NE:
                    slots_t(e + 1, (0, 1))
                for q in range(2 * (e + 1) * FK - 4, 2 * (e + 1) * FK - 2):
                    pe.wait_ge(h_used[q % 4], q // 4 + 1)
                for i, (r0, n) in enumerate(ST):
                    q = e * NST + i
                    if q >= 2:
                        pe.wait_ge(y_used[q % 2], q // 2)
                    for ft in range(FK):
                        if i == 0 and ft == FK - 1:
                            for h in range(2 * (e + 1) * FK - 2, 2 * (e + 1) * FK):
                                pe.wait_ge(h_used[h % 4], h // 4 + 1)
                        for ti, (a, c) in enumerate(((0, 0), (0, 1), (1, 0))):
                            hid = (HH, HL)[a]
                            last = nc.tensor.matmul(bankM[q % 2][0:n, 0:D], hid[:, e % 2, ft, r0:r0 + n],
                                                    W2s[:, e % 2, c, ft, :], start=(ft == 0 and ti == 0),
                                                    stop=(ft == FK - 1 and ti == 2))
                    last.then_inc(y_full[q % 2], 1)
                    if e + 1 < NE and i + 2 < NST:
                        slots_t(e + 1, (i + 2,))

            slots_t(0, range(NST))
            for e in range(NE):
                up(e)
                down(e)

        @block.scalar
        def _(act):
            def drain(key, dst, src):
                filled(act, key)
                nc.scalar.activation(dst, src, ACT.Copy).then_inc(m_used[fills[key] % 2], 1)

            def high(name, which, u, hf):
                if u >= 1:
                    act.wait_ge(split_stored[which], 16 * u)
                key = (name, u, hf)
                filled(act, key)
                nc.scalar.activation(XS[:, which, 0, HT * hf:HT * (hf + 1)], bankM[fills[key] % 2][:, 0:HT],
                                     ACT.Copy).then_inc(hi_ready, 1)

            for job in order:
                k, a = job[0], job[1]
                if k == "hT":
                    f = job[2]
                    c0, w = (0, QT[3][0]) if f % 2 == 0 else (QT[3][0], 2 * P)
                    drain(job, hnT[:, f // 2, c0:c0 + w], bankM[fills[job] % 2][:, 0:w])
                elif k == "kv":
                    hf = job[2]
                    drain(job, lat[:, HT * hf:HT * (hf + 1)], bankM[fills[job] % 2][:, 0:HT])
                elif k == "V":
                    f = job[2]
                    if a == 0:
                        act.wait_ge(dve_const, 2)
                    filled(act, job)
                    for i in range(2 * f, min(2 * f + 2, len(KT))):
                        n = KT[i][1]
                        src = bankM[fills[job] % 2][0:n, D * (i % 2):D * (i % 2 + 1)]
                        last = nc.scalar.activation(V[0:n, a % 2, i, :, 1:1 + HD],
                                                    src.rearrange("p (h d) -> p h d", d=HD), ACT.Copy)
                    last.then_inc(m_used[fills[job] % 2], 1)
                elif k == "Q":
                    high("Q", 0, a, job[2])
                elif k == "K":
                    high("K", 1, a, job[2])
                elif k == "M":
                    f = job[2]
                    if a >= 1:
                        act.wait_ge(maxrow_ready[(a - 1) % 2], 48 * ((a - 1) // 2 + 1))
                    c0, w = (0, QT[3][0]) if f == 0 else (QT[3][0], 2 * P)
                    filled(act, job)
                    nc.scalar.activation(NS[:, 0, c0:c0 + w], bankM[fills[job] % 2][0:UH, 0:w], ACT.Copy,
                                         scale=-1.0).then_inc(nmhi_ready, 1)
                elif k == "T":
                    hh, p = UH * a + job[2], job[3]
                    if hh >= NP and p == 0:
                        act.wait_ge(o_full, (hh - NP) // 4 + 1)
                    n = 3 * hh + p
                    w = sum(x[2] for x in TPIECE[p])
                    act.wait_ge(t_full[n % 2], n // 2 + 1)
                    nc.scalar.activation(Pr[:, hh % NP, TOFF[p]:TOFF[p] + w], bankT[n % 2][:, 0:w], ACT.Exp,
                                         scale=SCALE).then_inc(t_used[n % 2], 1)
                elif k == "O":
                    gi = 2 * a + job[2]
                    gg = gi % 4
                    act.wait_ge(o_full, gi + 1)
                    b = gi // 4
                    if b >= 2:
                        used(act, ("W", b - 2, NQ - 1))
                    nc.scalar.activation(Of[:, b % 2, gg, :].rearrange("p (h t) -> p h t", h=2), bankO[:, :, 0:HT],
                                         ACT.Copy).then_inc(o_used, 1)
                elif k == "RT":
                    i = job[2]
                    n = QT[i][1]
                    if i >= 2:
                        filled(act, ("RL", a, i - 2))
                    elif a >= 1:
                        filled(act, ("RL", a - 1, NQ - 1))
                        filled(act, ("RL", a - 1, NQ - 2))
                    drain(job, xnT[:, i % 2, 0:DK * n], bankM[fills[job] % 2][:, 0:DK * n])
            act.wait_ge(rexp_in, 1)
            nc.scalar.activation(E2[:, :, :], EP[:, :, :], ACT.Exp).then_inc(rexp, 1)

            hb = [bankS[0], bankS[1], bankO[:, 0, :], bankO[:, 1, :]]
            for e in range(NE):
                for ft in range(FK):
                    for hf, (c0, w) in enumerate(CH):
                        q = 2 * (e * FK + ft) + hf
                        act.wait_ge(h_full[q % 4], q // 4 + 1)
                        nc.scalar.activation(HH[:, e % 2, ft, c0:c0 + w], hb[q % 4][:, 0:w],
                                             ACT.Relu).then_inc(hhi_ready, 1)
                for i, (r0, n) in enumerate(ST):
                    q = e * NST + i
                    act.wait_ge(y_full[q % 2], q // 2 + 1)
                    if e >= 2 and i == 0:
                        act.wait_ge(y_stored[e % 2], 16 * NST * (e // 2))
                    nc.scalar.activation(Y[0:n, e % 2, i, :], bankM[q % 2][0:n, 0:D],
                                         ACT.Copy).then_inc(y_used[q % 2], 1)

        @block.vector
        def _(dve):
            chain = [0]

            def link(ins):
                chain[0] += 1
                ins.then_inc(dve_chain, 1)
                dve.wait_ge(dve_chain, chain[0])

            nc.vector.memset(ones[:, :], 1.0)
            nc.vector.memset(wo[:, :, :], 0.0)
            nc.vector.memset(zero[:, :], 0.0).then_inc(dve_const, 1)
            nc.vector.memset(onesb[:, :], 1.0)
            for b in range(B):
                nc.vector.memset(H[:, b, 0, :], 0.0)
            nc.vector.memset(V[:, :, :, :, 0:1], 1.0)
            nc.vector.memset(mx[:, :, :, :], 0.0)
            nc.vector.memset(bankO[:, :, :], 0.0)
            nc.vector.memset(LG[:, :, :], 0.0).then_inc(dve_const, 1)

            norms = [0]

            def statistics(b):
                for i in range(NQ):
                    last = nc.vector.bn_stats(st[:, i, :], H[:, b, i, :])
                link(last)
                for i in range(NQ):
                    last = nc.vector.bn_aggr(mv[:, i, :], st[:, i, :])
                last.then_inc(mean_ready, 1)

            def normalise(b):
                norms[0] += 1
                dve.wait_ge(mean_ready, norms[0])
                dve.wait_ge(rstd_ready, norms[0])
                for i in range(NQ):
                    last = nc.vector.tensor_scalar(xh[:, i, :], H[:, b, i, :], mv[:, i, 0:1], rs[:, i:i + 1],
                                                   ALU.subtract, ALU.mult)
                last.then_inc(xhat_ready, 1)

            def xh_free():
                prev = ln_order[norms[0] - 1]
                if prev[0] == "ln1":
                    filled(dve, ("hT", prev[1], 3))
                    filled(dve, ("hT", prev[1], 2))
                else:
                    filled(dve, ("RT", prev[1], NQ - 1))
                    dve.wait_ge(xhl_ready, prev[1] + 1)

            def rest(name, which, u, hf):
                if hf == 0 and u + which > 0:
                    dve.wait_ge(lo_ready, lo_count[(name, u)] - 1)
                key = (name, u, hf)
                filled(dve, key)
                dve.wait_ge(hi_ready, 4 * u + 2 * which + hf + 1)
                c = slice(HT * hf, HT * (hf + 1))
                nc.vector.tensor_tensor(XR[:, c], bankM[fills[key] % 2][:, 0:HT],
                                        XS[:, which, 0, c], ALU.subtract).then_inc(m_used[fills[key] % 2], 1)

            def middle(name, which, u):
                for hf in range(2):
                    used(dve, (name, u, hf))
                if u >= 1:
                    dve.wait_ge(split_stored[which], 16 * u)
                link(nc.vector.tensor_copy(XS[:, which, 1, :], XR[:, :]))
                nc.vector.tensor_tensor(XS[:, which, 2, :], XR[:, :], XS[:, which, 1, :],
                                        ALU.subtract).then_inc(lo_ready, 1)

            def maxima(u, j, p):
                n = 3 * (UH * u + j) + p
                dve.wait_ge(s_full[n % 2], n // 2 + 1)
                for i, s0, w, c in SPIECE[p]:
                    nq = QT[i][1]
                    m0 = T - P if i == 0 else (s0 if i == NQ - 1 else T - w)
                    slot = NQ if (i == NQ - 1 and s0 > 0) else i
                    last = nc.vector.tensor_tensor_reduce(
                        out=bankS[n % 2][0:nq, c:c + w], in0=bankS[n % 2][0:nq, c:c + w], in1=maskn[0:nq, m0:m0 + w],
                        scale=1.0, scalar=-3.0e38, op0=ALU.add, op1=ALU.max,
                        accum_out=mx[0:nq, u % 2, slot, j:j + 1])
                last.then_inc(s_used[n % 2], 1)

            def combine_max(u):
                for p in range(3):
                    n = 3 * (UH * u + UH - 1) + p
                    dve.wait_ge(s_used[n % 2], n // 2 + 1)
                nc.vector.tensor_tensor(mx[:, u % 2, NQ - 1, :], mx[:, u % 2, NQ - 1, :], mx[:, u % 2, NQ, :],
                                        ALU.max).then_inc(max_ready, 1)

            def negative_rest(u, f):
                c0, w = (0, QT[3][0]) if f == 0 else (QT[3][0], 2 * P)
                key = ("M", u, f)
                filled(dve, key)
                dve.wait_ge(nmhi_ready, 2 * u + f + 1)
                nc.vector.scalar_tensor_tensor(out=NR[:, c0:c0 + w], in0=bankM[fills[key] % 2][0:UH, 0:w],
                                               scalar=-1.0, in1=NS[:, 0, c0:c0 + w], op0=ALU.mult,
                                               op1=ALU.subtract).then_inc(m_used[fills[key] % 2], 1)

            def negative_split(u):
                for f in range(2):
                    used(dve, ("M", u, f))
                if u >= 1:
                    dve.wait_ge(maxrow_ready[(u - 1) % 2], 48 * ((u - 1) // 2 + 1))
                link(nc.vector.tensor_copy(NS[:, 1, :], NR[:, :]))
                nc.vector.tensor_tensor(NS[:, 2, :], NR[:, :], NS[:, 1, :], ALU.subtract).then_inc(nm_ready, 1)

            def last_group(b, g):
                return divmod(4 * b + g - 1, 4)

            for job in order:
                k, a = job[0], job[1]
                if k == "embed":
                    filled(dve, job)
                    if a == 0:
                        dve.wait_ge(dve_const, 2)
                    nc.vector.tensor_copy(H[0:NIMG, a, 0, :], bankM[fills[job] % 2][0:NIMG, 0:D]
                                          ).then_inc(m_used[fills[job] % 2], 1)
                elif k == "ln1s":
                    dve.wait_ge(ld_txt[a], 16)
                    used(dve, ("embed", a))
                    if norms[0]:
                        dve.wait_ge(xhat_ready, norms[0])
                    statistics(a)
                elif k == "ln2s":
                    used(dve, ("W", a, NQ - 2))
                    used(dve, ("W", a, NQ - 1))
                    dve.wait_ge(xhat_ready, norms[0])
                    statistics(a)
                elif k in ("ln1", "ln2"):
                    if norms[0]:
                        xh_free()
                    normalise(a)
                elif k == "Q":
                    rest("Q", 0, a, job[2])
                elif k == "K":
                    rest("K", 1, a, job[2])
                elif k == "Qx":
                    middle("Q", 0, a)
                elif k == "Kx":
                    middle("K", 1, a)
                elif k == "S":
                    if job[1:] == (0, 0, 0):
                        dve.wait_ge(pool_const, 1)
                    maxima(*job[1:])
                elif k == "mxc":
                    combine_max(a)
                elif k == "M":
                    negative_rest(a, job[2])
                elif k == "Mx":
                    negative_split(a)
                elif k == "N":
                    filled(dve, job)
                    if 4 * a + job[2] >= 1:
                        for hf in range(2):
                            used(dve, ("Nx", *last_group(a, job[2]), hf))
                    d = bankM[fills[job] % 2][:, 0:2 * len(HTILE) * 4].rearrange("p (h i j) -> p h i j", h=2, j=4)
                    full, w = len(HTILE) - 1, HTILE[-1][1]
                    nc.vector.reciprocal(RD[:, :, 0:full, :], d[:, :, 0:full, :])
                    nc.vector.reciprocal(RD[0:w, :, full, :], d[0:w, :, full, :]).then_inc(m_used[fills[job] % 2], 1)
                elif k == "Nx":
                    filled(dve, job)
                    v = Of[:, a % 2, job[2], HT * job[3]:HT * (job[3] + 1)]
                    nc.vector.tensor_tensor(v, v, bankM[fills[job] % 2][:, 0:HT], ALU.mult
                                            ).then_inc(m_used[fills[job] % 2], 1)
                elif k == "W":
                    n = QT[job[2]][1]
                    filled(dve, job)
                    nc.vector.tensor_tensor(H[0:n, a, job[2], :], bankM[fills[job] % 2][0:n, 0:D],
                                            H[0:n, a, job[2], :], ALU.add).then_inc(m_used[fills[job] % 2], 1)
                elif k == "hl":
                    dve.wait_ge(xhat_ready, ln_count[("ln2", a)])
                    if a >= 2:
                        dve.wait_ge(xhl_stored, 16 * (a - 1))
                    nc.vector.tensor_copy(XHL[:, a % 2, :, 0:D], xh[:, :, :]).then_inc(xhi_ready, 1)
                elif k == "RL":
                    n = QT[job[2]][1]
                    filled(dve, job)
                    nc.vector.tensor_copy(LG[0:n, a * NQ + job[2], :], bankM[fills[job] % 2][0:n, 0:NE]
                                          ).then_inc(m_used[fills[job] % 2], 1)

            used(dve, ("RL", B - 1, NQ - 2))
            used(dve, ("RL", B - 1, NQ - 1))
            dve.wait_ge(xhl_stored, 16 * B)
            dve.wait_ge(pool_const, 1)
            bc = [P, NT, NE]

            def wide(x):
                return x.unsqueeze(2).to_broadcast(bc)

            def over_tiles(x):
                return x.unsqueeze(1).to_broadcast(bc)

            link(nc.vector.reduce_max(r20[:, 0, :], LG[:, :, :], AX))
            nc.vector.tensor_tensor(EP[:, :, :], LG[:, :, :], wide(r20[:, 0, :]), ALU.subtract).then_inc(rexp_in, 1)
            dve.wait_ge(rexp, 1)
            link(nc.vector.reduce_sum(r20[:, 1, :], E2[:, :, :], AX))
            link(nc.vector.reciprocal(r20[:, 2, :], r20[:, 1, :]))
            link(nc.vector.tensor_tensor(EP[:, :, :], E2[:, :, :], wide(r20[:, 2, :]), ALU.mult))
            for t in range(NT):
                last = nc.vector.max(v8[:, t, :], EP[:, t, :])
            link(last)
            for t in range(NT):
                last = nc.vector.max_index(i8[:, t, :], v8[:, t, :], EP[:, t, :])
            link(last)
            link(nc.vector.tensor_copy(i8f[:, :, :], i8[:, :, :]))
            for c in range(TOPK):
                link(nc.vector.tensor_tensor(E2[:, :, :], iota8[:, :, :], wide(i8f[:, :, c]), ALU.is_equal))
                link(nc.vector.tensor_tensor(OH[:, c, :, :], E2[:, :, :], valid[:, :, :], ALU.mult))
            link(nc.vector.tensor_tensor(E3[:, :, :], OH[:, 0, :, :], OH[:, 1, :, :], ALU.add))
            link(nc.vector.tensor_tensor(G[:, :, :], EP[:, :, :], E3[:, :, :], ALU.mult))
            link(nc.vector.tensor_scalar(E2[:, :, :], E3[:, :, :], 1.0, None, ALU.subtract))
            link(nc.vector.tensor_tensor(G[:, :, :], G[:, :, :], E2[:, :, :], ALU.add))

            n_in = 0
            link(nc.vector.memset(thr[:, :], 0.0))

            def count(src):
                nonlocal_n = src.rearrange("p t e -> p e t")
                nc.vector.reduce_sum(c8[:, :], nonlocal_n, AX).then_inc(cnt_in, 1)

            for r in range(ROUNDS):
                bit = 1 << (ROUNDS - 1 - r)
                link(nc.vector.tensor_scalar(cand[:, :].bitcast(u32), thr[:, :].bitcast(u32), bit, None,
                                             ALU.bitwise_or))
                link(nc.vector.tensor_tensor(E2[:, :, :], G[:, :, :], over_tiles(cand[:, :]), ALU.is_ge))
                count(E2[:, :, :])
                key = ("cnt", r)
                filled(dve, key)
                nc.vector.scalar_tensor_tensor(out=t8[:, :], in0=bankM[fills[key] % 2][:, 0:NE], scalar=float(CAP),
                                               in1=cand[:, :], op0=ALU.is_ge, op1=ALU.mult
                                               ).then_inc(m_used[fills[key] % 2], 1)
                used(dve, key)
                link(nc.vector.tensor_tensor(thr[:, :], thr[:, :], t8[:, :], ALU.max))
            link(nc.vector.tensor_tensor(KEEP[:, :, :], G[:, :, :], over_tiles(thr[:, :]), ALU.is_gt))
            count(KEEP[:, :, :])
            key = ("cgt", 0)
            filled(dve, key)
            nc.vector.tensor_scalar(room[:, :], bankM[fills[key] % 2][:, 0:NE], -1.0, float(CAP), ALU.mult, ALU.add
                                    ).then_inc(m_used[fills[key] % 2], 1)
            link(nc.vector.tensor_tensor(E2[:, :, :], G[:, :, :], over_tiles(thr[:, :]), ALU.is_equal))
            nc.vector.tensor_copy(Xb[:, :, :], E2[:, :, :]).then_inc(cnt_in, 1)
            key = ("ceq", 0)
            filled(dve, key)
            used(dve, ("cgt", 0))
            nc.vector.tensor_tensor(E3[:, :, :], bankM[fills[key] % 2][:, 0:NT * NE].rearrange("p (t e) -> p t e", e=NE),
                                    over_tiles(room[:, :]), ALU.is_lt).then_inc(m_used[fills[key] % 2], 1)
            used(dve, key)
            link(nc.vector.tensor_tensor(E3[:, :, :], E3[:, :, :], E2[:, :, :], ALU.mult))
            link(nc.vector.tensor_tensor(KEEP[:, :, :], KEEP[:, :, :], E3[:, :, :], ALU.add))
            nc.vector.tensor_copy(Xb[:, :, :], KEEP[:, :, :]).then_inc(cnt_in, 1)
            key = ("pos", 0)
            filled(dve, key)
            nc.vector.tensor_tensor(POS[:, :, :], bankM[fills[key] % 2][:, 0:NT * NE].rearrange("p (t e) -> p t e", e=NE),
                                    base8[:, :, :], ALU.add).then_inc(m_used[fills[key] % 2], 1)
            used(dve, key)
            for c in range(TOPK):
                link(nc.vector.tensor_tensor(E2[:, :, :], OH[:, c, :, :], KEEP[:, :, :], ALU.mult))
                link(nc.vector.reduce_sum(r20[:, 0, :], E2[:, :, :], AX))
                link(nc.vector.tensor_tensor(E3[:, :, :], E2[:, :, :], POS[:, :, :], ALU.mult))
                link(nc.vector.reduce_sum(r20[:, 1, :], E3[:, :, :], AX))
                link(nc.vector.tensor_tensor(gate[:, c, :], r20[:, 0, :], v8[:, :, c], ALU.mult))
                link(nc.vector.tensor_scalar(r20[:, 2, :], r20[:, 0, :], -65536.0, 65536.0, ALU.mult, ALU.add))
                link(nc.vector.tensor_tensor(r20[:, 3, :], r20[:, 2, :], r20[:, 1, :], ALU.add))
                link(nc.vector.tensor_copy(sidx[:, c, :], r20[:, 3, :]))
                last = nc.vector.tensor_scalar(gidx[:, c, :], r20[:, 3, :], float(SLOTS), None, ALU.min)
                if c < TOPK - 1:
                    link(last)
            last.then_inc(idx_ready, 1)

            trb = [bankT[i][:, 0:256].bitcast(bf16).rearrange("p (c s) -> p c s", c=4) for i in range(2)]
            hb = [bankS[0], bankS[1], bankO[:, 0, :], bankO[:, 1, :]]

            def weights_high(e, k):
                if k == 0:
                    dve.wait_ge(w_loaded[e % 2], 32 * (e // 2 + 1))
                    if e >= 2:
                        q = (e - 1) * NST - 1
                        dve.wait_ge(y_full[q % 2], q // 2 + 1)
                if k < 2:
                    nc.vector.tensor_copy(W1s[:, e % 2, 0, k, :], W1f[:, k, :])
                else:
                    f = slice(FK // 2 * (k - 2), FK // 2 * (k - 1))
                    last = nc.vector.tensor_copy(W2s[:, e % 2, 0, f, :], W2f[:, f, :])
                    if k == 3:
                        last.then_inc(whi_ready, 1)

            def slots_in(e):
                if e >= 2:
                    q = 2 * (e - 1) * FK - 1
                    dve.wait_ge(h_full[q % 4], q // 4 + 1)
                for i, (r0, n) in enumerate(ST):
                    q = e * NST + i
                    dve.wait_ge(tr_full[q % 2], q // 2 + 1)
                    nc.vector.tensor_copy(XT[:, e % 2, :, r0:r0 + n], trb[q % 2][:, :, 0:n]).then_inc(tr_used[q % 2], 1)

            for k in range(4):
                weights_high(0, k)
            slots_in(0)
            for e in range(NE):
                if e >= 2:
                    q = (e - 1) * NST - 1
                    dve.wait_ge(y_full[q % 2], q // 2 + 1)
                for ft in range(FK):
                    for hf, (c0, w) in enumerate(CH):
                        q = 2 * (e * FK + ft) + hf
                        dve.wait_ge(hhi_ready, q + 1)
                        nc.vector.scalar_tensor_tensor(out=HL[:, e % 2, ft, c0:c0 + w], in0=hb[q % 4][:, 0:w], scalar=0.0,
                                                       in1=HH[:, e % 2, ft, c0:c0 + w], op0=ALU.max,
                                                       op1=ALU.subtract).then_inc(h_used[q % 4], 1)
                    if 1 <= ft <= 4 and e + 1 < NE:
                        weights_high(e + 1, ft - 1)
                if e + 1 < NE:
                    slots_in(e + 1)

            for t in range(NT):
                b, i = t // NQ, t % NQ
                n = QT[i][1]
                dve.wait_ge(gathered[t % 4], 32 * (t // 4 + 1))
                link(nc.vector.scalar_tensor_tensor(out=H[0:n, b, i, :], in0=GY[0:n, t % 4, 0, :],
                                                    scalar=gate[0:n, 0, t:t + 1], in1=H[0:n, b, i, :],
                                                    op0=ALU.mult, op1=ALU.add))
                nc.vector.scalar_tensor_tensor(out=H[0:n, b, i, :], in0=GY[0:n, t % 4, 1, :],
                                               scalar=gate[0:n, 1, t:t + 1], in1=H[0:n, b, i, :],
                                               op0=ALU.mult, op1=ALU.add).then_inc(combined, 1)


def kernel(**inputs):
    import numpy as np
    import concourse.bacc as bacc
    from concourse import mybir as mb
    from concourse.bass_utils import run_bass_kernel_spmd as run

    def c(a):
        return np.ascontiguousarray(a)

    x = np.asarray(inputs["x"])
    nb, ch, hh, ww = x.shape
    p = 16
    pt = x.reshape(nb, ch, hh // p, p, ww // p, p).transpose(0, 2, 3, 1, 4, 5).reshape(-1, ch * p * p).T
    q2l = np.asarray(inputs["L0_attn_q_to_latent"])
    vu = np.asarray(inputs["L0_attn_v_up"])
    arrays = {
        "patchesT": c(pt), "txt": c(inputs["txt"]), "tokWT": c(np.asarray(inputs["L0_tok_W"]).T),
        "tokb": c(inputs["L0_tok_b"]), "WqT": c(np.asarray(inputs["L0_attn_Wq"]).T),
        "WkvT": c(np.concatenate([np.asarray(inputs["L0_attn_Wk_down"]), np.asarray(inputs["L0_attn_Wv_down"])], 0).T),
        "q2lT": c(q2l.transpose(2, 0, 1).reshape(q2l.shape[2], -1)),
        "vup": c(vu.transpose(1, 0, 2).reshape(vu.shape[1], -1)),
        "WoT": c(np.asarray(inputs["L0_attn_Wout"]).T), "Wr": c(inputs["L0_ffn_Wr"]),
        "W1": c(inputs["L0_ffn_W1"]), "W2": c(inputs["L0_ffn_W2"]),
    }
    nc = bacc.Bacc("TRN2", target_bir_lowering=False, num_devices=1)
    args = [nc.dram_tensor(k, a.shape, mb.dt.from_np(a.dtype), kind="ExternalInput").ap() for k, a in arrays.items()]
    nb, nt, d = arrays["txt"].shape
    t = nt + arrays["patchesT"].shape[1] // nb
    o = nc.dram_tensor("out", (nb, t, d), mb.dt.float32, kind="ExternalOutput").ap()
    early_fusion_kernel(nc, *args, o)
    r = run(nc, [arrays], core_ids=[0])
    return r.results[0]["out"]
```

```python
import concourse.bass as bass
from concourse import mybir
from contextlib import ExitStack


def early_fusion_kernel(nc, patchesT, txt, tokWT, tokb, WqT, WkvT, q2lT, vup, WoT, Wr, W1, W2, out):
    f32, bf16, u32 = mybir.dt.float32, mybir.dt.bfloat16, mybir.dt.uint32
    ALU = mybir.AluOpType
    ACT = mybir.ActivationFunctionType
    AX = mybir.AxisListType.X

    P = 128
    B, NTXT, D = txt.shape
    NIMG = patchesT.shape[1] // B
    T = NIMG + NTXT
    PK = patchesT.shape[0] // P
    DK = D // P
    HEADS, HD = 16, 16
    LAT = q2lT.shape[0]
    UH = P // HD
    UNITS = B * HEADS // UH
    HT = T // 2
    SP_ = 640
    NE, _, FF = W1.shape
    FK = FF // P
    NTOK = B * T
    TOPK = 2
    CAP = -(-NTOK * TOPK * 5 // (4 * NE))
    SLOTS = NE * CAP
    SROWS = -(-(SLOTS + 1) // P) * P
    NT = B * (1 + NTXT // P)
    ROWC = 2 * D + 4
    YROWS = TOPK * NT * P
    EPS = 1e-5
    SCALE = float(LAT) ** -0.5
    NEG = -1e30
    QT = [(0, NIMG)] + [(NIMG + P * i, P) for i in range(NTXT // P)]
    NQ = len(QT)
    KT = [(P * i, min(P, T - P * i)) for i in range(-(-T // P))]
    QROWS = [0, 0, 0, 1, 1, 2]
    KROWS = [0, 1, 2, 0, 1, 0]
    CON = HD * len(QROWS)
    CONM = CON + 3

    SPIECE = [[(0, 0, 36, 0), (1, 0, 164, 36), (2, 0, 292, 200)],
              [(3, 0, 420, 0), (4, 512, 36, 420)],
              [(4, 0, 512, 0)]]
    TPIECE = [[(0, 0, 512, 0)],
              [(0, 512, 36, 0), (1, 128, 420, 36)],
              [(2, 256, 292, 0), (3, 384, 164, 292), (4, 512, 36, 456)]]
    TOFF = [0, 512, 968]
    PW = 1460
    DIAG = [(0, P), (512 + 36, P), (968, P), (968 + 292, P), (968 + 456, T - 4 * P)]
    SEG = []
    for pc, off in zip(TPIECE, TOFF):
        for kt, q0, w, c in pc:
            for h0 in (0, HT):
                lo, hi = max(q0, h0), min(q0 + w, h0 + HT)
                if lo < hi:
                    SEG.append((h0 // HT, kt, off + c + lo - q0, lo, hi - lo))
    SEG.sort()
    HTILE = [(i, min(P, HT - i)) for i in range(0, HT, P)]
    CLEARS = 9
    NP = 7



    def spread(*lists):
        at = [((i + 0.5) / len(x), n, job) for n, x in enumerate(lists) for i, job in enumerate(x)]
        return [job for _, _, job in sorted(at, key=lambda a: a[:2])]

    def halves(name, u):
        return [(name, u, 0), (name, u, 1)]

    def maxima_of(u, heads):
        return [("S", u, j, p) for j in heads for p in range(len(SPIECE))]

    def unit_stages(u, j):
        if u % 2 == 0:
            b, pb = u // 2 + 1, u // 2 - 1
            front = {0: [("hT", b, 0), ("hT", b, 1)] if u else [], 1: [("hT", b, 2), ("hT", b, 3)] if u else [],
                     2: halves("kv", b) + halves("Q", u + 2) + [("Qx", u + 2)],
                     3: halves("K", u + 2) + [("Kx", u + 2), ("Qy", u + 2)],
                     4: [("Ky", u + 2), ("V", b, 0)], 5: [("V", b, 1)], 6: [("V", b, 2)]}
            back = {4: [("W", pb, i) for i in range(2)], 7: [("W", pb, i) for i in range(2, 4)]}
        else:
            b, pb = (u + 1) // 2 + 1, (u - 3) // 2
            front = {}
            if u + 2 < UNITS:
                front = {1: halves("Q", u + 2), 2: [("Qx", u + 2)],
                         3: halves("K", u + 2) + [("Kx", u + 2), ("Qy", u + 2)], 4: [("Ky", u + 2)]}
            if b < B:
                front.update({6: [("ln1s", b), ("rs", b)], 7: [("ln1", b)]})
            back = {0: [("W", pb, 4), ("ln2s", pb), ("rs", pb)], 1: [("ln2", pb)],
                    2: [("hl", pb), ("RT", pb, 0), ("RT", pb, 1), ("RL", pb, 0)],
                    3: [("RL", pb, 1), ("RT", pb, 2), ("RL", pb, 2), ("RT", pb, 3)],
                    4: [("RL", pb, 3), ("RT", pb, 4), ("RL", pb, 4)],
                    5: [("pr", pb), ("norm", pb)], 6: [("two", pb), ("top", pb)], 7: [("slot", pb)]}
        out = []
        if u % 2 == 0 and u >= 4 and j < NQ:
            out += [("sc", u // 2 - 2, j)]
        if pb >= 0:
            out += back.get(j, [])
        if b < B or u % 2 == 1:
            out += front.get(j, [])
        return out

    order = [("embed", 0), ("ln1s", 0), ("rs", 0), ("ln1", 0)] + [("hT", 0, f) for f in range(4)]
    order += halves("kv", 0) + halves("Q", 0) + [("Qx", 0)] + halves("K", 0) + [("Kx", 0), ("Qy", 0), ("Ky", 0)]
    order += halves("Q", 1) + [("Qx", 1)] + halves("K", 1) + [("Kx", 1)]
    order += [("V", 0, f) for f in range(3)] + [("embed", 1), ("Qy", 1), ("Ky", 1)]
    order += spread(maxima_of(0, range(UH)), [("ln1s", 1), ("rs", 1), ("embed", 2), ("ln1", 1)])
    order += [("mxc", 0), ("M", 0, 0), ("M", 0, 1), ("Mx", 0)]
    order += [("hT", 1, f) for f in range(4)] + maxima_of(1, [0]) + [("embed", 3)]
    S_AT = {0: [0], 1: [1], 2: [2, 3], 3: [4], 4: [5, 6], 5: [7]}
    for u in range(UNITS):
        nxt = u + 1 < UNITS
        for j in range(UH):
            ctx_of = (u - 1, 1) if j < 4 else (u, 0)
            half = (len(SEG) + 1) // 2
            parts = {1: range(half), 2: range(half, len(SEG))}.get(j % 4, [])
            pv = [("PV", *ctx_of, i) for i in parts] if ctx_of[0] >= 0 else []
            if j == 6 and nxt:
                order += [("mxc", u + 1)]
            norm = []
            if j % 4 == 3 and ctx_of[0] >= 0:
                norm = [("N", ctx_of[0] // 2, 2 * (ctx_of[0] % 2) + ctx_of[1])]
            scores = [("T", u, j, p) for p in range(len(TPIECE))]
            if j == 6 and nxt:
                scores[2:] = [("M", u + 1, 0)] + scores[2:] + [("M", u + 1, 1), ("Mx", u + 1)]
            order += spread(scores,
                            maxima_of(u + 1, S_AT.get(j, [])) if nxt and (u, j) != (0, 0) else [], pv, norm,
                            unit_stages(u, j))
            if j % 4 == 2 and ctx_of[0] >= 0:
                order += [("O", *ctx_of)]
            if j in (2, 5, 7) and 3 * u + (2, 5, 7).index(j) < CLEARS:
                order += [("clear", 3 * u + (2, 5, 7).index(j))]
            if j % 4 == 3 and ctx_of[0] >= 0:
                b, g = ctx_of[0] // 2, 2 * (ctx_of[0] % 2) + ctx_of[1]
                order += [("Nx", b, g, 0), ("Nx", b, g, 1)]
    b = B - 1
    order += [("sc", b - 1, i) for i in range(NQ)] + [("Wa", b, 0), ("Wa", b, 1)]
    order += [("PV", UNITS - 1, 1, i) for i in range(len(SEG))] + [("O", UNITS - 1, 1), ("Wa", b, 2)]
    order += [("N", b, 3), ("Wa", b, 3), ("Nx", b, 3, 0), ("Nx", b, 3, 1)] + [("W", b, i) for i in range(NQ)]
    order += [("ln2s", b), ("rs", b), ("w0",), ("ln2", b), ("hl", b), ("RT", b, 0)]
    for i in range(1, NQ):
        order += [("RT", b, i), ("RL", b, i - 1)]
    order += [("RL", b, NQ - 1), ("pr", b), ("norm", b), ("two", b), ("top", b), ("slot", b)]
    order += [("sc", b, i) for i in range(NQ)]

    fills = {}
    for job in order:
        if job[0] in ("embed", "hT", "kv", "V", "Q", "K", "M", "N", "Nx", "W", "RT", "RL", "slot"):
            fills[job] = len(fills)
    ROUNDS = 30

    lo_count = {(job[0][0], job[1]): n + 1 for n, job in enumerate(x for x in order if x[0] in ("Qx", "Kx"))}
    ln_order = [job for job in order if job[0] in ("ln1", "ln2")]
    ln_count = {job: n + 1 for n, job in enumerate(ln_order)}

    ctx = ExitStack()
    with ctx:
        def sem(name):
            return ctx.enter_context(nc.semaphore(name))

        def sb(name, shape, dt, where=ctx):
            return where.enter_context(nc.sbuf_tensor(name, shape, dt))

        xs_d = nc.dram_tensor("split_scratch", [2, UNITS, 3, P, T], bf16).ap()
        xe_d = nc.dram_tensor("expert_in", [SROWS, ROWC], bf16).ap()
        xhl_d = nc.dram_tensor("xhl_scratch", [P, NT, ROWC], bf16).ap()
        y_d = nc.dram_tensor("expert_out", [YROWS, D], f32).ap()

        ident = sb("ident", [P, P], f32)
        identb = sb("identb", [P, P], bf16)
        H = sb("H", [P, B, NQ, D], f32)
        LG = sb("LG", [P, NT, NE], f32)
        zero = sb("zero", [P, ROWC], bf16)
        ones = sb("ones", [P, P], f32)
        onesb = sb("onesb", [P, P], bf16)
        trib = sb("trib", [P, P], bf16)
        valid = sb("valid", [P, NT, NE], f32)
        iota8 = sb("iota8", [P, NT, NE], f32)
        base8 = sb("base8", [P, NT, NE], f32)
        sidx = sb("sidx", [P, TOPK, NT], u32)
        token1 = sb("token1", [P, NT], f32)
        dest = sb("dest", [P, 2, CAP // P + 1], u32)
        dst = sb("dst", [P, 3, CAP // P + 1], f32)
        gate = sb("gate", [P, TOPK, NT], f32)
        EP = sb("EP", [P, NT, NE], f32)
        E2 = sb("E2", [P, NT, NE], f32)
        E3 = sb("E3", [P, NT, NE], f32)
        OH = sb("OH", [P, TOPK, NT, NE], f32)
        POS = sb("POS", [P, NT, NE], f32)
        Xb = sb("Xb", [P, NT, NE], bf16)
        r20 = sb("r20", [P, 4, NT], f32)
        v8 = sb("v8", [P, NT, 8], f32)
        i8 = sb("i8", [P, NT, 8], u32)
        i8f = sb("i8f", [P, NT, 8], f32)
        c8 = sb("c8", [P, NE], f32)
        most = sb("most", [P, 1], u32)

        att = ExitStack()
        wq = sb("wq", [P, DK, D], f32, att)
        wkv = sb("wkv", [P, DK, 2 * LAT], f32, att)
        q2l = sb("q2l", [LAT, HEADS * HD], f32, att)
        vu = sb("vu", [P, HEADS * HD], f32, att)
        wo = sb("wo", [P, 4, D], f32, att)
        wr = sb("wr", [P, DK, NE], f32, att)
        nhalf = sb("nhalf", [P, NQ], f32, att)
        maskn = sb("maskn", [P, T], f32, att)
        st = sb("st", [P, NQ, 6], f32, att)
        mv = sb("mv", [P, NQ, 2], f32, att)
        rs = sb("rs", [P, NQ], f32, att)
        ve = sb("ve", [P, NQ], f32, att)
        xh = sb("xh", [P, NQ, D], f32, att)
        hnT = sb("hnT", [P, DK, T], f32, att)
        lat = sb("lat", [P, T], f32, att)
        V = sb("V", [P, 2, NQ, HEADS, 1 + HD], f32, att)
        XS = sb("XS", [P, 2, 3, T], bf16, att)
        XR = sb("XR", [P, T], f32, att)
        Qs = [sb(f"Qs{i}", [P, UH, T], bf16, att) for i in range(3)]
        Ks = [sb(f"Ks{i}", [P, UH, SP_], bf16, att) for i in range(3)]
        mx = sb("mx", [P, 2, NQ + 1, UH], f32, att)
        NS = sb("NS", [UH, 3, T], bf16, att)
        NR = sb("NR", [UH, T], f32, att)
        Pr = sb("Pr", [P, NP, PW], f32, att)
        Of = sb("Of", [P, 2, 4, T], f32, att)
        RD = sb("RD", [P, 2, len(HTILE), 4], f32, att)
        first = sb("first", [P, 4], f32, att)
        emb = ExitStack()
        PT = sb("PT", [P, PK, B * NIMG], f32, emb)
        TW = sb("TW", [P, PK, D], f32, emb)
        tb = sb("tb", [1, D], f32, emb)
        emb.close()
        XHL = sb("XHL", [P, 2, NQ, ROWC], bf16, att)
        xnT = sb("xnT", [P, 2, DK * P], f32, att)

        bankS = [ctx.enter_context(nc.psum_tensor(f"bankS{i}", [P, 512], f32)) for i in range(2)]
        bankT = [ctx.enter_context(nc.psum_tensor(f"bankT{i}", [P, 512], f32)) for i in range(2)]
        bankO = ctx.enter_context(nc.psum_tensor("bankO", [P, 2, 512], f32))
        bankM = [ctx.enter_context(nc.psum_tensor(f"bankM{i}", [P, 512], f32)) for i in range(2)]

        ld_tok, ld_att = sem("ld_tok"), sem("ld_att")
        ld_txt = [sem(f"ld_txt{b}") for b in range(B)]
        zeroed = sem("zeroed")
        pool_const, dve_const = sem("pool_const"), sem("dve_const")
        keys_const = sem("keys_const")
        m_full = [sem(f"m_full{i}") for i in range(2)]
        m_used = [sem(f"m_used{i}") for i in range(2)]
        mean_ready, rstd_ready, xhat_ready = sem("mean_ready"), sem("rstd_ready"), sem("xhat_ready")
        hi_ready, lo_ready = sem("hi_ready"), sem("lo_ready")
        split_stored = [sem(f"split_stored{i}") for i in range(2)]
        stack_ready = [sem(f"stack_ready{i}") for i in range(3)]
        s_full = [sem(f"s_full{i}") for i in range(2)]
        s_used = [sem(f"s_used{i}") for i in range(2)]
        t_full = [sem(f"t_full{i}") for i in range(2)]
        t_used = [sem(f"t_used{i}") for i in range(2)]
        max_ready, nmhi_ready, nm_ready = sem("max_ready"), sem("nmhi_ready"), sem("nm_ready")
        maxrow_ready = [sem(f"maxrow_ready{i}") for i in range(2)]
        prob_ready = sem("prob_ready")
        o_full, o_used = sem("o_full"), sem("o_used")
        xhi_ready, xhl_ready = sem("xhi_ready"), sem("xhl_ready")
        xhl_stored = sem("xhl_stored")
        rexp_in, rexp = sem("rexp_in"), sem("rexp")
        cnt_in = sem("cnt_in")
        idx_ready = sem("idx_ready")
        most_ready = sem("most_ready")
        scattered = [sem("scattered0"), sem("scattered1")]
        over_in, over_out, over_chain = sem("over_in"), sem("over_out"), sem("over_chain")
        over_idx, over_xa, over_scattered = sem("over_idx"), sem("over_xa"), sem("over_scattered")
        rest_w, rest_xe, rest_whi, rest_wlo = sem("rest_w"), sem("rest_xe"), sem("rest_whi"), sem("rest_wlo")
        rest_tr, rest_xt, rest_up, rest_hi = sem("rest_tr"), sem("rest_xt"), sem("rest_up"), sem("rest_hi")
        rest_lo, rest_down, rest_y, rest_stored = sem("rest_lo"), sem("rest_down"), sem("rest_y"), sem("rest_stored")
        rest_chain = sem("rest_chain")
        dve_chain, pool_chain = sem("dve_chain"), sem("pool_chain")
        w_loaded, xe_loaded = [sem("w_loaded0"), sem("w_loaded1")], [sem("xe_loaded0"), sem("xe_loaded1")]
        whi_ready, wlo_ready = sem("whi_ready"), sem("wlo_ready")
        tr_full = [sem(f"tr_full{i}") for i in range(2)]
        tr_used = [sem(f"tr_used{i}") for i in range(2)]
        h_full = [sem(f"h_full{i}") for i in range(4)]
        hhi_ready = sem("hhi_ready")
        h_used = [sem(f"h_used{i}") for i in range(4)]
        y_full = [sem(f"y_full{i}") for i in range(2)]
        y_used = [sem(f"y_used{i}") for i in range(2)]
        y_stored = [sem("y_stored0"), sem("y_stored1")]
        dest_ready = sem("dest_ready")
        gathered = [sem(f"gathered{i}") for i in range(B)]
        combined = sem("combined")
        gated = sem("gated")
        combined_last, combine_chain = sem("combined_last"), sem("combine_chain")
        stored = sem("stored")

        def filled(eng, key):
            n = fills[key]
            eng.wait_ge(m_full[n % 2], n // 2 + 1)

        def used(eng, key):
            n = fills[key]
            eng.wait_ge(m_used[n % 2], n // 2 + 1)

        def open_fill(pe, key):
            n = fills[key]
            if n >= 2:
                pe.wait_ge(m_used[n % 2], n // 2)
            return bankM[n % 2]

        att.close()
        ffn = ExitStack()
        NMAIN = CAP // P * P
        NREST = CAP - NMAIN
        NST = NMAIN // P
        XE = sb("XE", [P, 2, NST, ROWC], bf16, ffn)
        XT = sb("XT", [P, 2, 2 * DK, NMAIN], bf16, ffn)
        HH = sb("HH", [P, 2, FK, NMAIN], bf16, ffn)
        W1f = sb("W1f", [P, DK, FF], f32, ffn)
        W2f = sb("W2f", [P, FK, D], f32, ffn)
        W1s = sb("W1s", [P, 2, 2, DK, FF], bf16, ffn)
        W2s = sb("W2s", [P, 2, 2, FK, D], bf16, ffn)
        HL = sb("HL", [P, 2, FK, NMAIN], bf16, ffn)
        Y = sb("Y", [P, 2, NST, D], f32, ffn)
        XA = sb("XA", [P, NT, ROWC], bf16, ffn)
        G = sb("G", [P, NT, NE], f32, ffn)
        KEEP = sb("KEEP", [P, NT, NE], f32, ffn)
        thr = sb("thr", [P, NE], f32, ffn)
        cand = sb("cand", [P, NE], f32, ffn)
        t8 = sb("t8", [P, NE], f32, ffn)
        room = sb("room", [P, NE], f32, ffn)
        ffn.close()
        combine = ExitStack()
        GY = sb("GY", [P, B, NQ, TOPK, D], f32, combine)
        combine.close()
        ST = [(P * i, P) for i in range(NST)]
        CH = [(0, NMAIN // 2), (NMAIN // 2, NMAIN // 2)]

        FIRST = 3 * UH

        def score_bank(n):
            return (bankS, bankT)[n // 2 % 2 if n < FIRST else 0][n % 2]

        def attended(b, i):
            n = QT[i][1]
            if b == B - 1 and i < 4:
                return (bankS, bankT)[i // 2][i % 2][0:n, 0:D]
            return bankM[fills[("W", b, i)] % 2][0:n, 0:D]

        def most_tokens(eng):
            eng.wait_ge(most_ready, 1)
            return eng.value_load(most[0:1, 0:1], min_val=0, max_val=NTOK)

        def earlier_tokens(o, t0, tiles):
            nc.tensor.matmul(o, trib[:, :], Xb[:, t0:t0 + tiles, :], start=True, stop=False)
            for t in range(t0 + tiles - 1):
                f = max(t + 1 - t0, 0)
                last = nc.tensor.matmul(o[:, f:, :], onesb[:, :],
                                        Xb[:, t:t + 1, :].to_broadcast([P, tiles - f, NE]),
                                        start=False, stop=(t == t0 + tiles - 2))
            return last

        block = ctx.enter_context(nc.Block())

        @block.sync
        def _(sp):
            sp.dma_start(PT[:, :, :], patchesT.rearrange("(k p) n -> p k n", p=P)).then_inc(ld_tok, 16)
            sp.dma_start(TW[:, :, :], tokWT.rearrange("(k p) n -> p k n", p=P)).then_inc(ld_tok, 16)
            sp.dma_start(tb[:, :], tokb.unsqueeze(0)).then_inc(ld_tok, 16)
            for b in range(B):
                sp.dma_start(H[:, b, 1:, :], txt[b].rearrange("(i p) d -> p i d", p=P)).then_inc(ld_txt[b], 16)
                if b == 0:
                    sp.dma_start(wkv[:, :, :], WkvT.rearrange("(k p) n -> p k n", p=P)).then_inc(ld_att, 16)
                    sp.dma_start(wq[:, :, :], WqT.rearrange("(k p) n -> p k n", p=P)).then_inc(ld_att, 16)
                    sp.dma_start(q2l[:, :], q2lT).then_inc(ld_att, 16)
                    sp.dma_start(vu[LAT:2 * LAT, :], vup).then_inc(ld_att, 16)
                    sp.dma_start(wr[:, :, :], Wr.rearrange("(k p) n -> p k n", p=P)).then_inc(ld_att, 16)
                    sp.wait_ge(dve_const, 1)
                    wv = WoT.rearrange("(g j d) n -> j d g n", j=4, d=HD)
                    for j in range(4):
                        sp.dma_start(wo[32 * j + 1:32 * j + 1 + HD, :, :], wv[j]).then_inc(ld_att, 16)

            def clear(k):
                sp.wait_ge(dve_const, 1)
                n = SROWS // P
                r0, r1 = P * (n * k // CLEARS), P * (n * (k + 1) // CLEARS)
                sp.dma_start(xe_d[r0:r1, :].rearrange("(p r) c -> p r c", p=P),
                             zero[:, :].unsqueeze(1).to_broadcast([P, (r1 - r0) // P, ROWC])).then_inc(zeroed, 16)
                n = YROWS // P
                r0, r1 = P * (n * k // CLEARS), P * (n * (k + 1) // CLEARS)
                sp.dma_start(y_d[r0:r1, :].rearrange("(p r) d -> p r d", p=P),
                             zero[:, 0:2 * D].bitcast(f32).unsqueeze(1).to_broadcast([P, (r1 - r0) // P, D])
                             ).then_inc(zeroed, 16)

            def split_out(which, u):
                sp.wait_ge(lo_ready, 2 * u + which + 1)
                sp.dma_start(xs_d[which, u].rearrange("s p t -> p s t"),
                             XS[:, which, :, :]).then_inc(split_stored[which], 16)

            def stack_in(which, u):
                stacks, rows = (Qs, QROWS) if which == 0 else (Ks, KROWS)
                sp.wait_ge(split_stored[which], 16 * (u + 1))
                if u >= 3:
                    n = 3 * UH * (u - 2) - 1
                    sp.wait_ge(t_full[n % 2], n // 2 + 1)
                for g, part in enumerate(rows):
                    sp.dma_start(stacks[u % 3][HD * g:HD * (g + 1), :, 0:T],
                                 xs_d[which, u, part].rearrange("(j d) t -> d j t", d=HD)
                                 ).then_inc(stack_ready[u % 3], 16)

            def load_weights(e):
                if e >= 1:
                    sp.wait_ge(whi_ready, e)
                    sp.wait_ge(wlo_ready, e)
                sp.dma_start(W1f[:, :, :], W1[e].rearrange("(k p) f -> p k f", p=P)).then_inc(w_loaded[e % 2], 16)
                sp.dma_start(W2f[:, :, :], W2[e].rearrange("(k p) d -> p k d", p=P)).then_inc(w_loaded[e % 2], 16)

            def max_rows(u):
                sp.wait_ge(nm_ready, u + 1)
                for g in range(3):
                    sp.dma_start(Qs[u % 3][CON + g:CON + g + 1, :, :],
                                 NS[:, g, :]).then_inc(maxrow_ready[u % 2], 16)

            for job in order:
                k, a = job[0], (job[1] if len(job) > 1 else None)
                if k == "Qx":
                    split_out(0, a)
                elif k == "Kx":
                    split_out(1, a)
                elif k == "Qy":
                    stack_in(0, a)
                elif k == "Ky":
                    stack_in(1, a)
                elif k == "Mx":
                    max_rows(a)
                elif k == "clear":
                    clear(a)
                elif k == "w0":
                    for n in range(3 * UH * UNITS - 2, 3 * UH * UNITS):
                        sp.wait_ge(t_full[n % 2], n // 2 + 1)
                    load_weights(0)
                elif k == "slot":
                    sp.wait_ge(xhl_ready, a + 1)
                    sp.wait_ge(idx_ready, a + 1)
                    sp.dma_start(xhl_d[:, NQ * a:NQ * (a + 1), :], XHL[:, a % 2, :, :]).then_inc(xhl_stored, 16)


            def load_slots(e):
                if e >= 2:
                    sp.wait_ge(dest_ready, e - 1)
                    n = NST * (e - 1) - 1
                    sp.wait_ge(tr_full[n % 2], n // 2 + 1)
                sp.dma_start(XE[:, e % 2, :, :],
                             xe_d[e * CAP:e * CAP + NMAIN, :].rearrange("(i p) c -> p i c", p=P)
                             ).then_inc(xe_loaded[e % 2], 16)

            for p in range(2):
                sp.wait_ge(scattered[p], 16 * TOPK * NQ * B // 2)
            used(sp, ("slot", B - 1))
            tokens = most_tokens(sp)
            with sp.If(tokens > CAP):
                sp.wait_ge(xhl_stored, 16 * B)
                sp.dma_start(XA[:, :, :], xhl_d).then_inc(over_xa, 16)
                sp.wait_ge(over_scattered, 16 * TOPK * NT)
            load_slots(0)
            load_weights(1)
            for e in range(NE):
                if e + 1 < NE:
                    load_slots(e + 1)
                if e + 2 < NE:
                    load_weights(e + 2)
            with sp.If(tokens > NMAIN):
                for e in range(NE):
                    if e == 0:
                        sp.wait_ge(whi_ready, NE)
                        sp.wait_ge(wlo_ready, NE)
                        sp.wait_ge(dest_ready, NE)
                        for q in (NE * NST - 2, NE * NST - 1):
                            sp.wait_ge(tr_full[q % 2], q // 2 + 1)
                    else:
                        sp.wait_ge(rest_whi, e)
                        sp.wait_ge(rest_wlo, e)
                        sp.wait_ge(rest_tr, e)
                        sp.wait_ge(dest_ready, NE + e)
                    sp.dma_start(W1f[:, :, :], W1[e].rearrange("(k p) f -> p k f", p=P)).then_inc(rest_w, 16)
                    sp.dma_start(W2f[:, :, :], W2[e].rearrange("(k p) d -> p k d", p=P)).then_inc(rest_w, 16)
                    sp.dma_start(XE[0:NREST, 0, 0, :], xe_d[e * CAP + NMAIN:(e + 1) * CAP, :]).then_inc(rest_xe, 16)
                sp.wait_ge(rest_stored, 16 * NE)
            for p in range(2):
                sp.wait_ge(y_stored[p], 16 * NST * NE // 2)
            yv = y_d.rearrange("(t c p) d -> p t c d", c=TOPK, p=P)
            for b in (0, 1, B - 1, *range(2, B - 1)):
                sp.dma_start(GY[0:NIMG, b, 0, :, :], yv[0:NIMG, NQ * b, :, :]).then_inc(gathered[b], 16)
                sp.dma_start(GY[:, b, 1:, :, :], yv[:, NQ * b + 1:NQ * (b + 1), :, :]).then_inc(gathered[b], 16)

            def rows_out(b, i, tiles):
                q0, n = QT[i][0], QT[i][1]
                sp.dma_start(out[b, q0:q0 + n * tiles, :].rearrange("(i p) d -> p i d", p=n),
                             H[0:n, b, i:i + tiles, :]).then_inc(stored, 16)

            for b in range(B - 1):
                sp.wait_ge(combined, NQ * b + 1)
                rows_out(b, 0, 1)
                for i in (1, 3):
                    sp.wait_ge(combined, NQ * b + i + 2)
                    rows_out(b, i, 2)
                if b == B - 3:
                    sp.wait_ge(combined_last, 1)
                    rows_out(B - 1, 0, 1)
                    rows_out(B - 1, 1, 4)
            sp.wait_ge(stored, 16 * (3 * (B - 1) + 2))

        @block.gpsimd
        def _(pool):
            chain = [0]

            def link(ins):
                chain[0] += 1
                ins.then_inc(pool_chain, 1)
                pool.wait_ge(pool_chain, chain[0])

            link(nc.gpsimd.memset(ident[:, :], 0.0))
            link(nc.gpsimd.affine_select(out=ident[:, :], in_=ident[:, :], compare_op=ALU.not_equal, fill=1.0,
                                         base=0, pattern=[[-1, P]], channel_multiplier=1))
            nc.gpsimd.tensor_copy(identb[:, :], ident[:, :])
            link(nc.gpsimd.memset(maskn[:, :], 0.0))
            tri = maskn[:, T - P:T]
            link(nc.gpsimd.affine_select(out=tri, in_=tri, compare_op=ALU.is_ge, fill=NEG,
                                         base=0, pattern=[[-1, P]], channel_multiplier=1))
            link(nc.gpsimd.memset(first[:, :], 0.0))
            link(nc.gpsimd.affine_select(out=first[:, :], in_=first[:, :], compare_op=ALU.not_equal, fill=1.0,
                                         base=0, pattern=[[-32, 4]], channel_multiplier=1))
            link(nc.gpsimd.memset(trib[:, :], 1.0))
            link(nc.gpsimd.affine_select(out=trib[:, :], in_=trib[:, :], compare_op=ALU.is_gt, fill=0.0,
                                         base=0, pattern=[[1, P]], channel_multiplier=-1))
            link(nc.gpsimd.memset(valid[:, :, :], 1.0))
            for b in range(B):
                v = valid[:, b * NQ, :]
                link(nc.gpsimd.affine_select(out=v, in_=v, compare_op=ALU.is_gt, fill=0.0,
                                             base=NIMG, pattern=[[0, NE]], channel_multiplier=-1))
            nc.gpsimd.iota(iota8[:, :, :], pattern=[[0, NT], [1, NE]], base=0, channel_multiplier=0,
                           allow_small_or_imprecise_dtypes=True)
            nc.gpsimd.iota(base8[:, :, :], pattern=[[0, NT], [CAP, NE]], base=0, channel_multiplier=0,
                           allow_small_or_imprecise_dtypes=True)
            nc.gpsimd.iota(token1[:, :], pattern=[[TOPK * P, NT]], base=1, channel_multiplier=1,
                           allow_small_or_imprecise_dtypes=True)
            nc.gpsimd.memset(nhalf[:, :], -0.5).then_inc(pool_const, 1)

            norms = [0]

            def rstd():
                norms[0] += 1
                pool.wait_ge(mean_ready, norms[0])
                link(nc.gpsimd.tensor_scalar(ve[:, :], mv[:, :, 1], EPS, None, ALU.add))
                nc.gpsimd.tensor_tensor(rs[:, :], ve[:, :], nhalf[:, :], ALU.pow).then_inc(rstd_ready, 1)

            def key_constants():
                for i in range(3):
                    link(nc.gpsimd.memset(Ks[i][:, :, T:SP_].bitcast(f32), 0.0))
                    nc.gpsimd.memset(Ks[i][CON:P, :, 0:T].bitcast(u32), 0x3F803F80).then_inc(keys_const, 1)
                    pool.wait_ge(keys_const, i + 1)

            def causal(u, j, p):
                hh = UH * u + j
                n = 3 * hh + p
                pool.wait_ge(t_used[n % 2], n // 2 + 1)
                for c, w in ([DIAG[0]], [DIAG[1]], DIAG[2:])[p]:
                    v = Pr[:, hh % NP, c:c + w]
                    last = nc.gpsimd.affine_select(out=v, in_=v, compare_op=ALU.is_ge, fill=0.0,
                                                   base=0, pattern=[[1, w]], channel_multiplier=-1)
                if p == 2:
                    last.then_inc(prob_ready, 1)

            def scatter(rows, t, c, done):
                n = QT[t % NQ][1]
                nc.gpsimd.indirect_dma_start(
                    out=xe_d[:, :], out_offset=bass.IndirectOffsetOnAxis(ap=sidx[0:n, c, t:t + 1], axis=0),
                    in_=rows, in_offset=None, bounds_check=SLOTS - 1, oob_is_err=False).then_inc(done, 16)

            def weights_low(e):
                pool.wait_ge(w_loaded[e % 2], 32 * (e // 2 + 1))
                pool.wait_ge(whi_ready, e + 1)
                nc.gpsimd.tensor_tensor(W1s[:, e % 2, 1, :, :], W1f[:, :, :], W1s[:, e % 2, 0, :, :], ALU.subtract)
                nc.gpsimd.tensor_tensor(W2s[:, e % 2, 1, :, :], W2f[:, :, :], W2s[:, e % 2, 0, :, :],
                                        ALU.subtract).then_inc(wlo_ready, 1)

            for job in order:
                k, a = job[0], (job[1] if len(job) > 1 else None)
                if k == "rs":
                    rstd()
                    if a == 0 and norms[0] == 1:
                        key_constants()
                elif k == "T":
                    causal(*job[1:])
                elif k == "w0":
                    weights_low(0)
                elif k == "sc":
                    if job[2] == 0:
                        pool.wait_ge(idx_ready, a + 1)
                        pool.wait_ge(zeroed, 32 * CLEARS)
                        pool.wait_ge(xhl_ready, a + 1)
                    for c in range(TOPK):
                        scatter(XHL[0:QT[job[2]][1], a % 2, job[2], :], NQ * a + job[2], c, scattered[a % 2])
                elif k == "hl":
                    pool.wait_ge(xhi_ready, a + 1)
                    nc.gpsimd.tensor_tensor(XHL[:, a % 2, :, D:2 * D], xh[:, :, :], XHL[:, a % 2, :, 0:D],
                                            ALU.subtract).then_inc(xhl_ready, 1)

            tokens = most_tokens(pool)
            with pool.If(tokens > CAP):
                pool.wait_ge(over_idx, 1)
                pool.wait_ge(over_xa, 16)
                for t in range(NT):
                    for c in range(TOPK):
                        scatter(XA[0:QT[t % NQ][1], t, :], t, c, over_scattered)

            def results_out(n, p, i, done):
                nc.gpsimd.indirect_dma_start(
                    out=y_d[:, :], out_offset=bass.IndirectOffsetOnAxis(ap=dest[0:n, p, i:i + 1], axis=0),
                    in_=Y[0:n, p, i, :], in_offset=None, bounds_check=YROWS - 1, oob_is_err=False).then_inc(done, 16)

            for e in range(NE):
                if e + 1 < NE:
                    if e >= 1:
                        q = e * NST - 1
                        pool.wait_ge(y_full[q % 2], q // 2 + 1)
                    weights_low(e + 1)
                pool.wait_ge(dest_ready, e + 1)
                for i in range(NST):
                    q = e * NST + i
                    pool.wait_ge(y_used[q % 2], q // 2 + 1)
                    results_out(P, e % 2, i, y_stored[e % 2])
            with pool.If(tokens > NMAIN):
                for e in range(NE):
                    pool.wait_ge(rest_w, 32 * (e + 1))
                    pool.wait_ge(rest_whi, e + 1)
                    nc.gpsimd.tensor_tensor(W1s[:, 0, 1, :, :], W1f[:, :, :], W1s[:, 0, 0, :, :], ALU.subtract)
                    nc.gpsimd.tensor_tensor(W2s[:, 0, 1, :, :], W2f[:, :, :], W2s[:, 0, 0, :, :],
                                            ALU.subtract).then_inc(rest_wlo, 1)
                    pool.wait_ge(dest_ready, NE + e + 1)
                    pool.wait_ge(rest_y, e + 1)
                    results_out(NREST, 0, 0, rest_stored)

            for c in range(TOPK):
                pool.wait_ge(gated, c + 1)
                if c > 0:
                    pool.wait_ge(combine_chain, 2)
                for i, tiles, n in ((0, 1, NIMG), (1, NQ - 1, P)):
                    h = H[0:n, B - 1, i:i + tiles, :]
                    last = nc.gpsimd.tensor_tensor(h, h, GY[0:n, B - 1, i:i + tiles, c, :], ALU.add)
                    if c < TOPK - 1:
                        last.then_inc(combine_chain, 1)
            last.then_inc(combined_last, 1)

        @block.tensor
        def _(pe):
            pe.wait_ge(dve_const, 1)

            def project(key, lhsT_of, rhs_of, nk, n=HT):
                bank = open_fill(pe, key)
                for k in range(nk):
                    last = nc.tensor.matmul(bank[:, 0:n], lhsT_of(k), rhs_of(k), start=(k == 0), stop=(k == nk - 1))
                last.then_inc(m_full[fills[key] % 2], 1)

            def embed(b):
                if b == 0:
                    pe.wait_ge(ld_tok, 48)
                bank = open_fill(pe, ("embed", b))
                o = bank[0:NIMG, 0:D]
                for k in range(PK):
                    nc.tensor.matmul(o, PT[:, k, NIMG * b:NIMG * (b + 1)], TW[:, k, :], start=(k == 0), stop=False)
                nc.tensor.matmul(o, ones[0:1, 0:NIMG], tb[0:1, :], start=False, stop=True
                                 ).then_inc(m_full[fills[("embed", b)] % 2], 1)

            def transpose_h(b, f):
                if b == 0 and f == 0:
                    pe.wait_ge(pool_const, 1)
                if f == 0:
                    pe.wait_ge(xhat_ready, ln_count[("ln1", b)])
                k, tiles = f // 2, (QT[0:3] if f % 2 == 0 else QT[3:5])
                bank = open_fill(pe, ("hT", b, f))
                for q0, n in tiles:
                    i = QT.index((q0, n))
                    c = q0 - tiles[0][0]
                    last = nc.tensor.transpose(bank[:, c:c + n], xh[0:n, i, P * k:P * (k + 1)], ident[0:n, 0:n])
                last.then_inc(m_full[fills[("hT", b, f)] % 2], 1)

            def kv(b, hf):
                if b == 0 and hf == 0:
                    pe.wait_ge(ld_att, 16 * 9)
                for f in range(4):
                    used(pe, ("hT", b, f))
                project(("kv", b, hf), lambda k: wkv[:, k, :], lambda k: hnT[:, k, HT * hf:HT * (hf + 1)], DK)

            def values(b, f):
                for hf in range(2):
                    used(pe, ("kv", b, hf))
                bank = open_fill(pe, ("V", b, f))
                for i in range(2 * f, min(2 * f + 2, len(KT))):
                    s0, n = KT[i]
                    last = nc.tensor.matmul(bank[0:n, D * (i % 2):D * (i % 2 + 1)], lat[LAT:2 * LAT, s0:s0 + n],
                                            vu[LAT:2 * LAT, :], start=True, stop=True)
                last.then_inc(m_full[fills[("V", b, f)] % 2], 1)

            def queries(u, hf):
                for f in range(4):
                    used(pe, ("hT", u // 2, f))
                m = P * (u % 2)
                project(("Q", u, hf), lambda k: wq[:, k, m:m + P], lambda k: hnT[:, k, HT * hf:HT * (hf + 1)], DK)

            def keys(u, hf):
                for h in range(2):
                    used(pe, ("kv", u // 2, h))
                m = P * (u % 2)
                project(("K", u, hf), lambda k: q2l[:, m:m + P], lambda k: lat[0:LAT, HT * hf:HT * (hf + 1)], 1)

            def scores(u, j, p):
                if j == 0 and p == 0:
                    pe.wait_ge(stack_ready[u % 3], 16 * 12 * (u // 3 + 1))
                    if u < 3:
                        pe.wait_ge(keys_const, u + 1)
                n = 3 * (UH * u + j) + p
                if n >= (4 if n < FIRST else 2):
                    pe.wait_ge(s_used[n % 2], n // 2 - (1 if n < FIRST else 0))
                for i, s0, w, c in SPIECE[p]:
                    q0, nq = QT[i]
                    last = nc.tensor.matmul(score_bank(n)[0:nq, c:c + w], Qs[u % 3][0:CON, j, q0:q0 + nq],
                                            Ks[u % 3][0:CON, j, s0:s0 + w], start=True, stop=True)
                last.then_inc(s_full[n % 2], 1)

            def transpose_max(u, f):
                pe.wait_ge(max_ready, u + 1)
                tiles = QT[0:3] if f == 0 else QT[3:5]
                bank = open_fill(pe, ("M", u, f))
                for q0, n in tiles:
                    i = QT.index((q0, n))
                    c = q0 - tiles[0][0]
                    last = nc.tensor.transpose(bank[0:UH, c:c + n], mx[0:n, u % 2, i, :], ident[0:n, 0:n])
                last.then_inc(m_full[fills[("M", u, f)] % 2], 1)

            def scores_t(u, j, p):
                if j == 0 and p == 0:
                    pe.wait_ge(maxrow_ready[u % 2], 48 * (u // 2 + 1))
                n = 3 * (UH * u + j) + p
                if n >= 2:
                    pe.wait_ge(t_used[n % 2], n // 2)
                for i, q0, w, c in TPIECE[p]:
                    last = nc.tensor.matmul(bankT[n % 2][:, c:c + w], Ks[u % 3][0:CONM, j, P * i:P * (i + 1)],
                                            Qs[u % 3][0:CONM, j, q0:q0 + w], start=True, stop=True)
                last.then_inc(t_full[n % 2], 1)

            def context(u, g, si):
                b, gi = u // 2, 2 * u + g
                if u == 0 and g == 0 and si == 0:
                    pe.wait_ge(dve_const, 2)
                if si == 0:
                    pe.wait_ge(prob_ready, 4 * (gi + 1))
                    used(pe, ("V", b, 2))
                    used(pe, ("V", b, 1))
                    if gi >= 1:
                        pe.wait_ge(o_used, gi)
                firsts = [SEG[0], next(s for s in SEG if s[0] == 1)]
                lasts = [[s for s in SEG if s[0] == h][-1] for h in range(2)]
                s = SEG[si]
                half, kt, c, q0, w = s
                n = KT[kt][1]
                for j in range(4):
                    hh = UH * u + 4 * g + j
                    last = nc.tensor.matmul(
                        bankO[32 * j:32 * j + 1 + HD, half, q0 - HT * half:q0 - HT * half + w],
                        V[0:n, b % 2, kt, (UH * (u % 2) + 4 * g + j), :],
                        Pr[0:n, hh % NP, c:c + w], start=(s in firsts), stop=(s in lasts),
                        tile_position=(0, 32 * j))
                if si == len(SEG) - 1:
                    last.then_inc(o_full, 1)

            def denominators(b, g):
                pe.wait_ge(o_used, 4 * b + g + 1)
                bank = open_fill(pe, ("N", b, g))
                d = bank[:, 0:2 * len(HTILE) * 4].rearrange("p (h i j) -> p h i j", h=2, j=4)
                for hf in range(2):
                    for i, (c0, w) in enumerate(HTILE):
                        c = HT * hf + c0
                        last = nc.tensor.matmul(d[0:w, hf, i, :], Of[:, b % 2, g, c:c + w], first[:, :],
                                                start=True, stop=True)
                last.then_inc(m_full[fills[("N", b, g)] % 2], 1)

            def reciprocals(b, g, hf):
                used(pe, ("N", b, g))
                bank = open_fill(pe, ("Nx", b, g, hf))
                for i, (c0, w) in enumerate(HTILE):
                    for j in range(4):
                        last = nc.tensor.matmul(bank[32 * j:32 * (j + 1), c0:c0 + w],
                                                RD[0:w, hf, i, j:j + 1].to_broadcast([w, 32]),
                                                ident[0:w, 0:w], start=True, stop=True, tile_position=(0, 32 * j))
                last.then_inc(m_full[fills[("Nx", b, g, hf)] % 2], 1)

            def attend_most(b, i):
                if i == 0:
                    for n in range(FIRST * UNITS - 2, FIRST * UNITS):
                        pe.wait_ge(s_used[n % 2], n // 2 + 1)
                        pe.wait_ge(t_used[n % 2], n // 2 + 1)
                    for hf in range(2):
                        used(pe, ("Nx", b, 2, hf))
                q0, n = QT[i]
                for g in range(3):
                    nc.tensor.matmul(attended(b, i), Of[:, b % 2, g, q0:q0 + n], wo[:, g, :],
                                     start=(g == 0), stop=False)

            def attend_out(b, i):
                for hf in range(2):
                    used(pe, ("Nx", b, 3, hf))
                q0, n = QT[i]
                open_fill(pe, ("W", b, i))
                for g in range(3 if b == B - 1 and i < 4 else 0, 4):
                    last = nc.tensor.matmul(attended(b, i), Of[:, b % 2, g, q0:q0 + n], wo[:, g, :],
                                            start=(g == 0), stop=(g == 3))
                last.then_inc(m_full[fills[("W", b, i)] % 2], 1)

            def router_t(b, i):
                pe.wait_ge(xhat_ready, ln_count[("ln2", b)])
                n = QT[i][1]
                bank = open_fill(pe, ("RT", b, i))
                for k in range(DK):
                    last = nc.tensor.transpose(bank[:, k * n:(k + 1) * n], xh[0:n, i, P * k:P * (k + 1)],
                                               ident[0:n, 0:n])
                last.then_inc(m_full[fills[("RT", b, i)] % 2], 1)

            def router(b, i):
                n = QT[i][1]
                used(pe, ("RT", b, i))
                bank = open_fill(pe, ("RL", b, i))
                for k in range(DK):
                    last = nc.tensor.matmul(bank[0:n, 0:NE], xnT[:, i % 2, k * n:(k + 1) * n],
                                            wr[:, k, :], start=(k == 0), stop=(k == DK - 1))
                last.then_inc(m_full[fills[("RL", b, i)] % 2], 1)

            def positions(b):
                pe.wait_ge(cnt_in, b + 1)
                bank = open_fill(pe, ("slot", b))
                last = earlier_tokens(bank[:, 0:NQ * NE].rearrange("p (t e) -> p t e", e=NE), NQ * b, NQ)
                if b == B - 1:
                    last = nc.tensor.matmul(bank[:, NQ * NE:(NQ + 1) * NE], ones[:, :], c8[:, :], start=True, stop=True)
                last.then_inc(m_full[fills[("slot", b)] % 2], 1)

            stages = {"embed": embed, "hT": transpose_h, "kv": kv, "V": values, "Q": queries, "K": keys, "S": scores,
                      "M": transpose_max, "T": scores_t, "PV": context, "N": denominators, "Nx": reciprocals, "Wa": attend_most, "W": attend_out, "RT": router_t, "RL": router, "slot": positions}
            for job in order:
                if job[0] in stages:
                    stages[job[0]](*job[1:])

            tokens = most_tokens(pe)
            with pe.If(tokens > CAP):
                for r in range(ROUNDS + 1):
                    pe.wait_ge(over_in, r + 1)
                    nc.tensor.matmul(bankM[0][:, 0:NE], ones[:, :], c8[:, :], start=True, stop=True
                                     ).then_inc(over_out, 1)
                for r in range(ROUNDS + 1, ROUNDS + 3):
                    pe.wait_ge(over_in, r + 1)
                    earlier_tokens(bankM[0][:, 0:NT * NE].rearrange("p (t e) -> p t e", e=NE), 0, NT
                                   ).then_inc(over_out, 1)

            trb = [bankT[i][:, 0:256].bitcast(bf16).rearrange("p (c s) -> p c s", c=4) for i in range(2)]
            hb = [bankS[0], bankS[1], bankO[:, 0, :], bankO[:, 1, :]]

            def slots_t(e, tiles):
                for i in tiles:
                    if i == 0:
                        pe.wait_ge(xe_loaded[e % 2], 16 * (e // 2 + 1))
                    n = ST[i][1]
                    q = e * NST + i
                    if q >= 2:
                        pe.wait_ge(tr_used[q % 2], q // 2)
                    for c in range(4):
                        last = nc.tensor.transpose(trb[q % 2][:, c, 0:n], XE[0:n, e % 2, i, P * c:P * (c + 1)],
                                                   identb[0:n, 0:n])
                    last.then_inc(tr_full[q % 2], 1)

            def up(e):
                pe.wait_ge(wlo_ready, e + 1)
                pe.wait_ge(whi_ready, e + 1)
                for i in (NST - 2, NST - 1):
                    q = e * NST + i
                    pe.wait_ge(tr_used[q % 2], q // 2 + 1)
                for ft in range(FK):
                    banks = []
                    for hf in range(2):
                        q = 2 * (e * FK + ft) + hf
                        if q >= 4:
                            pe.wait_ge(h_used[q % 4], q // 4)
                        banks.append(hb[q % 4])
                    terms = [(k, a, c) for k in range(DK) for a, c in ((0, 0), (0, 1), (1, 0))]
                    for ti, (k, a, c) in enumerate(terms):
                        for hf, (c0, w) in enumerate(CH):
                            last = nc.tensor.matmul(banks[hf][:, 0:w], W1s[:, e % 2, a, k, P * ft:P * (ft + 1)],
                                                    XT[:, e % 2, 2 * c + k, c0:c0 + w],
                                                    start=(ti == 0), stop=(ti == len(terms) - 1))
                            if ti == len(terms) - 1:
                                last.then_inc(h_full[(2 * (e * FK + ft) + hf) % 4], 1)

            def down(e):
                if e + 1 < NE:
                    slots_t(e + 1, (0, 1))
                for q in range(2 * (e + 1) * FK - 4, 2 * (e + 1) * FK - 2):
                    pe.wait_ge(h_used[q % 4], q // 4 + 1)
                for i, (r0, n) in enumerate(ST):
                    q = e * NST + i
                    if q >= 2:
                        pe.wait_ge(y_used[q % 2], q // 2)
                    for ft in range(FK):
                        if i == 0 and ft == FK - 1:
                            for h in range(2 * (e + 1) * FK - 2, 2 * (e + 1) * FK):
                                pe.wait_ge(h_used[h % 4], h // 4 + 1)
                        for ti, (a, c) in enumerate(((0, 0), (0, 1), (1, 0))):
                            hid = (HH, HL)[a]
                            last = nc.tensor.matmul(bankM[q % 2][0:n, 0:D], hid[:, e % 2, ft, r0:r0 + n],
                                                    W2s[:, e % 2, c, ft, :], start=(ft == 0 and ti == 0),
                                                    stop=(ft == FK - 1 and ti == 2))
                    last.then_inc(y_full[q % 2], 1)
                    if e + 1 < NE and i + 2 < NST:
                        slots_t(e + 1, (i + 2,))

            slots_t(0, range(NST))
            for e in range(NE):
                up(e)
                down(e)
            with pe.If(tokens > NMAIN):
                for q in (NE * NST - 2, NE * NST - 1):
                    pe.wait_ge(y_used[q % 2], q // 2 + 1)
                for e in range(NE):
                    pe.wait_ge(rest_xe, 16 * (e + 1))
                    for c in range(4):
                        last = nc.tensor.transpose(trb[0][:, c, 0:NREST], XE[0:NREST, 0, 0, P * c:P * (c + 1)],
                                                   identb[0:NREST, 0:NREST])
                    last.then_inc(rest_tr, 1)
                    pe.wait_ge(rest_whi, e + 1)
                    pe.wait_ge(rest_wlo, e + 1)
                    pe.wait_ge(rest_xt, e + 1)
                    terms = [(k, a, c) for k in range(DK) for a, c in ((0, 0), (0, 1), (1, 0))]
                    for ft in range(FK):
                        for ti, (k, a, c) in enumerate(terms):
                            last = nc.tensor.matmul(bankS[0][:, NREST * ft:NREST * (ft + 1)],
                                                    W1s[:, 0, a, k, P * ft:P * (ft + 1)], XT[:, 0, 2 * c + k, 0:NREST],
                                                    start=(ti == 0), stop=(ti == len(terms) - 1))
                    last.then_inc(rest_up, 1)
                    pe.wait_ge(rest_lo, e + 1)
                    if e >= 1:
                        pe.wait_ge(rest_y, e)
                    for ft in range(FK):
                        for ti, (a, c) in enumerate(((0, 0), (0, 1), (1, 0))):
                            last = nc.tensor.matmul(bankM[0][0:NREST, 0:D], (HH, HL)[a][:, 0, ft, 0:NREST],
                                                    W2s[:, 0, c, ft, :], start=(ft == 0 and ti == 0),
                                                    stop=(ft == FK - 1 and ti == 2))
                    last.then_inc(rest_down, 1)

        @block.scalar
        def _(act):
            def drain(key, dst, src):
                filled(act, key)
                nc.scalar.activation(dst, src, ACT.Copy).then_inc(m_used[fills[key] % 2], 1)

            def high(name, which, u, hf):
                if u >= 1:
                    act.wait_ge(split_stored[which], 16 * u)
                key = (name, u, hf)
                filled(act, key)
                nc.scalar.activation(XS[:, which, 0, HT * hf:HT * (hf + 1)], bankM[fills[key] % 2][:, 0:HT],
                                     ACT.Copy).then_inc(hi_ready, 1)

            for job in order:
                k, a = job[0], (job[1] if len(job) > 1 else None)
                if k == "hT":
                    f = job[2]
                    c0, w = (0, QT[3][0]) if f % 2 == 0 else (QT[3][0], 2 * P)
                    drain(job, hnT[:, f // 2, c0:c0 + w], bankM[fills[job] % 2][:, 0:w])
                elif k == "kv":
                    hf = job[2]
                    drain(job, lat[:, HT * hf:HT * (hf + 1)], bankM[fills[job] % 2][:, 0:HT])
                elif k == "V":
                    f = job[2]
                    if a == 0:
                        act.wait_ge(dve_const, 2)
                    filled(act, job)
                    for i in range(2 * f, min(2 * f + 2, len(KT))):
                        n = KT[i][1]
                        src = bankM[fills[job] % 2][0:n, D * (i % 2):D * (i % 2 + 1)]
                        last = nc.scalar.activation(V[0:n, a % 2, i, :, 1:1 + HD],
                                                    src.rearrange("p (h d) -> p h d", d=HD), ACT.Copy)
                    last.then_inc(m_used[fills[job] % 2], 1)
                elif k == "Q":
                    high("Q", 0, a, job[2])
                elif k == "K":
                    high("K", 1, a, job[2])
                elif k == "M":
                    f = job[2]
                    if a >= 1:
                        act.wait_ge(maxrow_ready[(a - 1) % 2], 48 * ((a - 1) // 2 + 1))
                    c0, w = (0, QT[3][0]) if f == 0 else (QT[3][0], 2 * P)
                    filled(act, job)
                    nc.scalar.activation(NS[:, 0, c0:c0 + w], bankM[fills[job] % 2][0:UH, 0:w], ACT.Copy,
                                         scale=-1.0).then_inc(nmhi_ready, 1)
                elif k == "T":
                    hh, p = UH * a + job[2], job[3]
                    if hh >= NP and p == 0:
                        act.wait_ge(o_full, (hh - NP) // 4 + 1)
                    n = 3 * hh + p
                    w = sum(x[2] for x in TPIECE[p])
                    act.wait_ge(t_full[n % 2], n // 2 + 1)
                    nc.scalar.activation(Pr[:, hh % NP, TOFF[p]:TOFF[p] + w], bankT[n % 2][:, 0:w], ACT.Exp,
                                         scale=SCALE).then_inc(t_used[n % 2], 1)
                elif k == "O":
                    gi = 2 * a + job[2]
                    gg = gi % 4
                    act.wait_ge(o_full, gi + 1)
                    b = gi // 4
                    if b >= 2:
                        used(act, ("W", b - 2, NQ - 1))
                    nc.scalar.activation(Of[:, b % 2, gg, :].rearrange("p (h t) -> p h t", h=2), bankO[:, :, 0:HT],
                                         ACT.Copy).then_inc(o_used, 1)
                elif k == "RT":
                    i = job[2]
                    n = QT[i][1]
                    if i >= 2:
                        filled(act, ("RL", a, i - 2))
                    elif a >= 1:
                        filled(act, ("RL", a - 1, NQ - 1))
                        filled(act, ("RL", a - 1, NQ - 2))
                    drain(job, xnT[:, i % 2, 0:DK * n], bankM[fills[job] % 2][:, 0:DK * n])
                elif k == "pr":
                    act.wait_ge(rexp_in, a + 1)
                    t = slice(NQ * a, NQ * (a + 1))
                    nc.scalar.activation(E2[:, t, :], EP[:, t, :], ACT.Exp).then_inc(rexp, 1)
            tokens = most_tokens(act)
            hb = [bankS[0], bankS[1], bankO[:, 0, :], bankO[:, 1, :]]
            for e in range(NE):
                for ft in range(FK):
                    for hf, (c0, w) in enumerate(CH):
                        q = 2 * (e * FK + ft) + hf
                        act.wait_ge(h_full[q % 4], q // 4 + 1)
                        nc.scalar.activation(HH[:, e % 2, ft, c0:c0 + w], hb[q % 4][:, 0:w],
                                             ACT.Relu).then_inc(hhi_ready, 1)
                for i, (r0, n) in enumerate(ST):
                    q = e * NST + i
                    act.wait_ge(y_full[q % 2], q // 2 + 1)
                    if e >= 2 and i == 0:
                        act.wait_ge(y_stored[e % 2], 16 * NST * (e // 2))
                    nc.scalar.activation(Y[0:n, e % 2, i, :], bankM[q % 2][0:n, 0:D],
                                         ACT.Copy).then_inc(y_used[q % 2], 1)
            with act.If(tokens > NMAIN):
                act.wait_ge(y_stored[0], 16 * NST * NE // 2)
                for e in range(NE):
                    act.wait_ge(rest_up, e + 1)
                    nc.scalar.activation(HH[:, 0, :, 0:NREST],
                                         bankS[0][:, 0:FK * NREST].rearrange("p (f s) -> p f s", f=FK),
                                         ACT.Relu).then_inc(rest_hi, 1)
                    act.wait_ge(rest_down, e + 1)
                    if e >= 1:
                        act.wait_ge(rest_stored, 16 * e)
                    nc.scalar.activation(Y[0:NREST, 0, 0, :], bankM[0][0:NREST, 0:D], ACT.Copy).then_inc(rest_y, 1)

            act.wait_ge(gathered[B - 1], 32)
            for c in range(TOPK):
                for i in range(NQ):
                    n, t = QT[i][1], NQ * (B - 1) + i
                    last = nc.scalar.activation(GY[0:n, B - 1, i, c, :], GY[0:n, B - 1, i, c, :], ACT.Copy,
                                                scale=gate[0:n, c, t:t + 1])
                last.then_inc(gated, 1)

        @block.vector
        def _(dve):
            chain = [0]

            def link(ins):
                chain[0] += 1
                ins.then_inc(dve_chain, 1)
                dve.wait_ge(dve_chain, chain[0])

            nc.vector.memset(ones[:, :], 1.0)
            nc.vector.memset(wo[:, :, :], 0.0)
            nc.vector.memset(zero[:, :], 0.0).then_inc(dve_const, 1)
            nc.vector.memset(onesb[:, :], 1.0)
            for b in range(B):
                nc.vector.memset(H[:, b, 0, :], 0.0)
            nc.vector.memset(V[:, :, :, :, 0:1], 1.0)
            nc.vector.memset(mx[:, :, :, :], 0.0)
            nc.vector.memset(bankO[:, :, :], 0.0)
            nc.vector.memset(LG[:, :, :], 0.0).then_inc(dve_const, 1)

            norms = [0]

            def statistics(b, all_of=True):
                if all_of:
                    for i in range(NQ):
                        last = nc.vector.bn_stats(st[:, i, :], H[:, b, i, :])
                    link(last)
                for i in range(NQ):
                    last = nc.vector.bn_aggr(mv[:, i, :], st[:, i, :])
                last.then_inc(mean_ready, 1)

            def normalise(b):
                norms[0] += 1
                dve.wait_ge(mean_ready, norms[0])
                dve.wait_ge(rstd_ready, norms[0])
                for i in range(NQ):
                    last = nc.vector.tensor_scalar(xh[:, i, :], H[:, b, i, :], mv[:, i, 0:1], rs[:, i:i + 1],
                                                   ALU.subtract, ALU.mult)
                last.then_inc(xhat_ready, 1)

            def xh_free():
                prev = ln_order[norms[0] - 1]
                if prev[0] == "ln1":
                    filled(dve, ("hT", prev[1], 3))
                    filled(dve, ("hT", prev[1], 2))
                else:
                    filled(dve, ("RT", prev[1], NQ - 1))
                    dve.wait_ge(xhl_ready, prev[1] + 1)

            def rest(name, which, u, hf):
                if hf == 0 and u + which > 0:
                    dve.wait_ge(lo_ready, lo_count[(name, u)] - 1)
                key = (name, u, hf)
                filled(dve, key)
                dve.wait_ge(hi_ready, 4 * u + 2 * which + hf + 1)
                c = slice(HT * hf, HT * (hf + 1))
                nc.vector.tensor_tensor(XR[:, c], bankM[fills[key] % 2][:, 0:HT],
                                        XS[:, which, 0, c], ALU.subtract).then_inc(m_used[fills[key] % 2], 1)

            def middle(name, which, u):
                for hf in range(2):
                    used(dve, (name, u, hf))
                if u >= 1:
                    dve.wait_ge(split_stored[which], 16 * u)
                link(nc.vector.tensor_copy(XS[:, which, 1, :], XR[:, :]))
                nc.vector.tensor_tensor(XS[:, which, 2, :], XR[:, :], XS[:, which, 1, :],
                                        ALU.subtract).then_inc(lo_ready, 1)

            def maxima(u, j, p):
                n = 3 * (UH * u + j) + p
                dve.wait_ge(s_full[n % 2], n // 2 + 1)
                for i, s0, w, c in SPIECE[p]:
                    nq = QT[i][1]
                    m0 = T - P if i == 0 else (s0 if i == NQ - 1 else T - w)
                    slot = NQ if (i == NQ - 1 and s0 > 0) else i
                    last = nc.vector.tensor_tensor_reduce(
                        out=score_bank(n)[0:nq, c:c + w], in0=score_bank(n)[0:nq, c:c + w], in1=maskn[0:nq, m0:m0 + w],
                        scale=1.0, scalar=-3.0e38, op0=ALU.add, op1=ALU.max,
                        accum_out=mx[0:nq, u % 2, slot, j:j + 1])
                last.then_inc(s_used[n % 2], 1)

            def combine_max(u):
                for p in range(3):
                    n = 3 * (UH * u + UH - 1) + p
                    dve.wait_ge(s_used[n % 2], n // 2 + 1)
                nc.vector.tensor_tensor(mx[:, u % 2, NQ - 1, :], mx[:, u % 2, NQ - 1, :], mx[:, u % 2, NQ, :],
                                        ALU.max).then_inc(max_ready, 1)

            def negative_rest(u, f):
                c0, w = (0, QT[3][0]) if f == 0 else (QT[3][0], 2 * P)
                key = ("M", u, f)
                filled(dve, key)
                dve.wait_ge(nmhi_ready, 2 * u + f + 1)
                nc.vector.scalar_tensor_tensor(out=NR[:, c0:c0 + w], in0=bankM[fills[key] % 2][0:UH, 0:w],
                                               scalar=-1.0, in1=NS[:, 0, c0:c0 + w], op0=ALU.mult,
                                               op1=ALU.subtract).then_inc(m_used[fills[key] % 2], 1)

            def negative_split(u):
                for f in range(2):
                    used(dve, ("M", u, f))
                if u >= 1:
                    dve.wait_ge(maxrow_ready[(u - 1) % 2], 48 * ((u - 1) // 2 + 1))
                link(nc.vector.tensor_copy(NS[:, 1, :], NR[:, :]))
                nc.vector.tensor_tensor(NS[:, 2, :], NR[:, :], NS[:, 1, :], ALU.subtract).then_inc(nm_ready, 1)

            def tile_range(b):
                return slice(NQ * b, NQ * (b + 1))

            def wide(x):
                return x.unsqueeze(2).to_broadcast([P, NQ, NE])

            def over_tiles(x):
                return x.unsqueeze(1).to_broadcast([P, NT, NE])

            def probabilities(b):
                t = tile_range(b)
                used(dve, ("RL", b, NQ - 2))
                used(dve, ("RL", b, NQ - 1))
                link(nc.vector.reduce_max(r20[:, 0, t], LG[:, t, :], AX))
                nc.vector.tensor_tensor(EP[:, t, :], LG[:, t, :], wide(r20[:, 0, t]), ALU.subtract
                                        ).then_inc(rexp_in, 1)

            def over_sums(b):
                t = tile_range(b)
                dve.wait_ge(rexp, b + 1)
                link(nc.vector.reduce_sum(r20[:, 1, t], E2[:, t, :], AX))
                link(nc.vector.reciprocal(r20[:, 2, t], r20[:, 1, t]))
                link(nc.vector.tensor_tensor(EP[:, t, :], E2[:, t, :], wide(r20[:, 2, t]), ALU.mult))

            def two_largest(b):
                t = tile_range(b)
                tiles = range(NQ * b, NQ * (b + 1))
                for i in tiles:
                    last = nc.vector.max(v8[:, i, :], EP[:, i, :])
                link(last)
                for i in tiles:
                    last = nc.vector.max_index(i8[:, i, :], v8[:, i, :], EP[:, i, :])
                link(last)
                link(nc.vector.tensor_copy(i8f[:, t, :], i8[:, t, :]))

            def top_experts(b):
                t = tile_range(b)
                for c in range(TOPK):
                    last = nc.vector.tensor_tensor(OH[:, c, t, :], iota8[:, t, :], wide(i8f[:, t, c]), ALU.is_equal)
                link(last)
                link(nc.vector.tensor_tensor(E3[:, t, :], OH[:, 0, t, :], OH[:, 1, t, :], ALU.add))
                tail = XHL[:, b % 2, :, :].bitcast(f32)
                nc.vector.tensor_copy(tail[:, :, D], token1[:, t])
                nc.vector.tensor_copy(tail[:, :, D + 1], i8f[:, t, 0])
                last = nc.vector.tensor_tensor(Xb[:, t, :], E3[:, t, :], valid[:, t, :], ALU.mult)
                if b == B - 1:
                    link(last)
                    last = nc.vector.reduce_sum(c8[:, :], Xb[:, :, :].rearrange("p t e -> p e t"), AX)
                last.then_inc(cnt_in, 1)

            def slots_of(b):
                t = tile_range(b)
                key = ("slot", b)
                bank = bankM[fills[key] % 2]
                filled(dve, key)
                ranks = bank[:, 0:NQ * NE].rearrange("p (t e) -> p t e", e=NE)
                nc.vector.tensor_scalar(E3[:, t, :], ranks, float(CAP), 65536.0, ALU.is_ge, ALU.mult)
                last = nc.vector.tensor_tensor(POS[:, t, :], ranks, base8[:, t, :], ALU.add)
                if b == B - 1:
                    link(last)
                    last = nc.vector.reduce_max(c8[:, 0:1], bank[:, NQ * NE:(NQ + 1) * NE], AX)
                last.then_inc(m_used[fills[key] % 2], 1)
                used(dve, key)
                link(nc.vector.tensor_tensor(POS[:, t, :], POS[:, t, :], E3[:, t, :], ALU.add))
                for c in range(TOPK):
                    link(nc.vector.tensor_tensor(E2[:, t, :], OH[:, c, t, :], POS[:, t, :], ALU.mult))
                    link(nc.vector.reduce_sum(r20[:, 3, t], E2[:, t, :], AX))
                    last = nc.vector.tensor_copy(sidx[:, c, t], r20[:, 3, t])
                    if c < TOPK - 1:
                        link(last)
                last.then_inc(idx_ready, 1)
                for c in range(TOPK):
                    nc.vector.tensor_copy(gate[:, c, t], v8[:, t, c])
                if b == B - 1:
                    nc.vector.tensor_copy(most[:, :], c8[:, 0:1]).then_inc(most_ready, 1)

            def weights_high(e, k):
                if k == 0:
                    dve.wait_ge(w_loaded[e % 2], 32 * (e // 2 + 1))
                    if e >= 2:
                        q = (e - 1) * NST - 1
                        dve.wait_ge(y_full[q % 2], q // 2 + 1)
                if k < 2:
                    nc.vector.tensor_copy(W1s[:, e % 2, 0, k, :], W1f[:, k, :])
                else:
                    f = slice(FK // 2 * (k - 2), FK // 2 * (k - 1))
                    last = nc.vector.tensor_copy(W2s[:, e % 2, 0, f, :], W2f[:, f, :])
                    if k == 3:
                        last.then_inc(whi_ready, 1)

            def last_group(b, g):
                return divmod(4 * b + g - 1, 4)

            for job in order:
                k, a = job[0], (job[1] if len(job) > 1 else None)
                if k == "embed":
                    filled(dve, job)
                    if a == 0:
                        dve.wait_ge(dve_const, 2)
                    nc.vector.tensor_copy(H[0:NIMG, a, 0, :], bankM[fills[job] % 2][0:NIMG, 0:D]
                                          ).then_inc(m_used[fills[job] % 2], 1)
                elif k == "ln1s":
                    dve.wait_ge(ld_txt[a], 16)
                    used(dve, ("embed", a))
                    if norms[0]:
                        dve.wait_ge(xhat_ready, norms[0])
                    statistics(a)
                elif k == "ln2s":
                    used(dve, ("W", a, NQ - 2))
                    used(dve, ("W", a, NQ - 1))
                    dve.wait_ge(xhat_ready, norms[0])
                    statistics(a, a < B - 1)
                elif k in ("ln1", "ln2"):
                    if norms[0]:
                        xh_free()
                    normalise(a)
                elif k == "Q":
                    rest("Q", 0, a, job[2])
                elif k == "K":
                    rest("K", 1, a, job[2])
                elif k == "Qx":
                    middle("Q", 0, a)
                elif k == "Kx":
                    middle("K", 1, a)
                elif k == "S":
                    if job[1:] == (0, 0, 0):
                        dve.wait_ge(pool_const, 1)
                    maxima(*job[1:])
                elif k == "mxc":
                    combine_max(a)
                elif k == "M":
                    negative_rest(a, job[2])
                elif k == "Mx":
                    negative_split(a)
                elif k == "N":
                    filled(dve, job)
                    if 4 * a + job[2] >= 1:
                        for hf in range(2):
                            used(dve, ("Nx", *last_group(a, job[2]), hf))
                    d = bankM[fills[job] % 2][:, 0:2 * len(HTILE) * 4].rearrange("p (h i j) -> p h i j", h=2, j=4)
                    full, w = len(HTILE) - 1, HTILE[-1][1]
                    nc.vector.reciprocal(RD[:, :, 0:full, :], d[:, :, 0:full, :])
                    nc.vector.reciprocal(RD[0:w, :, full, :], d[0:w, :, full, :]).then_inc(m_used[fills[job] % 2], 1)
                elif k == "Nx":
                    filled(dve, job)
                    v = Of[:, a % 2, job[2], HT * job[3]:HT * (job[3] + 1)]
                    nc.vector.tensor_tensor(v, v, bankM[fills[job] % 2][:, 0:HT], ALU.mult
                                            ).then_inc(m_used[fills[job] % 2], 1)
                elif k == "W":
                    n = QT[job[2]][1]
                    filled(dve, job)
                    nc.vector.tensor_tensor(H[0:n, a, job[2], :], attended(a, job[2]),
                                            H[0:n, a, job[2], :], ALU.add).then_inc(m_used[fills[job] % 2], 1)
                    if a == B - 1:
                        used(dve, job)
                        dve.wait_ge(xhat_ready, norms[0])
                        last = nc.vector.bn_stats(st[:, job[2], :], H[:, a, job[2], :])
                        if job[2] == NQ - 1:
                            link(last)
                elif k == "pr":
                    probabilities(a)
                elif k == "norm":
                    over_sums(a)
                elif k == "two":
                    two_largest(a)
                elif k == "top":
                    top_experts(a)
                elif k == "slot":
                    slots_of(a)
                elif k == "w0":
                    for q in range(4):
                        weights_high(0, q)
                elif k == "hl":
                    dve.wait_ge(xhat_ready, ln_count[("ln2", a)])
                    if a >= 2:
                        dve.wait_ge(xhl_stored, 16 * (a - 1))
                        dve.wait_ge(scattered[a % 2], 16 * TOPK * NQ * (a // 2))
                    nc.vector.tensor_copy(XHL[:, a % 2, :, 0:D], xh[:, :, :]).then_inc(xhi_ready, 1)
                elif k == "RL":
                    n = QT[job[2]][1]
                    filled(dve, job)
                    nc.vector.tensor_copy(LG[0:n, a * NQ + job[2], :], bankM[fills[job] % 2][0:n, 0:NE]
                                          ).then_inc(m_used[fills[job] % 2], 1)

            tokens = most_tokens(dve)
            with dve.If(tokens > CAP):
                over_links = [0]

                def over_link(ins):
                    over_links[0] += 1
                    ins.then_inc(over_chain, 1)
                    dve.wait_ge(over_chain, over_links[0])

                for p in range(2):
                    dve.wait_ge(scattered[p], 16 * TOPK * NQ * B // 2)
                over_link(nc.vector.tensor_tensor(E3[:, :, :], OH[:, 0, :, :], OH[:, 1, :, :], ALU.add))
                over_link(nc.vector.tensor_tensor(E3[:, :, :], E3[:, :, :], valid[:, :, :], ALU.mult))
                over_link(nc.vector.tensor_tensor(G[:, :, :], EP[:, :, :], E3[:, :, :], ALU.mult))
                over_link(nc.vector.tensor_scalar(E2[:, :, :], E3[:, :, :], 1.0, None, ALU.subtract))
                over_link(nc.vector.tensor_tensor(G[:, :, :], G[:, :, :], E2[:, :, :], ALU.add))
                over_link(nc.vector.memset(thr[:, :], 0.0))

                def count(src):
                    nc.vector.reduce_sum(c8[:, :], src.rearrange("p t e -> p e t"), AX).then_inc(over_in, 1)

                for r in range(ROUNDS):
                    bit = 1 << (ROUNDS - 1 - r)
                    over_link(nc.vector.tensor_scalar(cand[:, :].bitcast(u32), thr[:, :].bitcast(u32), bit, None,
                                                      ALU.bitwise_or))
                    over_link(nc.vector.tensor_tensor(E2[:, :, :], G[:, :, :], over_tiles(cand[:, :]), ALU.is_ge))
                    count(E2[:, :, :])
                    dve.wait_ge(over_out, r + 1)
                    over_link(nc.vector.scalar_tensor_tensor(out=t8[:, :], in0=bankM[0][:, 0:NE], scalar=float(CAP),
                                                             in1=cand[:, :], op0=ALU.is_ge, op1=ALU.mult))
                    over_link(nc.vector.tensor_tensor(thr[:, :], thr[:, :], t8[:, :], ALU.max))
                over_link(nc.vector.tensor_tensor(KEEP[:, :, :], G[:, :, :], over_tiles(thr[:, :]), ALU.is_gt))
                count(KEEP[:, :, :])
                dve.wait_ge(over_out, ROUNDS + 1)
                over_link(nc.vector.tensor_scalar(room[:, :], bankM[0][:, 0:NE], -1.0, float(CAP), ALU.mult, ALU.add))
                over_link(nc.vector.tensor_tensor(E2[:, :, :], G[:, :, :], over_tiles(thr[:, :]), ALU.is_equal))
                nc.vector.tensor_copy(Xb[:, :, :], E2[:, :, :]).then_inc(over_in, 1)
                dve.wait_ge(over_out, ROUNDS + 2)
                o = bankM[0][:, 0:NT * NE].rearrange("p (t e) -> p t e", e=NE)
                over_link(nc.vector.tensor_tensor(E3[:, :, :], o, over_tiles(room[:, :]), ALU.is_lt))
                over_link(nc.vector.tensor_tensor(E3[:, :, :], E3[:, :, :], E2[:, :, :], ALU.mult))
                over_link(nc.vector.tensor_tensor(KEEP[:, :, :], KEEP[:, :, :], E3[:, :, :], ALU.add))
                nc.vector.tensor_copy(Xb[:, :, :], KEEP[:, :, :]).then_inc(over_in, 1)
                dve.wait_ge(over_out, ROUNDS + 3)
                over_link(nc.vector.tensor_tensor(POS[:, :, :], o, base8[:, :, :], ALU.add))
                for c in range(TOPK):
                    over_link(nc.vector.tensor_tensor(E2[:, :, :], OH[:, c, :, :], KEEP[:, :, :], ALU.mult))
                    over_link(nc.vector.reduce_sum(r20[:, 0, :], E2[:, :, :], AX))
                    over_link(nc.vector.tensor_tensor(E3[:, :, :], E2[:, :, :], POS[:, :, :], ALU.mult))
                    over_link(nc.vector.reduce_sum(r20[:, 1, :], E3[:, :, :], AX))
                    over_link(nc.vector.tensor_tensor(gate[:, c, :], r20[:, 0, :], v8[:, :, c], ALU.mult))
                    over_link(nc.vector.tensor_scalar(r20[:, 2, :], r20[:, 0, :], -65536.0, 65536.0, ALU.mult, ALU.add))
                    over_link(nc.vector.tensor_tensor(r20[:, 3, :], r20[:, 2, :], r20[:, 1, :], ALU.add))
                    over_link(nc.vector.tensor_copy(sidx[:, c, :], r20[:, 3, :]))
                nc.vector.memset(room[:, :], 0.0).then_inc(over_idx, 1)

            trb = [bankT[i][:, 0:256].bitcast(bf16).rearrange("p (c s) -> p c s", c=4) for i in range(2)]
            hb = [bankS[0], bankS[1], bankO[:, 0, :], bankO[:, 1, :]]

            def slots_in(e):
                if e >= 2:
                    q = 2 * (e - 1) * FK - 1
                    dve.wait_ge(h_full[q % 4], q // 4 + 1)
                for i, (r0, n) in enumerate(ST):
                    q = e * NST + i
                    dve.wait_ge(tr_full[q % 2], q // 2 + 1)
                    nc.vector.tensor_copy(XT[:, e % 2, :, r0:r0 + n], trb[q % 2][:, :, 0:n]).then_inc(tr_used[q % 2], 1)

            def destinations(e, p, tiles, n, chained):
                info = XE[0:n, p, 0:tiles, :].bitcast(f32)
                own, choice, none = (dst[0:n, j, 0:tiles] for j in range(3))
                nc.vector.tensor_scalar(choice, info[:, :, D + 1], float(e), float(P), ALU.not_equal, ALU.mult)
                nc.vector.tensor_scalar(none, info[:, :, D], 0.0, 65536.0, ALU.is_equal, ALU.mult)
                chained(nc.vector.tensor_scalar(own, info[:, :, D], -1.0, None, ALU.add))
                chained(nc.vector.tensor_tensor(own, own, choice, ALU.add))
                chained(nc.vector.tensor_tensor(own, own, none, ALU.add))
                nc.vector.tensor_copy(dest[0:n, p, 0:tiles], own).then_inc(dest_ready, 1)

            def slot_owners(e):
                dve.wait_ge(xe_loaded[e % 2], 16 * (e // 2 + 1))
                if e >= 1:
                    dve.wait_ge(dest_ready, e)
                if e >= 2:
                    dve.wait_ge(y_stored[e % 2], 16 * NST * (e // 2))
                destinations(e, e % 2, NST, P, link)

            slots_in(0)
            slot_owners(0)
            for e in range(NE):
                if e >= 2:
                    q = (e - 1) * NST - 1
                    dve.wait_ge(y_full[q % 2], q // 2 + 1)
                for ft in range(FK):
                    for hf, (c0, w) in enumerate(CH):
                        q = 2 * (e * FK + ft) + hf
                        dve.wait_ge(hhi_ready, q + 1)
                        nc.vector.scalar_tensor_tensor(out=HL[:, e % 2, ft, c0:c0 + w], in0=hb[q % 4][:, 0:w], scalar=0.0,
                                                       in1=HH[:, e % 2, ft, c0:c0 + w], op0=ALU.max,
                                                       op1=ALU.subtract).then_inc(h_used[q % 4], 1)
                    if 1 <= ft <= 4 and e + 1 < NE:
                        weights_high(e + 1, ft - 1)
                if e + 1 < NE:
                    slots_in(e + 1)
                    slot_owners(e + 1)

            with dve.If(tokens > NMAIN):
                rest_links = [0]

                def rest_link(ins):
                    rest_links[0] += 1
                    ins.then_inc(rest_chain, 1)
                    dve.wait_ge(rest_chain, rest_links[0])

                for q in (NE * NST - 2, NE * NST - 1):
                    dve.wait_ge(y_full[q % 2], q // 2 + 1)
                for e in range(NE):
                    dve.wait_ge(rest_w, 32 * (e + 1))
                    if e >= 1:
                        dve.wait_ge(rest_down, e)
                    nc.vector.tensor_copy(W1s[:, 0, 0, :, :], W1f[:, :, :])
                    nc.vector.tensor_copy(W2s[:, 0, 0, :, :], W2f[:, :, :]).then_inc(rest_whi, 1)
                    dve.wait_ge(rest_tr, e + 1)
                    nc.vector.tensor_copy(XT[:, 0, :, 0:NREST], trb[0][:, :, 0:NREST]).then_inc(rest_xt, 1)
                    dve.wait_ge(rest_xe, 16 * (e + 1))
                    dve.wait_ge(dest_ready, NE + e)
                    dve.wait_ge(y_stored[0], 16 * NST * NE // 2)
                    if e >= 1:
                        dve.wait_ge(rest_stored, 16 * e)
                    destinations(e, 0, 1, NREST, rest_link)
                    dve.wait_ge(rest_hi, e + 1)
                    nc.vector.scalar_tensor_tensor(out=HL[:, 0, :, 0:NREST],
                                                   in0=bankS[0][:, 0:FK * NREST].rearrange("p (f s) -> p f s", f=FK),
                                                   scalar=0.0, in1=HH[:, 0, :, 0:NREST], op0=ALU.max,
                                                   op1=ALU.subtract).then_inc(rest_lo, 1)

            for b in range(B - 1):
                dve.wait_ge(gathered[b], 32)
                for c in range(TOPK):
                    for i in range(NQ):
                        n, t = QT[i][1], NQ * b + i
                        last = nc.vector.scalar_tensor_tensor(out=H[0:n, b, i, :], in0=GY[0:n, b, i, c, :],
                                                              scalar=gate[0:n, c, t:t + 1], in1=H[0:n, b, i, :],
                                                              op0=ALU.mult, op1=ALU.add)
                        if c == TOPK - 1:
                            last.then_inc(combined, 1)
                    if c < TOPK - 1:
                        link(last)


def kernel(**inputs):
    import numpy as np
    import concourse.bacc as bacc
    from concourse import mybir as mb
    from concourse.bass_utils import run_bass_kernel_spmd as run

    def c(a):
        return np.ascontiguousarray(a)

    x = np.asarray(inputs["x"])
    nb, ch, hh, ww = x.shape
    p = 16
    pt = x.reshape(nb, ch, hh // p, p, ww // p, p).transpose(0, 2, 3, 1, 4, 5).reshape(-1, ch * p * p).T
    q2l = np.asarray(inputs["L0_attn_q_to_latent"])
    vu = np.asarray(inputs["L0_attn_v_up"])
    arrays = {
        "patchesT": c(pt), "txt": c(inputs["txt"]), "tokWT": c(np.asarray(inputs["L0_tok_W"]).T),
        "tokb": c(inputs["L0_tok_b"]), "WqT": c(np.asarray(inputs["L0_attn_Wq"]).T),
        "WkvT": c(np.concatenate([np.asarray(inputs["L0_attn_Wk_down"]), np.asarray(inputs["L0_attn_Wv_down"])], 0).T),
        "q2lT": c(q2l.transpose(2, 0, 1).reshape(q2l.shape[2], -1)),
        "vup": c(vu.transpose(1, 0, 2).reshape(vu.shape[1], -1)),
        "WoT": c(np.asarray(inputs["L0_attn_Wout"]).T), "Wr": c(inputs["L0_ffn_Wr"]),
        "W1": c(inputs["L0_ffn_W1"]), "W2": c(inputs["L0_ffn_W2"]),
    }
    nc = bacc.Bacc("TRN2", target_bir_lowering=False, num_devices=1)
    args = [nc.dram_tensor(k, a.shape, mb.dt.from_np(a.dtype), kind="ExternalInput").ap() for k, a in arrays.items()]
    nb, nt, d = arrays["txt"].shape
    t = nt + arrays["patchesT"].shape[1] // nb
    o = nc.dram_tensor("out", (nb, t, d), mb.dt.float32, kind="ExternalOutput").ap()
    early_fusion_kernel(nc, *args, o)
    r = run(nc, [arrays], core_ids=[0])
    return r.results[0]["out"]
```
